# Optimizing a Trainium2 kernel written in Bass

```python
import numpy as np
import jax
import jax.numpy as jnp

def _softmax(x, axis=-1):
    return jax.nn.softmax(x, axis=axis)

def _gelu(x):
    return jax.nn.gelu(x, approximate=True)

def _silu(x):
    return jax.nn.silu(x)

def _sigmoid(x):
    return jax.nn.sigmoid(x)

def _layernorm(x, axis=-1, eps=1e-05):
    m = jnp.mean(x, axis=axis, keepdims=True)
    v = jnp.var(x, axis=axis, keepdims=True)
    return (x - m) / jnp.sqrt(v + eps)

def _scatter_add(tgt, idx, src, axis=0):
    return tgt.at[idx].add(src)

def _segment_sum(src, seg, n):
    return jax.ops.segment_sum(src, seg, n)
kernel_name = 'mk_adaln_d1_jaxref_r4_478657'

def setup_inputs(seed: int=0):
    np.random.seed(seed)
    _w = jnp.asarray

    def _L0_attn_setup():
        import jax, jax.numpy as jnp
        import numpy as np
        D_MODEL, D_STATE, D_CONV = (256, 16, 4)
        BATCH, SEQ = (4, 512)
        LN_EPS = 1e-05

        def _causal_depthwise_conv(x_btd, conv_w, conv_b):
            x_bdt = jnp.transpose(x_btd, (0, 2, 1))
            y = jax.lax.conv_general_dilated(x_bdt, conv_w, window_strides=(1,), padding=[(D_CONV - 1, 0)], dimension_numbers=('NCH', 'OIH', 'NCH'), feature_group_count=D_MODEL)
            y = y + conv_b[None, :, None]
            return jnp.transpose(y, (0, 2, 1))

        def _mamba_forward(x, W_in, b_in, conv_w, conv_b, W_bc, b_bc, W_dt, b_dt, A_log, D, W_out, b_out, ln_g, ln_b):
            B_, T, _ = x.shape
            proj = x @ W_in + b_in
            x_ssm, x_gate = jnp.split(proj, 2, axis=-1)
            x_conv = jax.nn.silu(_causal_depthwise_conv(x_ssm, conv_w, conv_b))
            BC = x_conv @ W_bc + b_bc
            Bm, Cm = jnp.split(BC, 2, axis=-1)
            dt = jax.nn.softplus(x_conv @ W_dt + b_dt)
            A = -jnp.exp(A_log)

            def step(h, inp):
                xt, dtt, Bt, Ct = inp
                dA = jnp.exp(dtt[:, :, None] * A)
                h = h * dA + (dtt * xt)[:, :, None] * Bt[:, None, :]
                y = jnp.einsum('bdn,bn->bd', h, Ct) + xt * D
                return (h, y)
            h0 = jnp.zeros((B_, D_MODEL, D_STATE), x.dtype)
            xs = (jnp.swapaxes(x_conv, 0, 1), jnp.swapaxes(dt, 0, 1), jnp.swapaxes(Bm, 0, 1), jnp.swapaxes(Cm, 0, 1))
            _, ys = jax.lax.scan(step, h0, xs)
            y = jnp.swapaxes(ys, 0, 1)
            y = y * jax.nn.silu(x_gate)
            out = y @ W_out + b_out
            res = out + x
            mu = jnp.mean(res, axis=-1, keepdims=True)
            var = jnp.var(res, axis=-1, keepdims=True)
            return (res - mu) * jax.lax.rsqrt(var + LN_EPS) * ln_g + ln_b
        key = jax.random.key(seed)
        ks = jax.random.split(key, 16)
        s_in = 1.0 / np.sqrt(D_MODEL)
        inp = {'x': jax.random.normal(ks[0], (BATCH, SEQ, D_MODEL), dtype=jnp.float32), 'W_in': jax.random.normal(ks[1], (D_MODEL, 2 * D_MODEL), dtype=jnp.float32) * s_in, 'b_in': jnp.zeros((2 * D_MODEL,), jnp.float32), 'conv_w': jax.random.normal(ks[2], (D_MODEL, 1, D_CONV), dtype=jnp.float32) * 0.5, 'conv_b': jnp.zeros((D_MODEL,), jnp.float32), 'W_bc': jax.random.normal(ks[3], (D_MODEL, 2 * D_STATE), dtype=jnp.float32) * s_in, 'b_bc': jnp.zeros((2 * D_STATE,), jnp.float32), 'W_dt': jax.random.normal(ks[4], (D_MODEL, D_MODEL), dtype=jnp.float32) * s_in, 'b_dt': jnp.zeros((D_MODEL,), jnp.float32), 'A_log': jax.random.normal(ks[5], (D_MODEL, D_STATE), dtype=jnp.float32), 'D': jnp.ones((D_MODEL,), jnp.float32), 'W_out': jax.random.normal(ks[6], (D_MODEL, D_MODEL), dtype=jnp.float32) * s_in, 'b_out': jnp.zeros((D_MODEL,), jnp.float32), 'ln_g': jnp.ones((D_MODEL,), jnp.float32), 'ln_b': jnp.zeros((D_MODEL,), jnp.float32)}
        return inp
    _L0_attn_in = _L0_attn_setup()

    def _L0_ffn_setup():
        import jax, jax.numpy as jnp
        import numpy as np
        from jax.scipy.linalg import expm
        D = 256
        E = 6
        K = 2
        H = 2 * D
        A4 = 4 * D
        NROT = 4
        LN_EPS = 1e-05

        def _xavier(key, shape):
            fan_in, fan_out = (shape[-2], shape[-1])
            lim = np.sqrt(6.0 / (fan_in + fan_out))
            return jax.random.uniform(key, shape, jnp.float32, -lim, lim)

        def _layernorm(x, g, b):
            mu = jnp.mean(x, axis=-1, keepdims=True)
            var = jnp.var(x, axis=-1, keepdims=True)
            return (x - mu) * jax.lax.rsqrt(var + LN_EPS) * g + b

        def _moe(xn, gate_w, gate_b, ew1, eb1, ew2, eb2):
            logits = xn @ gate_w + gate_b
            tw, ti = jax.lax.top_k(logits, K)
            tw = jax.nn.softmax(tw, axis=-1)
            w_full = jnp.sum(tw[..., None] * jax.nn.one_hot(ti, E, dtype=tw.dtype), axis=-2)
            h = jax.nn.gelu(jnp.einsum('bsd,edh->besh', xn, ew1) + eb1[None, :, None, :], approximate=False)
            eo = jnp.einsum('besh,ehd->besd', h, ew2) + eb2[None, :, None, :]
            return jnp.einsum('bse,besd->bsd', w_full, eo)

        def _rotate(x, gens):
            for i in range(NROT):
                x = x @ expm(gens[i])
            return x
        key = jax.random.key(seed)
        ks = jax.random.split(key, 16)
        x = jax.random.normal(ks[0], (4, 512, D), jnp.float32)
        gens_raw = _xavier(ks[1], (NROT, D, D))
        gens = 0.5 * (gens_raw - jnp.swapaxes(gens_raw, -1, -2))
        return {'x': x, 'ln_g': jnp.ones((D,), jnp.float32), 'ln_b': jnp.zeros((D,), jnp.float32), 'aw1': _xavier(ks[2], (D, A4)), 'ab1': jnp.zeros((A4,), jnp.float32), 'aw2': _xavier(ks[3], (A4, D)), 'ab2': jnp.zeros((D,), jnp.float32), 'gate_w': _xavier(ks[4], (D, E)), 'gate_b': jnp.zeros((E,), jnp.float32), 'ew1': _xavier(ks[5], (E, D, H)), 'eb1': jnp.zeros((E, H), jnp.float32), 'ew2': _xavier(ks[6], (E, H, D)), 'eb2': jnp.zeros((E, D), jnp.float32), 'gens': gens, 'gc_w': _xavier(ks[7], (2 * D, 1)), 'gc_b': jnp.zeros((1,), jnp.float32)}
    _L0_ffn_in = _L0_ffn_setup()
    _L0_c = _w((lambda *s: np.random.randn(*s).astype(np.float32) * 0.05)(8, 256))
    _L0_wmod = _w((lambda *s: np.random.randn(*s).astype(np.float32) * 0.05)(256, 6 * 256) * 256 ** (-0.5))
    _d = {'L0_attn_x': _L0_attn_in['x'], 'L0_attn_W_in': _L0_attn_in['W_in'], 'L0_attn_b_in': _L0_attn_in['b_in'], 'L0_attn_conv_w': _L0_attn_in['conv_w'], 'L0_attn_conv_b': _L0_attn_in['conv_b'], 'L0_attn_W_bc': _L0_attn_in['W_bc'], 'L0_attn_b_bc': _L0_attn_in['b_bc'], 'L0_attn_W_dt': _L0_attn_in['W_dt'], 'L0_attn_b_dt': _L0_attn_in['b_dt'], 'L0_attn_A_log': _L0_attn_in['A_log'], 'L0_attn_D': _L0_attn_in['D'], 'L0_attn_W_out': _L0_attn_in['W_out'], 'L0_attn_b_out': _L0_attn_in['b_out'], 'L0_attn_ln_g': _L0_attn_in['ln_g'], 'L0_attn_ln_b': _L0_attn_in['ln_b'], 'L0_ffn_ln_g': _L0_ffn_in['ln_g'], 'L0_ffn_ln_b': _L0_ffn_in['ln_b'], 'L0_ffn_aw1': _L0_ffn_in['aw1'], 'L0_ffn_ab1': _L0_ffn_in['ab1'], 'L0_ffn_aw2': _L0_ffn_in['aw2'], 'L0_ffn_ab2': _L0_ffn_in['ab2'], 'L0_ffn_gate_w': _L0_ffn_in['gate_w'], 'L0_ffn_gate_b': _L0_ffn_in['gate_b'], 'L0_ffn_ew1': _L0_ffn_in['ew1'], 'L0_ffn_eb1': _L0_ffn_in['eb1'], 'L0_ffn_ew2': _L0_ffn_in['ew2'], 'L0_ffn_eb2': _L0_ffn_in['eb2'], 'L0_ffn_gens': _L0_ffn_in['gens'], 'L0_ffn_gc_w': _L0_ffn_in['gc_w'], 'L0_ffn_gc_b': _L0_ffn_in['gc_b'], 'L0_c': _L0_c, 'L0_wmod': _L0_wmod}
    _x0 = _d['L0_attn_x']
    _d['L0_attn_x'] = jax.random.normal(jax.random.fold_in(jax.random.key(seed), 1), (8, 1024, 256), dtype=_x0.dtype)
    del _x0
    return _d

def reference(L0_attn_x, L0_attn_W_in, L0_attn_b_in, L0_attn_conv_w, L0_attn_conv_b, L0_attn_W_bc, L0_attn_b_bc, L0_attn_W_dt, L0_attn_b_dt, L0_attn_A_log, L0_attn_D, L0_attn_W_out, L0_attn_b_out, L0_attn_ln_g, L0_attn_ln_b, L0_ffn_ln_g, L0_ffn_ln_b, L0_ffn_aw1, L0_ffn_ab1, L0_ffn_aw2, L0_ffn_ab2, L0_ffn_gate_w, L0_ffn_gate_b, L0_ffn_ew1, L0_ffn_eb1, L0_ffn_ew2, L0_ffn_eb2, L0_ffn_gens, L0_ffn_gc_w, L0_ffn_gc_b, L0_c, L0_wmod):

    def _L0_attn_ref(x, W_in, b_in, conv_w, conv_b, W_bc, b_bc, W_dt, b_dt, A_log, D, W_out, b_out, ln_g, ln_b):
        import jax, jax.numpy as jnp
        import numpy as np
        D_MODEL, D_STATE, D_CONV = (256, 16, 4)
        BATCH, SEQ = (4, 512)
        LN_EPS = 1e-05

        def _causal_depthwise_conv(x_btd, conv_w, conv_b):
            x_bdt = jnp.transpose(x_btd, (0, 2, 1))
            y = jax.lax.conv_general_dilated(x_bdt, conv_w, window_strides=(1,), padding=[(D_CONV - 1, 0)], dimension_numbers=('NCH', 'OIH', 'NCH'), feature_group_count=D_MODEL)
            y = y + conv_b[None, :, None]
            return jnp.transpose(y, (0, 2, 1))

        def _mamba_forward(x, W_in, b_in, conv_w, conv_b, W_bc, b_bc, W_dt, b_dt, A_log, D, W_out, b_out, ln_g, ln_b):
            B_, T, _ = x.shape
            proj = x @ W_in + b_in
            x_ssm, x_gate = jnp.split(proj, 2, axis=-1)
            x_conv = jax.nn.silu(_causal_depthwise_conv(x_ssm, conv_w, conv_b))
            BC = x_conv @ W_bc + b_bc
            Bm, Cm = jnp.split(BC, 2, axis=-1)
            dt = jax.nn.softplus(x_conv @ W_dt + b_dt)
            A = -jnp.exp(A_log)

            def step(h, inp):
                xt, dtt, Bt, Ct = inp
                dA = jnp.exp(dtt[:, :, None] * A)
                h = h * dA + (dtt * xt)[:, :, None] * Bt[:, None, :]
                y = jnp.einsum('bdn,bn->bd', h, Ct) + xt * D
                return (h, y)
            h0 = jnp.zeros((B_, D_MODEL, D_STATE), x.dtype)
            xs = (jnp.swapaxes(x_conv, 0, 1), jnp.swapaxes(dt, 0, 1), jnp.swapaxes(Bm, 0, 1), jnp.swapaxes(Cm, 0, 1))
            _, ys = jax.lax.scan(step, h0, xs)
            y = jnp.swapaxes(ys, 0, 1)
            y = y * jax.nn.silu(x_gate)
            out = y @ W_out + b_out
            res = out + x
            mu = jnp.mean(res, axis=-1, keepdims=True)
            var = jnp.var(res, axis=-1, keepdims=True)
            return (res - mu) * jax.lax.rsqrt(var + LN_EPS) * ln_g + ln_b
        return _mamba_forward(x, W_in, b_in, conv_w, conv_b, W_bc, b_bc, W_dt, b_dt, A_log, D, W_out, b_out, ln_g, ln_b)

    def _L0_ffn_ref(x, ln_g, ln_b, aw1, ab1, aw2, ab2, gate_w, gate_b, ew1, eb1, ew2, eb2, gens, gc_w, gc_b):
        import jax, jax.numpy as jnp
        import numpy as np
        from jax.scipy.linalg import expm
        D = 256
        E = 6
        K = 2
        H = 2 * D
        A4 = 4 * D
        NROT = 4
        LN_EPS = 1e-05

        def _xavier(key, shape):
            fan_in, fan_out = (shape[-2], shape[-1])
            lim = np.sqrt(6.0 / (fan_in + fan_out))
            return jax.random.uniform(key, shape, jnp.float32, -lim, lim)

        def _layernorm(x, g, b):
            mu = jnp.mean(x, axis=-1, keepdims=True)
            var = jnp.var(x, axis=-1, keepdims=True)
            return (x - mu) * jax.lax.rsqrt(var + LN_EPS) * g + b

        def _moe(xn, gate_w, gate_b, ew1, eb1, ew2, eb2):
            logits = xn @ gate_w + gate_b
            tw, ti = jax.lax.top_k(logits, K)
            tw = jax.nn.softmax(tw, axis=-1)
            w_full = jnp.sum(tw[..., None] * jax.nn.one_hot(ti, E, dtype=tw.dtype), axis=-2)
            h = jax.nn.gelu(jnp.einsum('bsd,edh->besh', xn, ew1) + eb1[None, :, None, :], approximate=False)
            eo = jnp.einsum('besh,ehd->besd', h, ew2) + eb2[None, :, None, :]
            return jnp.einsum('bse,besd->bsd', w_full, eo)

        def _rotate(x, gens):
            for i in range(NROT):
                x = x @ expm(gens[i])
            return x
        residual = x
        xn = _layernorm(x, ln_g, ln_b)
        abel = jax.nn.gelu(xn @ aw1 + ab1, approximate=False) @ aw2 + ab2
        nonabel = _rotate(_moe(xn, gate_w, gate_b, ew1, eb1, ew2, eb2), gens)
        combined = jnp.concatenate([abel, nonabel], axis=-1)
        gate = jax.nn.sigmoid(combined @ gc_w + gc_b)
        mixed = abel * (1.0 - gate) + nonabel * gate
        return residual + mixed
    x = L0_attn_x
    mod = (_silu(L0_c) @ L0_wmod).reshape(L0_c.shape[0], 6, 1, -1)
    sa, ca, ga, sb, cb, gb = (mod[:, 0], mod[:, 1], mod[:, 2], mod[:, 3], mod[:, 4], mod[:, 5])
    ga = (2 * (ga >= 0) - 1) * jnp.maximum(jnp.abs(ga), 0.25)
    gb = (2 * (gb >= 0) - 1) * jnp.maximum(jnp.abs(gb), 0.25)
    h = _layernorm(x, axis=-1) * (1 + ca) + sa
    x = x + ga * _L0_attn_ref(h, L0_attn_W_in, L0_attn_b_in, L0_attn_conv_w, L0_attn_conv_b, L0_attn_W_bc, L0_attn_b_bc, L0_attn_W_dt, L0_attn_b_dt, L0_attn_A_log, L0_attn_D, L0_attn_W_out, L0_attn_b_out, L0_attn_ln_g, L0_attn_ln_b)
    h = _layernorm(x, axis=-1) * (1 + cb) + sb
    x = x + gb * _L0_ffn_ref(h, L0_ffn_ln_g, L0_ffn_ln_b, L0_ffn_aw1, L0_ffn_ab1, L0_ffn_aw2, L0_ffn_ab2, L0_ffn_gate_w, L0_ffn_gate_b, L0_ffn_ew1, L0_ffn_eb1, L0_ffn_ew2, L0_ffn_eb2, L0_ffn_gens, L0_ffn_gc_w, L0_ffn_gc_b)
    return x

_drawn_inputs = setup_inputs


def setup_inputs(seed=0):
    import zlib

    import numpy as np

    out = dict(_drawn_inputs(seed))
    spreads = {'L0_attn_b_in': (0.0, 0.1),
     'L0_attn_conv_b': (0.0, 0.288),
     'L0_attn_b_bc': (0.0, 0.1),
     'L0_attn_b_dt': (0.0, 0.8),
     'L0_attn_D': (1.0, 0.6),
     'L0_attn_b_out': (0.0, 0.408),
     'L0_attn_ln_g': (1.0, 0.2),
     'L0_attn_ln_b': (0.0, 0.309),
     'L0_ffn_ln_g': (1.0, 0.6),
     'L0_ffn_ln_b': (0.0, 0.543),
     'L0_ffn_ab1': (0.0, 0.783),
     'L0_ffn_ab2': (0.0, 0.664),
     'L0_ffn_gate_b': (0.0, 0.695),
     'L0_ffn_eb1': (0.0, 0.8),
     'L0_ffn_eb2': (0.0, 0.787)}
    factors = {}
    for name, (base, spread) in spreads.items():
        noise = np.random.default_rng([zlib.crc32(name.encode()), seed]).standard_normal(out[name].shape)
        drawn = base * np.exp(spread * noise) if base else spread * noise
        out[name] = jnp.asarray(drawn.astype(out[name].dtype))
    for name, factor in factors.items():
        out[name] = (out[name] * factor).astype(out[name].dtype)
    return out
```

```python
import concourse.bass as bass
from concourse import mybir
from contextlib import ExitStack
from math import factorial

f32 = mybir.dt.float32
f16 = mybir.dt.float16
bf16 = mybir.dt.bfloat16
ALU = mybir.AluOpType
ACT = mybir.ActivationFunctionType
AX = mybir.AxisListType.X


def build_adaln_mamba_moe(nc, a, out):
    NB, T, D = a["L0_attn_x"].shape
    NS = a["L0_attn_A_log"].shape[1]
    NE, _, H = a["L0_ffn_ew1"].shape
    HA = a["L0_ffn_aw1"].shape[1]
    P = 128
    KD = D // P
    CH = 512
    NT = CH // P
    CPB = T // CH
    NC = NB * CPB
    TAPS = a["L0_attn_conv_w"].shape[2]
    MA = HA // P
    ME = H // P
    MT = MA + NE * ME
    NOUT = NT + NE * NT
    D1 = D + 1
    RING = 6
    WS = 64.0
    EPS = 1e-5
    SQUARINGS = 4
    TAYLOR = 12
    NROT = a["L0_ffn_gens"].shape[0]
    assert CPB == 2 and KD == 2 and NT == 4 and NS == 16 and ME == 4 and MA == 8

    ctx = ExitStack()
    with ctx:
        def sb(name, shape, dt=f32):
            return ctx.enter_context(nc.sbuf_tensor(name, shape, dt))

        def pb(name, shape=(P, 512), dt=f32):
            return ctx.enter_context(nc.psum_tensor(name, list(shape), dt))

        def sem(name):
            return ctx.enter_context(nc.semaphore(name))

        w_in = sb("w_in", [P, KD, 2 * D])
        w_dt = sb("w_dt", [P, KD, D])
        w_bc = sb("w_bc", [P, KD, P])
        w_out = sb("w_out", [P, KD, D])
        w1h = sb("w1h", [P, KD, MT * P], f16)
        w1l = sb("w1l", [P, KD, MT * P], f16)
        w2 = sb("w2", [P, MT, D1])
        gate_w = sb("gate_w", [P, KD, NE])
        b1 = sb("b1", [P, MT])
        b_in = sb("b_in", [P, 4])
        b_gh = sb("b_gh", [P, KD])
        conv_w = sb("conv_w", [P, KD, TAPS])
        conv_b = sb("conv_b", [P, KD])
        b_dt = sb("b_dt", [P, KD])
        b_bc = sb("b_bc", [P, 1])
        neg_a = sb("neg_a", [P, KD, NS])
        d_skip = sb("d_skip", [P, KD])
        ln_g = sb("ln_g", [P, KD])
        ln_b = sb("ln_b", [P, KD])
        modT = sb("modT", [P, NB, 4])
        cur_mod = sb("cur_mod", [P, 4])
        b_out_bc = sb("b_out_bc", [P, D])
        ab2_bc = sb("ab2_bc", [P, D1])
        gate_b_bc = sb("gate_b_bc", [P, NE])
        gcb_half = sb("gcb_half", [P, 1])
        eb2r = sb("eb2r", [NE, D1])
        ident = sb("ident", [P, P])
        sel = sb("sel", [P, 2 * NS], bf16)
        before = sb("before", [P, NE, NE])
        after = sb("after", [P, NE, NE])
        neg_half = sb("neg_half", [P, NT])
        eps = sb("eps", [P, NT])
        spare = sb("spare", [P, 1])

        ring = sb("ring", [P, RING, KD, CH])
        u = sb("u", [P, KD, CH])
        xin = sb("xin", [P, NT, D])
        xr = sb("xr", [P, 2, NT, D])
        res = sb("res", [P, NT, D])
        h1T = sb("h1T", [P, 2, KD, CH])
        xs = sb("xs", [P, KD, TAPS - 1 + CH])
        xc = sb("xc", [P, KD, CH])
        th = sb("th", [P, KD, CH])
        sg = sb("sg", [P, KD, CH])
        bcs = sb("bcs", [P, 2, CH], bf16)
        bcf = sb("bcf", [P, CH])
        dt = sb("dt", [P, KD, CH])
        dtx = sb("dtx", [P, 2, KD, CH])
        xnT = sb("xnT", [P, KD, CH])
        xnh = sb("xnh", [P, KD, CH], f16)
        xnl = sb("xnl", [P, KD, CH], f16)
        rows = sb("rows", [P, 5, D])
        gb_fin = sb("gb_fin", [P, D])
        hid = sb("hid", [P, 2, ME, CH])
        ab = sb("ab", [P, NT, D1])
        na = sb("na", [P, NT, D1])
        y = sb("y", [P, KD, CH])
        state = sb("state", [P, NS, KD])
        st_f = sb("st_f", [P, NT, 6]); mv_f = sb("mv_f", [P, NT, 2]); rs_f = sb("rs_f", [P, NT])
        st_b = sb("st_b", [P, NT, 6]); mv_b = sb("mv_b", [P, NT, 2]); rs_b = sb("rs_b", [P, NT])
        lg = sb("lg", [P, NT, NE]); lgm = sb("lgm", [P, NT, 1]); lgs = sb("lgs", [P, NT, 1])
        rk = sb("rk", [P, NT, NE, NE]); rk2 = sb("rk2", [P, NT, NE, NE]); rsum = sb("rsum", [P, NT, NE])
        wE = sb("wE", [P, NT, NE])
        wT = bcf[0:NE, :]
        zs = sb("zs", [P, NT, 1])
        gt = sb("gt", [P, NT, 1])

        bcp = [pb(f"bcp{i}") for i in range(3)]
        hp = [pb(f"hp{i}") for i in range(2)]
        ep = [pb(f"ep{i}") for i in range(2)]
        misc = pb("misc")

        s_ld_mod = sem("s_ld_mod"); s_ld_attn = sem("s_ld_attn"); s_ld_ffn = sem("s_ld_ffn")
        s_ld_stage = [sem(f"s_ld_stage{i}") for i in range(2)]
        s_ld_gens = sem("s_ld_gens"); s_const = sem("s_const")
        s_mod_v = sem("s_mod_v"); s_mod_a = sem("s_mod_a"); s_mod_pe = sem("s_mod_pe")
        s_rows_out = sem("s_rows_out"); s_par_v = sem("s_par_v"); s_par_a = sem("s_par_a")
        s_hi = sem("s_hi"); s_lo = sem("s_lo")
        s_ex_pe = sem("s_ex_pe"); s_ex_v = sem("s_ex_v"); s_ex_q = sem("s_ex_q")
        s_v_pe = sem("s_v_pe"); s_v_ev = sem("s_v_ev")
        s_rt_pe = sem("s_rt_pe"); s_rt_ev = sem("s_rt_ev"); s_r_pe = sem("s_r_pe"); s_r_ev = sem("s_r_ev")
        s_aw = sem("s_aw")

        s_x_in = sem("s_x_in"); s_xr_in = [sem(f"s_xr_in{q}") for q in range(2)]; s_rows_in = sem("s_rows_in"); s_gbf_in = sem("s_gbf_in")
        s_out = sem("s_out")
        s_f_stat = sem("s_f_stat"); s_f_rstd = sem("s_f_rstd"); s_f_hat = sem("s_f_hat"); s_f_t = sem("s_f_t")
        s_curmod = sem("s_curmod"); s_h1 = sem("s_h1"); s_j = sem("s_j"); s_xs = sem("s_xs"); s_cv = sem("s_cv")
        s_th = sem("s_th"); s_xc = sem("s_xc"); s_bc_pe = sem("s_bc_pe"); s_bcf = sem("s_bcf"); s_bcs = sem("s_bcs")
        s_d_pe = sem("s_d_pe"); s_d_raw = sem("s_d_raw"); s_sp = sem("s_sp"); s_dt = sem("s_dt"); s_dtx = sem("s_dtx")
        s_g_pe = sem("s_g_pe"); s_gv = sem("s_gv"); s_gth = sem("s_gth"); s_sg = sem("s_sg")
        s_bb = sem("s_bb"); s_dA = sem("s_dA"); s_dbx = sem("s_dbx"); s_scan = sem("s_scan"); s_tail = sem("s_tail")
        s_hc = sem("s_hc"); s_y = sem("s_y"); s_yinit = sem("s_yinit"); s_y2 = sem("s_y2")
        s_o_pe = sem("s_o_pe"); s_res = sem("s_res"); s_b_stat = sem("s_b_stat"); s_b_rstd = sem("s_b_rstd")
        s_b_hat = sem("s_b_hat"); s_x1 = sem("s_x1"); s_h2 = sem("s_h2"); s_base = sem("s_base")
        s_x_t = sem("s_x_t"); s_xn = sem("s_xn"); s_xnl = sem("s_xnl")
        s_lg_pe = sem("s_lg_pe"); s_rt = sem("s_rt"); s_rexp = sem("s_rexp"); s_w = sem("s_w")
        s_wt_pe = sem("s_wt_pe"); s_wt = sem("s_wt"); s_n_pe = sem("s_n_pe"); s_na = sem("s_na")
        s_hid = sem("s_hid"); s_gelu = sem("s_gelu"); s_eo = sem("s_eo"); s_eo_ev = sem("s_eo_ev")
        s_zs = sem("s_zs"); s_gate = sem("s_gate"); s_wsum = sem("s_wsum"); s_gth4 = sem("s_gth4"); s_mix = sem("s_mix"); s_fin = sem("s_fin")

        rows_dram = nc.dram_tensor("mod_rows", (NB, 5 * D), f32, kind="Internal").ap()

        PLACE = [[n % RING for n in range(NS)], [4, 5, 0, 1, 2, 3, 4, 5, 0, 1, 4, 5, 2, 3, 4, 5]]

        def place_before(q, n):
            return next(m for m in range(n - 1, -NS - 1, -1) if PLACE[q if m >= 0 else 1 - q][m % NS] == PLACE[q][n])

        def on(c):
            return not isinstance(c, int) or 0 <= c < NC

        def wait(eng, s, value):
            if not isinstance(value, int) or value > 0:
                eng.wait_ge(s, value)

        def run_steps(eng, step):
            step(-1, 1)
            for it in range(0, LOOP0):
                step(it, 0)
                step(it, 1)
            if LOOP:
                with eng.Fori(LOOP0, LOOP1) as it:
                    step(it, 0)
                    step(it, 1)
            else:
                for it in range(LOOP0, LOOP1):
                    step(it, 0)
                    step(it, 1)
            for it in range(LOOP1, (NC + 4) // 2):
                step(it, 0)
                step(it, 1)
        LOOP = True
        LOOP0, LOOP1 = 2, (NC - 2) // 2

        MISC = [("logits", -2, s_rt, 5, 1), ("o0", -1, s_res, 2, 1), ("o1", -1, s_res, 2, 2),
                ("t0", 1, s_h1, 2, 1), ("t1", 1, s_h1, 2, 2), ("wt", -2, s_wt, 1, 1), ("j0", 1, s_xs, 2, 1),
                ("n0", -2, s_na, 4, 1), ("n1", -2, s_na, 4, 2), ("n2", -2, s_na, 4, 3), ("n3", -2, s_na, 4, 4),
                ("j1", 1, s_xs, 2, 2), ("g0", 0, s_gv, 2, 1), ("g1", 0, s_gv, 2, 2), ("bc", 1, s_bcf, 1, 1),
                ("d0", 1, s_d_raw, 4, 2), ("d1", 1, s_d_raw, 4, 4), ("x0", -1, s_xn, 4, 2), ("x1", -1, s_xn, 4, 4)]
        MISC_AT = {m[0]: i for i, m in enumerate(MISC)}

        def misc_free(eng, use, s):
            for back in range(1, 3 * len(MISC)):
                i = MISC_AT[use] - back
                steps_ago = -(i // len(MISC))
                _, delta, done, per, idx = MISC[i % len(MISC)]
                c = s - steps_ago + delta
                if on(c):
                    eng.wait_ge(done, per * c + idx)
                    return

        def xm(i, slot):
            n = i * 6 + slot
            if n < 12:
                return ring[:, n // 2, n % 2, :].rearrange("p (k c) -> p k c", k=KD)
            n -= 12
            if n < 8:
                return hid[:, n // 4, n % 4, :].rearrange("p (k c) -> p k c", k=KD)
            n -= 8
            return dtx[:, n // 2, n % 2, :].rearrange("p (k c) -> p k c", k=KD)
        eye = xnT[:, 0, :].rearrange("p (k c) -> p k c", k=KD)
        ex_bank = [bcp[0], bcp[1], bcp[2], hp[0]]
        N_GENS = 4
        stage = [hid[:, i, 0:2, :].rearrange("p a c -> p (a c)").rearrange("p (k c) -> p k c", k=KD) for i in range(2)]
        wmod_sb = ring[:, 0:3, :, :].rearrange("p a b c -> p (a b c)").rearrange("p (k c) -> p k c", k=KD)
        cT = ring[:, 3, 0, 0:KD * NB].rearrange("p (k b) -> p k b", k=KD)
        cTh = ring[:, 3, 0, 64:64 + KD * NB].rearrange("p (k b) -> p k b", k=KD)
        cTs = ring[:, 3, 0, 128:128 + KD * NB].rearrange("p (k b) -> p k b", k=KD)
        mrow = ring[0:NB, 4, :, :].rearrange("p a c -> p (a c)").rearrange("p (r c) -> p r c", r=4)
        lnrow = ring[0:NB, 5, 0, :].rearrange("p (r c) -> p r c", r=2)
        mtmp = ring[0:NB, 5, 1, :].rearrange("p (r c) -> p r c", r=2)
        prow = y[0:NB, :, :].rearrange("p k c -> p (k c)")[:, 0:4 * D].rearrange("p (r c) -> p r c", r=4)
        prow2 = sg[0:NB, 0, 0:D]
        sign = sg[0:NB, 1, 0:2 * D].rearrange("p (r c) -> p r c", r=2)
        aw_tmp = u[:, :, :].rearrange("p k c -> p (k c)").rearrange("p (t c) -> p t c", t=4)
        g1_bc = xin[:, 0, :]
        eb2T = xin[:, 1, 0:KD * NE].rearrange("p (k e) -> p k e", k=KD)
        V = [ab[:, 0:KD, :], na[:, 0:KD, :]]
        rT = [sg[:, i, :].rearrange("p (t k c) -> p t k c", t=2, k=KD) for i in range(2)]
        c_tay = [1.0 / factorial(j) for j in range(TAYLOR + 1)]
        SC = 2.0 ** -SQUARINGS

        def tok(c_half, b):
            return lambda t: t[b, c_half * CH:(c_half + 1) * CH, :].rearrange("(t p) d -> p t d", p=P)

        block = ctx.enter_context(nc.Block())

        @block.sync
        def _(sp):
            X = a["L0_attn_x"]
            n_mod = [0]

            def ld(s, dst, src):
                sp.dma_start(dst, src).then_inc(s, 16)

            colk = lambda v: v.rearrange("(k p) -> p k", p=P)
            with nc.allow_non_contiguous_dma(reason="small parameters, once"):
                ld(s_ld_mod, wmod_sb, a["L0_wmod"].rearrange("(k p) n -> p k n", p=P))
                for k in range(KD):
                    ld(s_ld_mod, cT[:, k, :], a["L0_c"][:, k * P:(k + 1) * P].rearrange("b p -> p b"))
                ld(s_ld_mod, lnrow[:, 0, :], a["L0_attn_ln_g"].partition_broadcast(NB))
                ld(s_ld_mod, lnrow[:, 1, :], a["L0_attn_ln_b"].partition_broadcast(NB))
                ld(s_ld_attn, w_in[:], a["L0_attn_W_in"].rearrange("(k p) n -> p k n", p=P))
                ld(s_ld_attn, w_dt[:], a["L0_attn_W_dt"].rearrange("(k p) n -> p k n", p=P))
                for r in range(4):
                    ld(s_ld_attn, w_bc[:, :, r * 2 * NS:(r + 1) * 2 * NS],
                       a["L0_attn_W_bc"].rearrange("(k p) n -> p k n", p=P))
                    ld(s_ld_attn, b_bc[r * 2 * NS:(r + 1) * 2 * NS, :],
                       a["L0_attn_b_bc"].rearrange("(n o) -> n o", o=1))
                ld(s_ld_attn, w_out[:], a["L0_attn_W_out"].rearrange("(k p) n -> p k n", p=P))
                ld(s_ld_attn, b_in[:], colk(a["L0_attn_b_in"]))
                ld(s_ld_attn, conv_w[:], a["L0_attn_conv_w"].rearrange("(k p) o t -> p k (o t)", p=P))
                ld(s_ld_attn, conv_b[:], colk(a["L0_attn_conv_b"]))
                ld(s_ld_attn, b_dt[:], colk(a["L0_attn_b_dt"]))
                ld(s_ld_attn, neg_a[:], a["L0_attn_A_log"].rearrange("(k p) n -> p k n", p=P))
                ld(s_ld_attn, d_skip[:], colk(a["L0_attn_D"]))
                ld(s_ld_attn, b_out_bc[:], a["L0_attn_b_out"].partition_broadcast(P))
                ld(s_ld_ffn, ln_g[:], colk(a["L0_ffn_ln_g"]))
                ld(s_ld_ffn, ln_b[:], colk(a["L0_ffn_ln_b"]))
                ld(s_ld_ffn, gate_w[:], a["L0_ffn_gate_w"].rearrange("(k p) e -> p k e", p=P))
                ld(s_ld_ffn, gate_b_bc[:], a["L0_ffn_gate_b"].partition_broadcast(P))
                ld(s_ld_ffn, gcb_half[:], a["L0_ffn_gc_b"].partition_broadcast(P))
                ld(s_ld_ffn, ab2_bc[:, 0:D], a["L0_ffn_ab2"].partition_broadcast(P))
                ld(s_ld_ffn, b1[:, 0:MA], a["L0_ffn_ab1"].rearrange("(m p) -> p m", p=P))
                ld(s_ld_ffn, b1[:, MA:MT], a["L0_ffn_eb1"].rearrange("e (m p) -> p (e m)", p=P))
                ld(s_ld_ffn, g1_bc, a["L0_ffn_gc_w"][0:D, :].rearrange("d o -> (d o)").partition_broadcast(P))
                ld(s_ld_ffn, V[0][:, :, D:D1], a["L0_ffn_gc_w"][D:2 * D, :].rearrange("(k p) o -> p k o", p=P))
                for k in range(KD):
                    ld(s_ld_ffn, eb2T[:, k, :], a["L0_ffn_eb2"][:, k * P:(k + 1) * P].rearrange("e p -> p e"))
                ld(s_ld_ffn, w2[:, 0:MA, 0:D], a["L0_ffn_aw2"].rearrange("(m p) d -> p m d", p=P))
                for e in range(NE):
                    ld(s_ld_ffn, w2[:, MA + e * ME:MA + (e + 1) * ME, 0:D],
                       a["L0_ffn_ew2"][e].rearrange("(m p) d -> p m d", p=P))
                for j in range(MT // ME):
                    if j >= 2:
                        sp.wait_ge(s_lo, j - 1)
                        sp.wait_ge(s_hi, j - 1)
                    src = a["L0_ffn_aw1"][:, j * H:(j + 1) * H] if j < 2 else a["L0_ffn_ew1"][j - 2]
                    ld(s_ld_stage[j % 2], stage[j % 2], src.rearrange("(k p) n -> p k n", p=P))
                sp.wait_ge(s_hi, MT // ME)
                sp.wait_ge(s_lo, MT // ME)
                sp.wait_ge(s_mod_v, 12)
                for i in range(NROT):
                    ld(s_ld_gens, xm(i, 0), a["L0_ffn_gens"][i].rearrange("(k p) n -> p k n", p=P))
                sp.wait_ge(s_mod_v, 12)
                sp.dma_start(rows_dram[:, 0:4 * D].rearrange("b (r c) -> b r c", r=4), prow).then_inc(s_rows_out, 16)
                sp.dma_start(rows_dram[:, 4 * D:5 * D], prow2).then_inc(s_rows_out, 16)
                sp.wait_ge(s_rows_out, 32)
                sp.dma_start(rows[:], rows_dram[0, :].partition_broadcast(P).rearrange("p (r c) -> p r c", r=5))\
                    .then_inc(s_rows_in, 16)
                sp.dma_start(gb_fin[:], rows_dram[0, 4 * D:5 * D].partition_broadcast(P)).then_inc(s_gbf_in, 16)
                sp.wait_ge(s_aw, 6)
                sp.wait_ge(s_r_pe, 1)
                sp.dma_start(xin[:], tok(0, 0)(X)).then_inc(s_x_in, 16)

            def step(it, r):
                s = 2 * it + r
                batch = lambda d: it + (r + d) // 2
                par = lambda d: (r + d) % 2
                if on(s - 1):
                    wait(sp, s_fin, 2 * (s - 2))
                    sp.dma_start(xr[:, par(-1), :, :], tok(par(-1), batch(-1))(X)).then_inc(s_xr_in[par(-1)], 16)
                if on(s - 3) and r == 0 and on(s - 2):
                    wait(sp, s_fin, 2 * (s - 2))
                    sp.dma_start(gb_fin[:], rows_dram[batch(-2), 4 * D:5 * D].partition_broadcast(P))\
                        .then_inc(s_gbf_in, 16)
                if on(s + 2):
                    wait(sp, s_f_t, 2 * (s + 2))
                    sp.dma_start(xin[:], tok(par(2), batch(2))(X)).then_inc(s_x_in, 16)
                if r == 0 and on(s - 1) and on(s):
                    wait(sp, s_base, 2 * (s - 1) + 2)
                    sp.dma_start(rows[:], rows_dram[batch(0), :].partition_broadcast(P)
                                 .rearrange("p (r c) -> p r c", r=5)).then_inc(s_rows_in, 16)
            run_steps(sp, step)

        N_LD_MOD = 16 * (1 + KD + 2)
        N_LD_ATTN = 16 * (2 + 8 + 8)
        N_LD_FFN = 16 * (10 + KD + 1 + NE)

        @block.gpsimd
        def _(g):
            G = nc.gpsimd
            G.memset(ident[:], 0.0).then_inc(s_const, 1)
            G.memset(sel[:], 0.0).then_inc(s_const, 1)
            G.memset(before[:], 0.0).then_inc(s_const, 1)
            G.memset(after[:], 0.0).then_inc(s_const, 1)
            G.memset(neg_half[:], -0.5).then_inc(s_const, 1)
            G.memset(eps[:], EPS).then_inc(s_const, 1)
            G.memset(xs[:, :, 0:TAPS - 1], 0.0).then_inc(s_const, 1)
            g.wait_ge(s_const, 7)
            G.affine_select(out=ident[:], in_=ident[:], compare_op=ALU.not_equal, fill=1.0, base=0,
                            pattern=[[-1, P]], channel_multiplier=1).then_inc(s_const, 1)
            for e in range(1, NE):
                G.memset(before[:, e, 0:e], 1.0).then_inc(s_const, 1)
                G.memset(after[:, e - 1, e:NE], 1.0).then_inc(s_const, 1)
            n0 = 8 + 2 * (NE - 1)
            for n, r in enumerate((0, 2, 3)):
                g.wait_ge(s_const, n0 + n)
                G.affine_select(out=sel[:], in_=sel[:], compare_op=ALU.not_equal, fill=1.0, base=-r * 2 * NS,
                                pattern=[[-1, 2 * NS]], channel_multiplier=1).then_inc(s_const, 1)

            def rstd(mv, rs, ready, value, done, per_c):
                g.wait_ge(ready, value)
                G.tensor_tensor(rs[:], mv[:, :, 1], eps[:], ALU.add).then_inc(done, 1)
                g.wait_ge(done, per_c + 1)
                G.tensor_tensor(rs[:], rs[:], neg_half[:], ALU.pow).then_inc(done, 1)

            tmp_rows = xnT[:, :, :].rearrange("p k c -> p (k c)").rearrange("p (t d) -> p t d", t=NT)

            def row(r):
                return rows[:, r:r + 1, :].to_broadcast([P, NT, D])

            g.wait_ge(s_ld_attn, N_LD_ATTN)
            g.wait_ge(s_rows_out, 32)

            def step(it, r):
                s = 2 * it + r
                par = lambda d: (r + d) % 2
                for n in range(NS):
                    if n == 0:
                        if on(s - 1):
                            g.wait_ge(s_sg, 2 * (s - 1) + 2)
                            g.wait_ge(s_y, 2 * NS * (s - 1) + 2 * NS)
                            for k in range(KD):
                                G.tensor_tensor(sg[:, k, :], sg[:, k, :], y[:, k, :], ALU.mult).then_inc(s_y2, 1)
                        if on(s):
                            g.wait_ge(s_xc, 2 * s + 2)
                            wait(g, s_y2, 2 * s)
                            for k in range(KD):
                                G.tensor_tensor(y[:, k, :], xc[:, k, :], d_skip[:, k:k + 1].to_broadcast([P, CH]), ALU.mult)\
                                    .then_inc(s_yinit, 1)
                    if on(s):
                        for k in range(KD):
                            i = 2 * NS * s + 2 * n + k
                            g.wait_ge(s_hc, i + 1)
                            if n == 0:
                                g.wait_ge(s_yinit, 2 * s + k + 1)
                            else:
                                g.wait_ge(s_y, i - 1)
                            G.tensor_tensor(y[:, k, :], y[:, k, :], ring[:, PLACE[par(0)][n], k, :], ALU.add).then_inc(s_y, 1)
                    if n == 0 and on(s + 1):
                        rstd(mv_f, rs_f, s_f_stat, 8 * (s + 1) + 8, s_f_rstd, 2 * (s + 1))
                    if n == 2 and on(s - 3):
                        c = s - 3
                        g.wait_ge(s_mix, 5 * c + 5)
                        g.wait_ge(s_gbf_in, 16 * (it + (r - 3) // 2) + 16)
                        G.tensor_tensor(na[:, :, 0:D], na[:, :, 0:D], gb_fin[:, :].unsqueeze(1).to_broadcast([P, NT, D]),
                                        ALU.mult).then_inc(s_fin, 1)
                        g.wait_ge(s_fin, 2 * c + 1)
                        G.tensor_tensor(na[:, :, 0:D], xr[:, par(-3), :, :], na[:, :, 0:D], ALU.add)\
                            .then_inc(s_fin, 1)
                    if on(s - 1):
                        c = s - 1
                        X = xr[:, par(-1), :, :]
                        if n == 3:
                            rstd(mv_b, rs_b, s_b_stat, 24 * c + 8, s_b_rstd, 6 * c)
                        if n == 5:
                            g.wait_ge(s_b_hat, 12 * c + 4)
                            g.wait_ge(s_rows_in, 16 * (it + (r - 1) // 2) + 16)
                            g.wait_ge(s_xr_in[par(-1)], 16 * (it + (r - 1) // 2) + 16)
                            G.tensor_tensor(res[:], res[:], row(0), ALU.mult).then_inc(s_x1, 1)
                            G.tensor_tensor(X, X, row(1), ALU.add).then_inc(s_x1, 1)
                            g.wait_ge(s_x1, 3 * c + 2)
                            G.tensor_tensor(X, X, res[:], ALU.add).then_inc(s_x1, 1)
                        if n == 8:
                            rstd(mv_b, rs_b, s_b_stat, 24 * c + 16, s_b_rstd, 6 * c + 2)
                        if n == 10:
                            g.wait_ge(s_b_hat, 12 * c + 8)
                            G.tensor_tensor(res[:], res[:], row(2), ALU.mult).then_inc(s_h2, 1)
                            g.wait_ge(s_h2, 2 * c + 1)
                            G.tensor_tensor(res[:], res[:], row(3), ALU.add).then_inc(s_h2, 1)
                            g.wait_ge(s_h2, 2 * c + 2)
                            wait(g, s_lg_pe, c)
                            wait(g, s_xnl, 2 * c)
                            G.tensor_tensor(tmp_rows, res[:], row(4), ALU.mult).then_inc(s_base, 1)
                        if n == 11:
                            rstd(mv_b, rs_b, s_b_stat, 24 * c + 24, s_b_rstd, 6 * c + 4)
                    if n == 12 and on(s - 1):
                        c = s - 1
                        g.wait_ge(s_base, 2 * c + 1)
                        G.tensor_tensor(X, X, tmp_rows, ALU.add).then_inc(s_base, 1)
                    if n == 14 and on(s + 1):
                        c = s + 1
                        for k in range(KD):
                            g.wait_ge(s_sp, 2 * c + 2)
                            G.tensor_tensor(dt[:, k, :], dt[:, k, :], th[:, k, :], ALU.add).then_inc(s_dt, 1)
                        for k in range(KD):
                            g.wait_ge(s_dt, 2 * c + k + 1)
                            G.tensor_tensor(dtx[:, par(1), k, :], dt[:, k, :], xc[:, k, :], ALU.mult)\
                                .then_inc(s_dtx, 1)
            run_steps(g, step)

        @block.tensor
        def _(pe):
            M = nc.tensor.matmul
            TR = nc.tensor.transpose
            pe.wait_ge(s_mod_v, 2)
            for j in range(4):
                for k in range(KD):
                    last = M(misc[:, j * NB:(j + 1) * NB], wmod_sb[:, k, j * P:(j + 1) * P], cTs[:, k, :],
                             start=(k == 0), stop=(k == KD - 1))
            last.then_inc(s_mod_pe, 1)
            for h in range(2):
                for k in range(KD):
                    last = M(ep[h][0:NB, :], cTs[:, k, :], wmod_sb[:, k, 512 * (h + 1):512 * (h + 2)],
                             start=(k == 0), stop=(k == KD - 1))
                last.then_inc(s_mod_pe, 1)

            pe.wait_ge(s_const, 8)
            pe.wait_ge(s_ld_gens, 16 * NROT)
            rnd = [0]

            def turn(i):
                if rnd[0]:
                    pe.wait_ge(s_ex_v, NROT * (rnd[0] - 1) + i + 1)

            def transpose_all(src):
                for i in range(NROT):
                    turn(i)
                    for kr in range(KD):
                        for kc in range(KD):
                            last = TR(ex_bank[i][:, kc * D + kr * P:kc * D + (kr + 1) * P],
                                      xm(i, src)[:, kr, kc * P:(kc + 1) * P], ident[:])
                    last.then_inc(s_ex_pe, 1)
                rnd[0] += 1

            def product_all(lhsT, rhs):
                for i in range(NROT):
                    turn(i)
                    for m in range(KD):
                        for k in range(KD):
                            last = M(ex_bank[i][:, m * D:(m + 1) * D], xm(i, lhsT)[:, k, m * P:(m + 1) * P],
                                     xm(i, rhs)[:, k, :], start=(k == 0), stop=(k == KD - 1))
                    last.then_inc(s_ex_pe, 1)
                rnd[0] += 1
            transpose_all(0)
            product_all(1, 0)
            product_all(2, 1)
            product_all(1, 2)
            for _ in range(TAYLOR // 3 - 1):
                product_all(3, 4)
            for _ in range(SQUARINGS):
                transpose_all(4)
                product_all(5, 4)
            transpose_all(4)
            for j, i in enumerate(reversed(range(NROT))):
                if j == 0:
                    pe.wait_ge(s_ex_v, NROT * rnd[0])
                    pe.wait_ge(s_ld_ffn, N_LD_FFN)
                pe.wait_ge(s_v_ev, 2 * j + 1)
                for m in range(KD):
                    for k in range(KD):
                        last = M(ep[m][:, 0:D1], xm(i, 5)[:, k, m * P:(m + 1) * P], V[j % 2][:, k, :],
                                 start=(k == 0), stop=(k == KD - 1))
                    last.then_inc(s_v_pe, 1)
            pe.wait_ge(s_v_ev, 2 * NROT + 1)
            pe.wait_ge(s_mod_a, 2)
            R = V[NROT % 2]
            for k in range(KD):
                last = M(misc[0:NE, 0:D1], eb2T[:, k, :], R[:, k, :], start=(k == 0), stop=(k == KD - 1))
            last.then_inc(s_r_pe, 1)
            for j in range((MT - MA) // 2 + 1):
                if j < (MT - MA) // 2:
                    if j >= 2:
                        pe.wait_ge(s_rt_ev, j - 1)
                    for t in range(2):
                        for k in range(KD):
                            last = TR(bcp[j % 2][:, (2 * t + k) * P:(2 * t + k + 1) * P],
                                      w2[:, MA + 2 * j + t, k * P:(k + 1) * P], ident[:])
                    last.then_inc(s_rt_pe, 1)
                if j >= 1:
                    jj = j - 1
                    pe.wait_ge(s_rt_ev, jj + 1)
                    for t in range(2):
                        if jj >= 1:
                            pe.wait_ge(s_r_ev, 2 * (jj - 1) + t + 2)
                        for k in range(KD):
                            last = M(hp[t][:, 0:D1], rT[jj % 2][:, t, k, :], R[:, k, :], start=(k == 0), stop=(k == KD - 1))
                        last.then_inc(s_r_pe, 1)
            pe.wait_ge(s_r_ev, MT - MA + 1)
            pe.wait_ge(s_hi, MT // ME)
            pe.wait_ge(s_lo, MT // ME)
            pe.wait_ge(s_const, 8 + 2 * (NE - 1) + 3)
            pe.wait_ge(s_ld_attn, N_LD_ATTN)
            pe.wait_ge(s_mod_a, 2)
            pe.wait_ge(s_aw, 6)

            def spread(c, n, j, q):
                i = 2 * n + j
                prev = i - 3 if i >= 3 else {0: 30, 1: 31, 2: 29}[i] - 2 * NS
                if prev % 2 == 0:
                    wait(pe, s_dbx, 2 * NS * c + (prev - prev % 2) + 2)
                else:
                    wait(pe, s_hc, 2 * NS * c + (prev - prev % 2) + 2)
                M(bcp[i % 3][:], sel[:, j * NS + n:j * NS + n + 1].to_broadcast([P, P]), bcs[:, q, :],
                  start=True, stop=True).then_inc(s_bb, 1)

            def step(it, r):
                s = 2 * it + r
                par = lambda d: (r + d) % 2
                f, sc, b, m = s + 1, s, s - 1, s - 2

                def small(use):
                    misc_free(pe, use, s)
                    if use == "logits":
                        pe.wait_ge(s_xn, 4 * m + 4)
                        for t in range(NT):
                            for k in range(KD):
                                last = M(misc[:, t * 8:t * 8 + NE], xnT[:, k, t * P:(t + 1) * P], gate_w[:, k, :],
                                         start=(k == 0), stop=(k == KD - 1))
                        last.then_inc(s_lg_pe, 1)
                    elif use in ("o0", "o1"):
                        pe.wait_ge(s_y2, 2 * b + 2)
                        for t in range(2):
                            tt = 2 * (use == "o1") + t
                            ts = slice(tt * P, (tt + 1) * P)
                            for k in range(KD):
                                M(misc[:, t * D:(t + 1) * D], sg[:, k, ts], w_out[:, k, :], start=(k == 0), stop=False)
                            for k in range(KD):
                                last = M(misc[:, t * D + k * P:t * D + (k + 1) * P], h1T[:, par(-1), k, ts], ident[:],
                                         start=False, stop=(k == KD - 1))
                        last.then_inc(s_o_pe, 1)
                    elif use in ("t0", "t1"):
                        k = int(use[1])
                        pe.wait_ge(s_f_hat, 4 * f + 4)
                        for t in range(NT):
                            last = TR(misc[:, t * P:(t + 1) * P], xin[:, t, k * P:(k + 1) * P], ident[:])
                        last.then_inc(s_f_t, 1)
                    elif use in ("j0", "j1", "g0", "g1"):
                        j = int(use[1]) + 2 * (use[0] == "g")
                        c, q, done = (f, par(1), s_j) if use[0] == "j" else (sc, par(0), s_g_pe)
                        pe.wait_ge(s_h1, 2 * c + 2)
                        for k in range(KD):
                            last = M(misc[:], w_in[:, k, j * P:(j + 1) * P], h1T[:, q, k, :],
                                     start=(k == 0), stop=(k == KD - 1))
                        last.then_inc(done, 1)
                    elif use == "bc":
                        pe.wait_ge(s_xc, 2 * f + 2)
                        for k in range(KD):
                            last = M(misc[0:P, :], w_bc[:, k, :], xc[:, k, :], start=(k == 0), stop=(k == KD - 1))
                        last.then_inc(s_bc_pe, 1)
                    elif use in ("d0", "d1"):
                        j = int(use[1])
                        for k in range(KD):
                            last = M(misc[:], w_dt[:, k, j * P:(j + 1) * P], xc[:, k, :], start=(k == 0), stop=(k == KD - 1))
                        last.then_inc(s_d_pe, 1)
                    elif use in ("x0", "x1"):
                        k = int(use[1])
                        pe.wait_ge(s_b_hat, 12 * b + 12)
                        for t in range(NT):
                            last = TR(misc[:, t * P:(t + 1) * P], res[:, t, k * P:(k + 1) * P], ident[:])
                        last.then_inc(s_x_t, 1)
                    elif use == "wt":
                        pe.wait_ge(s_w, 3 * m + 3)
                        for t in range(NT):
                            last = TR(misc[0:NE, t * P:(t + 1) * P], wE[:, t, :], ident[:])
                        last.then_inc(s_wt_pe, 1)
                    else:
                        t = int(use[1])
                        pe.wait_ge(s_wt, m + 1)
                        M(misc[:, 0:D1], wT[:, t * P:(t + 1) * P], eb2r[:], start=True, stop=True).then_inc(s_n_pe, 1)

                def hidden(j, half):
                    for mm in (2 * half, 2 * half + 1):
                        h = ME * j + mm
                        wait(pe, s_gelu, MT * m + h - 1)
                        if h == 0:
                            pe.wait_ge(s_xnl, 2 * m + 2)
                        ms = slice(h * P, (h + 1) * P)
                        n = 0
                        for wpart, xpart in ((w1h, xnh), (w1h, xnl), (w1l, xnh)):
                            for k in range(KD):
                                last = M(hp[h % 2][:], wpart[:, k, ms], xpart[:, k, :], start=(n == 0), stop=(n == 5))
                                n += 1
                        last.then_inc(s_hid, 1)

                def second(o):
                    j0, nk, t = (0, MA, o) if o < NT else (2 + (o - NT) // NT, ME, (o - NT) % NT)
                    wait(pe, s_eo_ev, NOUT * m + o - 1)
                    pe.wait_ge(s_gelu, MT * m + ME * j0 + nk)
                    for kk in range(nk):
                        last = M(ep[o % 2][:, 0:D1], hid[:, (j0 + kk // ME) % 2, kk % ME, t * P:(t + 1) * P],
                                 w2[:, ME * j0 + kk, :], start=(kk == 0), stop=(kk == nk - 1))
                    last.then_inc(s_eo, 1)

                before_main = {0: ["logits"], 1: ["o0"], 2: ["o1"], 3: ["t0"], 4: ["wt"], 5: ["n0"], 6: ["n3"],
                               7: ["g0"], 8: ["g1"], 10: ["bc"], 12: ["d0"], 14: ["x0"]}
                amid = {3: ["t1"], 4: ["j0"], 5: ["n1"], 6: ["j1"], 12: ["d1"], 14: ["x1"]}
                at_end = {5: ["n2"]}

                def smalls(uses):
                    for use in uses:
                        if on(s + MISC[MISC_AT[use]][1]):
                            small(use)
                for n in range(NS):
                    if on(sc):
                        if n == 0:
                            pe.wait_ge(s_bcs, 4 * sc + 4)
                            spread(sc, 0, 0, par(0))
                        spread(sc, n, 1, par(0))
                        if n + 1 < NS:
                            spread(sc, n + 1, 0, par(0))
                    grp, i = n // 4, n % 4
                    smalls(before_main.get(n, []))
                    if on(m):
                        if i < 2:
                            hidden(2 * grp + i, 0)
                        elif grp == 0:
                            second(2 * (i - 2))
                        else:
                            for t in range(2):
                                second(NT + NT * (2 * grp + i - 4) + t)
                    smalls(amid.get(n, []))
                    if on(m):
                        if i < 2:
                            hidden(2 * grp + i, 1)
                        elif grp == 0:
                            second(2 * (i - 2) + 1)
                        else:
                            for t in range(2, 4):
                                second(NT + NT * (2 * grp + i - 4) + t)
                    smalls(at_end.get(n, []))
            run_steps(pe, step)

        @block.scalar
        def _(act):
            A = nc.scalar.activation
            act.wait_ge(s_ld_mod, N_LD_MOD)
            A(cTh, cT, ACT.Tanh, scale=0.5).then_inc(s_mod_a, 1)
            for j in range(MT // ME):
                act.wait_ge(s_ld_stage[j % 2], 16 * (j // 2 + 1))
                A(w1h[:, :, j * H:(j + 1) * H], stage[j % 2], ACT.Copy, scale=WS).then_inc(s_hi, 1)
            act.wait_ge(s_mod_pe, 3)
            A(modT[:, :, :].rearrange("p b j -> p j b"), misc[:, 0:4 * NB].rearrange("p (j b) -> p j b", j=4), ACT.Copy)\
                .then_inc(s_mod_a, 1)
            act.wait_ge(s_ld_attn, N_LD_ATTN)
            act.wait_ge(s_ld_ffn, N_LD_FFN)
            A(neg_a[:], neg_a[:], ACT.Exp).then_inc(s_par_a, 1)
            A(b_gh[:], b_in[:, 2:4], ACT.Copy, scale=0.5).then_inc(s_par_a, 1)
            A(gcb_half[:], gcb_half[:], ACT.Copy, scale=0.5).then_inc(s_par_a, 1)
            act.wait_ge(s_rows_out, 32)
            for j in range((MT - MA) // 2):
                act.wait_ge(s_rt_pe, j + 1)
                if j >= 2:
                    act.wait_ge(s_r_pe, 2 * (j - 1) + 1)
                A(rT[j % 2], bcp[j % 2][:].rearrange("p (t k c) -> p t k c", t=2, k=KD), ACT.Copy).then_inc(s_rt_ev, 1)
            act.wait_ge(s_par_v, 5)

            def exps(c, n, q):
                for k in range(KD):
                    if k == 0:
                        act.wait_ge(s_dt, 2 * c + 2)
                        wait(act, s_y, 2 * NS * c + 2 * place_before(q, n) + 2)
                    A(ring[:, PLACE[q][n], k, :], dt[:, k, :], ACT.Exp, scale=neg_a[:, k, n:n + 1]).then_inc(s_dA, 1)

            def step(it, r):
                s = 2 * it + r
                par = lambda d: (r + d) % 2
                f, sc, b, m, o = s + 1, s, s - 1, s - 2, s - 3

                def small(use):
                    if use in ("t0", "t1"):
                        k = int(use[1])
                        if k == 0 and (r + 1) % 2 == 0:
                            bt = it + (r + 1) // 2
                            if not (isinstance(bt, int) and bt == 0):
                                wait(act, s_h1, 2 * f)
                            A(cur_mod[:, :], modT[:, bass.ds(bt, 1), :].rearrange("p o j -> p (o j)"), ACT.Copy)\
                                .then_inc(s_curmod, 1)
                            act.wait_ge(s_curmod, bt + 1)
                        act.wait_ge(s_f_t, 2 * f + k + 1)
                        wait(act, s_o_pe, 2 * f - 2)
                        A(h1T[:, par(1), k, :], misc[:], ACT.Identity, bias=cur_mod[:, k:k + 1],
                          scale=cur_mod[:, 2 + k:3 + k]).then_inc(s_h1, 1)
                    elif use in ("j0", "j1"):
                        k = int(use[1])
                        act.wait_ge(s_j, 2 * f + k + 1)
                        wait(act, s_cv, 9 * f)
                        A(xs[:, k, TAPS - 1:], misc[:], ACT.Identity, bias=b_in[:, k:k + 1]).then_inc(s_xs, 1)
                    elif use in ("g0", "g1"):
                        k = int(use[1])
                        act.wait_ge(s_g_pe, 2 * sc + k + 1)
                        wait(act, s_o_pe, 2 * sc)
                        A(sg[:, k, :], misc[:], ACT.Identity, bias=b_gh[:, k:k + 1], scale=0.5).then_inc(s_gv, 1)
                    elif use == "wt":
                        act.wait_ge(s_wt_pe, m + 1)
                        wait(act, s_bcs, 4 * (sc + 1) if on(sc) else 0)
                        A(wT[:], misc[0:NE, :], ACT.Copy).then_inc(s_wt, 1)
                    elif use[0] == "n":
                        t = int(use[1])
                        act.wait_ge(s_n_pe, 4 * m + t + 1)
                        wait(act, s_out, 16 * m)
                        A(na[:, t, :], misc[:, 0:D1], ACT.Copy).then_inc(s_na, 1)
                    elif use == "bc":
                        act.wait_ge(s_bc_pe, f + 1)
                        wait(act, s_bcs, 4 * f)
                        A(bcf[:], misc[0:P, :], ACT.Identity, bias=b_bc[:]).then_inc(s_bcf, 1)
                    elif use in ("d0", "d1"):
                        k = int(use[1])
                        act.wait_ge(s_d_pe, 2 * f + k + 1)
                        wait(act, s_sg, 2 * f)
                        wait(act, s_dtx, 2 * f)
                        wait(act, s_dA, 2 * NS * f)
                        A(dt[:, k, :], misc[:], ACT.Relu, bias=b_dt[:, k:k + 1]).then_inc(s_d_raw, 1)
                        A(th[:, k, :], misc[:], ACT.Abs, bias=b_dt[:, k:k + 1]).then_inc(s_d_raw, 1)
                    elif use in ("x0", "x1"):
                        k = int(use[1])
                        act.wait_ge(s_x_t, 2 * b + k + 1)
                        wait(act, s_hid, MT * b)
                        act.wait_ge(s_base, 2 * b + 2)
                        A(xnT[:, k, :], misc[:], ACT.Identity, bias=ln_b[:, k:k + 1], scale=ln_g[:, k:k + 1])\
                            .then_inc(s_xn, 1)
                        A(xnh[:, k, :], misc[:], ACT.Identity, bias=ln_b[:, k:k + 1], scale=ln_g[:, k:k + 1])\
                            .then_inc(s_xn, 1)

                def gelus(j, half):
                    if not on(m):
                        return
                    for mm in (2 * half, 2 * half + 1):
                        h = ME * j + mm
                        act.wait_ge(s_hid, MT * m + h + 1)
                        if mm == 0:
                            read = NOUT * m + (-NT * (1 - j) if j < 2 else NT if j < 4 else NT + NT * (j - 3))
                            wait(act, s_eo, read)
                        A(hid[:, j % 2, mm, :], hp[h % 2][:], ACT.Gelu, bias=b1[:, h:h + 1], scale=1.0 / WS)\
                            .then_inc(s_gelu, 1)

                def smalls(uses):
                    for use in uses:
                        if on(s + MISC[MISC_AT[use]][1]):
                            small(use)
                before_main = {3: ["t0"], 4: ["wt"], 5: ["n0"], 6: ["n3"],
                               7: ["g0"], 8: ["g1"], 10: ["bc"], 12: ["d0"], 14: ["x0"]}
                amid = {3: ["t1"], 4: ["j0"], 5: ["n1"], 6: ["j1"], 12: ["d1"], 14: ["x1"]}
                at_end = {5: ["n2"]}
                for n in range(NS):
                    grp, i = n // 4, n % 4
                    smalls(before_main.get(n, []))
                    if i < 2:
                        gelus(2 * grp + i, 0)
                    if n == 0 and on(o):
                        act.wait_ge(s_zs, o + 1)
                        A(gt[:], zs[:], ACT.Tanh, scale=0.5, bias=gcb_half[:]).then_inc(s_gth4, 1)
                    if n == 2 and on(m):
                        act.wait_ge(s_rt, 5 * m + 4)
                        A(wE[:], lg[:], ACT.Exp).then_inc(s_rexp, 1)
                    if n == 14 and on(f):
                        act.wait_ge(s_d_raw, 4 * f + 4)
                        A(th[:], th[:], ACT.Exp, scale=-1.0).then_inc(s_sp, 1)
                        act.wait_ge(s_sp, 2 * f + 1)
                        A(th[:], th[:], ACT.Ln, bias=1.0).then_inc(s_sp, 1)
                    if i >= 2 and n < 14 and on(sc):
                        exps(sc, 4 * grp + 4 + 2 * (i - 2), par(0))
                        exps(sc, 4 * grp + 5 + 2 * (i - 2), par(0))
                    smalls(amid.get(n, []))
                    if i < 2:
                        gelus(2 * grp + i, 1)
                    if n == 3 and on(o):
                        act.wait_ge(s_fin, 2 * o + 2)
                        act.dma_start(tok(par(-3), it + (r - 3) // 2)(out), na[:, :, 0:D]).then_inc(s_out, 16)
                    smalls(at_end.get(n, []))
                    if n == 8 and on(f):
                        act.wait_ge(s_cv, 9 * f + 8)
                        A(th[:], xc[:], ACT.Tanh).then_inc(s_th, 1)
                    if n == 9 and on(sc):
                        if on(f):
                            act.wait_ge(s_xc, 2 * f + 2)
                        act.wait_ge(s_gv, 2 * sc + 2)
                        A(th[:], sg[:], ACT.Tanh).then_inc(s_gth, 1)
                    if n == 15 and on(f):
                        for nn in range(4):
                            exps(f, nn, par(1))
            run_steps(act, step)
            act.wait_ge(s_out, 16 * NC)

        @block.vector
        def _(v):
            V_ = nc.vector
            v.wait_ge(s_ld_mod, N_LD_MOD)
            v.wait_ge(s_mod_a, 1)
            V_.tensor_scalar(cTs, cT, 0.5, None, ALU.mult).then_inc(s_mod_v, 1)
            v.wait_ge(s_mod_v, 1)
            V_.scalar_tensor_tensor(cTs, cTh, 1.0, cTs, ALU.add, ALU.mult).then_inc(s_mod_v, 1)
            for j in range(MT // ME):
                v.wait_ge(s_hi, j + 1)
                V_.scalar_tensor_tensor(w1l[:, :, j * H:(j + 1) * H], stage[j % 2], WS, w1h[:, :, j * H:(j + 1) * H],
                                        ALU.mult, ALU.subtract).then_inc(s_lo, 1)
            v.wait_ge(s_mod_pe, 3)
            V_.tensor_copy(mrow[:, 0:2, :], ep[0][0:NB, :].rearrange("p (r c) -> p r c", r=2)).then_inc(s_mod_v, 1)
            V_.tensor_copy(mrow[:, 2:4, :], ep[1][0:NB, :].rearrange("p (r c) -> p r c", r=2)).then_inc(s_mod_v, 1)
            v.wait_ge(s_mod_v, 4)
            V_.tensor_scalar(sign, mrow[:, 0:4:3, :], 0.0, 2.0, ALU.is_ge, ALU.mult).then_inc(s_mod_v, 1)
            V_.tensor_scalar(mtmp, mrow[:, 0:4:3, :], -1.0, None, ALU.mult).then_inc(s_mod_v, 1)
            v.wait_ge(s_mod_v, 6)
            V_.tensor_tensor(mtmp, mtmp, mrow[:, 0:4:3, :], ALU.max).then_inc(s_mod_v, 1)
            v.wait_ge(s_mod_v, 7)
            V_.tensor_scalar(mtmp, mtmp, 0.25, None, ALU.max).then_inc(s_mod_v, 1)
            v.wait_ge(s_mod_v, 8)
            V_.scalar_tensor_tensor(mrow[:, 0:4:3, :], sign, -1.0, mtmp, ALU.add, ALU.mult).then_inc(s_mod_v, 1)
            v.wait_ge(s_mod_v, 9)
            V_.tensor_tensor(prow[:, 0:2, :], lnrow, mrow[:, 0:1, :].to_broadcast([NB, 2, D]), ALU.mult)
            V_.tensor_scalar(prow[:, 2, :], mrow[:, 2, :], 1.0, None, ALU.add).then_inc(s_mod_v, 1)
            V_.tensor_copy(prow[:, 3, :], mrow[:, 1, :]).then_inc(s_mod_v, 1)
            V_.tensor_copy(prow2, mrow[:, 3, :]).then_inc(s_mod_v, 1)
            v.wait_ge(s_mod_a, 2)
            V_.tensor_scalar(modT[:, :, 2:4], modT[:, :, 2:4], 1.0, None, ALU.add).then_inc(s_par_v, 1)
            v.wait_ge(s_par_a, 3)
            V_.tensor_scalar(neg_a[:], neg_a[:], -1.0, None, ALU.mult).then_inc(s_par_v, 1)
            V_.tensor_scalar(conv_w[:], conv_w[:], 0.5, None, ALU.mult).then_inc(s_par_v, 1)
            V_.tensor_scalar(conv_b[:], conv_b[:], 0.5, None, ALU.mult).then_inc(s_par_v, 1)
            v.wait_ge(s_ld_ffn, N_LD_FFN)
            for h in range(2):
                if h:
                    v.wait_ge(s_aw, 2)
                V_.tensor_tensor(aw_tmp, w2[:, 4 * h:4 * h + 4, 0:D], g1_bc.unsqueeze(1).to_broadcast([P, 4, D]), ALU.mult)\
                    .then_inc(s_aw, 1)
                v.wait_ge(s_aw, 2 * h + 1)
                V_.tensor_reduce(w2[:, 4 * h:4 * h + 4, D:D1], aw_tmp, AX, ALU.add).then_inc(s_aw, 1)
            v.wait_ge(s_aw, 4)
            V_.tensor_tensor(aw_tmp[:, 0, :], ab2_bc[:, 0:D], g1_bc, ALU.mult).then_inc(s_aw, 1)
            v.wait_ge(s_aw, 5)
            V_.tensor_reduce(ab2_bc[:, D:D1], aw_tmp[:, 0, :], AX, ALU.add).then_inc(s_aw, 1)
            v.wait_ge(s_const, 8)
            V_.memset(xnT[:, 0, :], 0.0).then_inc(s_par_v, 1)
            v.wait_ge(s_par_v, 5)
            for k in range(KD):
                V_.tensor_copy(eye[:, k, k * P:(k + 1) * P], ident[:]).then_inc(s_ex_q, 1)
            v.wait_ge(s_ex_q, 2)
            v.wait_ge(s_ld_gens, 16 * NROT)
            nq, nr = [2], [0]

            def q_all_one(i, g):
                for n, (src, cf) in enumerate(((eye, c_tay[3 * g]), (xm(i, 0), c_tay[3 * g + 1]), (xm(i, 2), c_tay[3 * g + 2]))):
                    if n == 0:
                        V_.tensor_scalar(xm(i, 5), src, cf, None, ALU.mult).then_inc(s_ex_q, 1)
                    else:
                        V_.scalar_tensor_tensor(xm(i, 5), src, cf, xm(i, 5), ALU.mult, ALU.add).then_inc(s_ex_q, 1)
                    nq[0] += 1
                    v.wait_ge(s_ex_q, nq[0])

            def evac_all(dst, how):
                for i in range(NROT):
                    v.wait_ge(s_ex_pe, NROT * nr[0] + i + 1)
                    bank = ex_bank[i][:].rearrange("p (k c) -> p k c", k=KD)
                    if how == "scale":
                        V_.tensor_scalar(xm(i, 0), xm(i, 0), SC, None, ALU.mult)
                        V_.tensor_scalar(xm(i, dst), bank, SC, None, ALU.mult).then_inc(s_ex_v, 1)
                    elif how == "copy":
                        V_.tensor_copy(xm(i, dst), bank).then_inc(s_ex_v, 1)
                    else:
                        V_.scalar_tensor_tensor(xm(i, dst), bank, how, xm(i, 5), ALU.mult, ALU.add).then_inc(s_ex_v, 1)
                nr[0] += 1
            evac_all(1, "scale")
            evac_all(2, "copy")
            v.wait_ge(s_ex_v, NROT * nr[0])
            evac_all(3, "copy")
            for i in range(NROT):
                q_all_one(i, 3)
            evac_all(4, c_tay[12])
            for g in (2, 1, 0):
                v.wait_ge(s_ex_v, NROT * nr[0])
                for i in range(NROT):
                    q_all_one(i, g)
                evac_all(4, 1.0)
            for _ in range(SQUARINGS):
                v.wait_ge(s_ex_v, NROT * nr[0])
                evac_all(5, "copy")
                evac_all(4, "copy")
            evac_all(5, "copy")
            V_.tensor_copy(V[0][:, :, 0:D], eye).then_inc(s_v_ev, 1)
            for j in range(NROT):
                for mt in range(KD):
                    v.wait_ge(s_v_pe, 2 * j + mt + 1)
                    if j >= 1:
                        v.wait_ge(s_v_pe, 2 * j + mt + 1)
                    V_.tensor_copy(V[(j + 1) % 2][:, mt, :], ep[mt][:, 0:D1]).then_inc(s_v_ev, 1)
            v.wait_ge(s_r_pe, 1)
            V_.tensor_copy(eb2r[:], misc[0:NE, 0:D1]).then_inc(s_r_ev, 1)
            for kt in range(MT - MA):
                v.wait_ge(s_r_pe, kt + 2)
                V_.tensor_copy(w2[:, MA + kt, :], hp[kt % 2][:, 0:D1]).then_inc(s_r_ev, 1)

            def stats(src, st, mv, done, base):
                for t in range(NT):
                    V_.bn_stats(st[:, t, :], src[:, t, :]).then_inc(done, 1)
                v.wait_ge(done, base + NT)
                V_.memset(spare[:], 0.0)
                for t in range(NT):
                    V_.bn_aggr(mv[:, t, :], st[:, t, :]).then_inc(done, 1)

            def normalise(dst, src, mv, rs, done):
                for t in range(NT):
                    V_.tensor_scalar(dst[:, t, :], src[:, t, :], mv[:, t, 0:1], rs[:, t:t + 1], ALU.subtract, ALU.mult)\
                        .then_inc(done, 1)

            def step(it, r):
                s = 2 * it + r
                par = lambda d: (r + d) % 2
                f, sc, b, m, o = s + 1, s, s - 1, s - 2, s - 3

                def take(oo):
                    if not on(m):
                        return
                    v.wait_ge(s_eo, NOUT * m + oo + 1)
                    bank = ep[oo % 2][:, 0:D1]
                    if oo < NT:
                        if oo == 0:
                            wait(v, s_mix, 5 * m)
                        V_.tensor_tensor(ab[:, oo, :], bank, ab2_bc[:], ALU.add).then_inc(s_eo_ev, 1)
                    else:
                        e, t = (oo - NT) // NT, (oo - NT) % NT
                        if e == 0:
                            v.wait_ge(s_na, 4 * m + t + 1)
                        else:
                            v.wait_ge(s_eo_ev, NOUT * m + oo - NT + 1)
                        V_.scalar_tensor_tensor(na[:, t, :], bank, wE[:, t, e:e + 1], na[:, t, :], ALU.mult, ALU.add)\
                            .then_inc(s_eo_ev, 1)

                for n in range(NS):
                    grp, i = n // 4, n % 4
                    outs = [] if i < 2 else [None, 2 * (i - 2), None, 2 * (i - 2) + 1] if grp == 0 else \
                        [NT + NT * (2 * grp + i - 4) + t for t in range(NT)]

                    def take_at(pos):
                        if outs and outs[pos] is not None:
                            take(outs[pos])
                    if n == 0 and on(o):
                        v.wait_ge(s_eo_ev, NOUT * o + NOUT)
                        V_.tensor_tensor(zs[:], ab[:, :, D:D1], na[:, :, D:D1], ALU.add).then_inc(s_zs, 1)
                        V_.tensor_tensor(na[:, :, 0:D], na[:, :, 0:D], ab[:, :, 0:D], ALU.subtract).then_inc(s_mix, 1)
                    if on(sc):
                        base = 2 * NS * sc + 2 * n
                        bi, ci = 2 * NS * sc + 2 * n + 1, 2 * NS * sc + 2 * n + 2
                        v.wait_ge(s_bb, bi)
                        if n == 0:
                            v.wait_ge(s_dtx, 2 * sc + 2)
                        wait(v, s_scan, base)
                        for k in range(KD):
                            V_.tensor_tensor(u[:, k, :], dtx[:, par(0), k, :], bcp[(2 * n) % 3][:], ALU.mult)\
                                .then_inc(s_dbx, 1)
                    take_at(0)
                    if on(sc):
                        slot_ = ring[:, PLACE[par(0)][n], :, :]
                        for k in range(KD):
                            v.wait_ge(s_dA, base + k + 1)
                            v.wait_ge(s_dbx, base + k + 1)
                            V_.tensor_tensor_scan(slot_[:, k, :], slot_[:, k, :], u[:, k, :],
                                                  0.0 if par(0) == 0 else state[:, n, k:k + 1], ALU.mult, ALU.add)\
                                .then_inc(s_scan, 1)
                            take_at(1 + k)
                        if par(0) == 0:
                            v.wait_ge(s_scan, base + 2)
                            V_.tensor_copy(state[:, n, :], slot_[:, :, CH - 1]).then_inc(s_tail, 1)
                        v.wait_ge(s_bb, ci)
                        if par(0) == 0:
                            v.wait_ge(s_tail, NS // 2 * sc + n + 1)
                        for k in range(KD):
                            v.wait_ge(s_scan, base + k + 1)
                            V_.tensor_tensor(slot_[:, k, :], slot_[:, k, :], bcp[(2 * n + 1) % 3][:], ALU.mult)\
                                .then_inc(s_hc, 1)
                    else:
                        take_at(1)
                        take_at(2)
                    take_at(3)

                    if n == 0:
                        if on(f):
                            v.wait_ge(s_x_in, 16 * (f + 1))
                            stats(xin, st_f, mv_f, s_f_stat, 8 * f)
                        if on(m):
                            v.wait_ge(s_lg_pe, m + 1)
                            V_.tensor_tensor(lg[:], misc[:, 0:8 * NT].rearrange("p (t e) -> p t e", t=NT)[:, :, 0:NE],
                                             gate_b_bc[:].unsqueeze(1).to_broadcast([P, NT, NE]), ALU.add)\
                                .then_inc(s_rt, 1)
                            v.wait_ge(s_rt, 5 * m + 1)
                            other = lg[:].unsqueeze(2).to_broadcast([P, NT, NE, NE])
                            mine = lg[:].unsqueeze(3).to_broadcast([P, NT, NE, NE])
                            V_.tensor_tensor(rk[:], other, mine, ALU.is_ge)
                            V_.tensor_tensor(rk2[:], other, mine, ALU.is_gt)
                            V_.tensor_reduce(lgm[:], lg[:], AX, ALU.max).then_inc(s_rt, 1)
                            v.wait_ge(s_rt, 5 * m + 2)
                            V_.tensor_tensor(lg[:], lg[:], lgm[:].to_broadcast([P, NT, NE]), ALU.subtract)
                            V_.tensor_tensor(rk[:], rk[:], before[:].unsqueeze(1).to_broadcast([P, NT, NE, NE]), ALU.mult)
                            V_.tensor_tensor(rk2[:], rk2[:], after[:].unsqueeze(1).to_broadcast([P, NT, NE, NE]), ALU.mult)\
                                .then_inc(s_rt, 1)
                            v.wait_ge(s_rt, 5 * m + 3)
                            V_.tensor_tensor(rk[:], rk[:], rk2[:], ALU.add).then_inc(s_rt, 1)
                            v.wait_ge(s_rt, 5 * m + 4)
                            V_.tensor_reduce(rsum[:], rk[:], AX, ALU.add).then_inc(s_rt, 1)
                    if n == 1:
                        if on(b):
                            v.wait_ge(s_o_pe, 2 * b + 1)
                            V_.tensor_tensor(res[:, 0:2, :], misc[:].rearrange("p (t c) -> p t c", t=2),
                                             b_out_bc[:].unsqueeze(1).to_broadcast([P, 2, D]), ALU.add).then_inc(s_res, 1)
                        if on(f):
                            v.wait_ge(s_f_rstd, 2 * f + 2)
                            normalise(xin, xin, mv_f, rs_f, s_f_hat)
                        if on(o):
                            v.wait_ge(s_gth4, o + 1)
                            v.wait_ge(s_mix, 5 * o + 1)
                            V_.tensor_scalar(gt[:], gt[:], 0.5, 0.5, ALU.mult, ALU.add).then_inc(s_gate, 1)
                            v.wait_ge(s_gate, o + 1)
                            for t in range(NT):
                                V_.scalar_tensor_tensor(na[:, t, 0:D], na[:, t, 0:D], gt[:, t, :], ab[:, t, 0:D],
                                                        ALU.mult, ALU.add).then_inc(s_mix, 1)
                    if n == 2 and on(b):
                        v.wait_ge(s_o_pe, 2 * b + 2)
                        V_.tensor_tensor(res[:, 2:4, :], misc[:].rearrange("p (t c) -> p t c", t=2),
                                         b_out_bc[:].unsqueeze(1).to_broadcast([P, 2, D]), ALU.add).then_inc(s_res, 1)
                        v.wait_ge(s_res, 2 * b + 2)
                        stats(res, st_b, mv_b, s_b_stat, 24 * b)
                    if n == 3 and on(m):
                        v.wait_ge(s_rexp, m + 1)
                        v.wait_ge(s_rt, 5 * m + 5)
                        V_.scalar_tensor_tensor(wE[:], rsum[:], 1.5, wE[:], ALU.is_lt, ALU.mult).then_inc(s_w, 1)
                        v.wait_ge(s_w, 3 * m + 1)
                        V_.tensor_reduce(lgs[:], wE[:], AX, ALU.add).then_inc(s_wsum, 1)
                        v.wait_ge(s_wsum, m + 1)
                        V_.reciprocal(lgs[:], lgs[:]).then_inc(s_w, 1)
                        v.wait_ge(s_w, 3 * m + 2)
                        V_.tensor_tensor(wE[:], wE[:], lgs[:].to_broadcast([P, NT, NE]), ALU.mult).then_inc(s_w, 1)
                    if n == 4 and on(b):
                        v.wait_ge(s_b_rstd, 6 * b + 2)
                        normalise(res, res, mv_b, rs_b, s_b_hat)
                    if n in (5, 7) and on(f):
                        k = (n - 5) // 2
                        v.wait_ge(s_xs, 2 * f + k + 1)
                        if k == 0:
                            wait(v, s_yinit, 2 * f)
                            wait(v, s_dtx, 2 * f)
                        for j in range(TAPS):
                            src = xs[:, k, j:j + CH]
                            if j == 0:
                                if k == 0 and isinstance(f, int) and f == 0:
                                    v.wait_ge(s_par_v, 4)
                                V_.tensor_scalar(xc[:, k, :], src, conv_w[:, k, 0:1], conv_b[:, k:k + 1], ALU.mult, ALU.add)\
                                    .then_inc(s_cv, 1)
                            else:
                                v.wait_ge(s_cv, 9 * f + 4 * k + j)
                                V_.scalar_tensor_tensor(xc[:, k, :], src, conv_w[:, k, j:j + 1], xc[:, k, :],
                                                        ALU.mult, ALU.add).then_inc(s_cv, 1)
                        if k == 1:
                            v.wait_ge(s_cv, 9 * f + 8)
                            if par(1) == 0:
                                V_.tensor_copy(xs[:, :, 0:TAPS - 1], xs[:, :, CH:CH + TAPS - 1]).then_inc(s_cv, 1)
                            else:
                                V_.memset(xs[:, :, 0:TAPS - 1], 0.0).then_inc(s_cv, 1)
                    if n == 7 and on(b):
                        v.wait_ge(s_x1, 3 * b + 3)
                        stats(xr[:, par(-1)], st_b, mv_b, s_b_stat, 24 * b + 8)
                    if n == 9:
                        if on(f):
                            v.wait_ge(s_th, f + 1)
                            for k in range(KD):
                                V_.scalar_tensor_tensor(xc[:, k, :], th[:, k, :], 1.0, xc[:, k, :], ALU.add, ALU.mult)\
                                    .then_inc(s_xc, 1)
                        if on(b):
                            v.wait_ge(s_b_rstd, 6 * b + 4)
                            normalise(res, xr[:, par(-1)], mv_b, rs_b, s_b_hat)
                    if n == 10 and on(sc):
                        v.wait_ge(s_gth, sc + 1)
                        for k in range(KD):
                            V_.scalar_tensor_tensor(sg[:, k, :], th[:, k, :], 1.0, sg[:, k, :], ALU.add, ALU.mult)\
                                .then_inc(s_sg, 1)
                    if n == 11:
                        if on(b):
                            v.wait_ge(s_h2, 2 * b + 2)
                            stats(res, st_b, mv_b, s_b_stat, 24 * b + 16)
                        if on(f):
                            v.wait_ge(s_bcf, f + 1)
                            q = par(1)
                            V_.tensor_copy(bcs[:, q, :], bcf[:]).then_inc(s_bcs, 1)
                            v.wait_ge(s_bcs, 4 * f + 1)
                            V_.tensor_tensor(bcf[P // 2:P, :], bcf[P // 2:P, :], bcs[P // 2:P, q, :], ALU.subtract)\
                                .then_inc(s_bcs, 1)
                            v.wait_ge(s_bcs, 4 * f + 2)
                            V_.tensor_copy(bcs[P // 2:P, q, :], bcf[P // 2:P, :]).then_inc(s_bcs, 1)
                            v.wait_ge(s_bcs, 4 * f + 3)
                            V_.tensor_tensor(bcs[3 * P // 4:P, q, :], bcf[3 * P // 4:P, :], bcs[3 * P // 4:P, q, :],
                                             ALU.subtract).then_inc(s_bcs, 1)
                    if n == 12 and on(b):
                        v.wait_ge(s_b_rstd, 6 * b + 6)
                        v.wait_ge(s_base, 2 * b + 1)
                        normalise(res, res, mv_b, rs_b, s_b_hat)
                    if n == 15 and on(b):
                        v.wait_ge(s_xn, 4 * b + 4)
                        wait(v, s_hid, MT * b)
                        for k in range(KD):
                            V_.tensor_tensor(xnl[:, k, :], xnT[:, k, :], xnh[:, k, :], ALU.subtract).then_inc(s_xnl, 1)
            run_steps(v, step)


def kernel(**inputs):
    import numpy as _np
    import concourse.bacc as _bacc
    from concourse import mybir as _mybir
    from concourse.bass_utils import run_bass_kernel_spmd as _run

    nc = _bacc.Bacc("TRN2", target_bir_lowering=False, num_devices=1)
    arrays, args = {}, {}
    for name, value in inputs.items():
        arr = _np.ascontiguousarray(value)
        arrays[f"in_{name}_dram"] = arr
        args[name] = nc.dram_tensor(f"in_{name}_dram", arr.shape, _mybir.dt.from_np(arr.dtype), kind="ExternalInput").ap()
    shape = inputs["L0_attn_x"].shape
    out = nc.dram_tensor("out_0_dram", shape, _mybir.dt.float32, kind="ExternalOutput").ap()
    build_adaln_mamba_moe(nc, args, out)
    r = _run(nc, [arrays], core_ids=[0])
    return r.results[0]["out_0_dram"]
```

```python
import concourse.bass as bass
from concourse import mybir
from contextlib import ExitStack
from math import factorial

f32 = mybir.dt.float32
f16 = mybir.dt.float16
bf16 = mybir.dt.bfloat16
ALU = mybir.AluOpType
ACT = mybir.ActivationFunctionType
AX = mybir.AxisListType.X


def build_adaln_mamba_moe(nc, a, out):
    NB, T, D = a["L0_attn_x"].shape
    NS = a["L0_attn_A_log"].shape[1]
    NE, _, H = a["L0_ffn_ew1"].shape
    HA = a["L0_ffn_aw1"].shape[1]
    P = 128
    KD = D // P
    CH = 512
    NT = CH // P
    CPB = T // CH
    NC = NB * CPB
    TAPS = a["L0_attn_conv_w"].shape[2]
    MA = HA // P
    ME = H // P
    MT = MA + NE * ME
    NOUT = NT + NE * NT
    D1 = D + 1
    RING = 6
    WS = 64.0
    EPS = 1e-5
    SQUARINGS = 4
    TAYLOR = 12
    NROT = a["L0_ffn_gens"].shape[0]
    assert CPB == 2 and KD == 2 and NT == 4 and NS == 16 and ME == 4 and MA == 8

    ctx = ExitStack()
    with ctx:
        def sb(name, shape, dt=f32):
            return ctx.enter_context(nc.sbuf_tensor(name, shape, dt))

        def pb(name, shape=(P, 512), dt=f32):
            return ctx.enter_context(nc.psum_tensor(name, list(shape), dt))

        def sem(name):
            return ctx.enter_context(nc.semaphore(name))

        w_in = sb("w_in", [P, KD, 2 * D])
        w_dt = sb("w_dt", [P, KD, D])
        w_bc = sb("w_bc", [P, KD, P])
        w_out = sb("w_out", [P, KD, D])
        w1h = sb("w1h", [P, KD, MT * P], f16)
        w1l = sb("w1l", [P, KD, MT * P], f16)
        w2 = sb("w2", [P, MT, D1])
        gate_w = sb("gate_w", [P, KD, NE])
        b1 = sb("b1", [P, MT])
        b_in = sb("b_in", [P, 4])
        b_gh = sb("b_gh", [P, KD])
        conv_w = sb("conv_w", [P, KD, TAPS])
        conv_b = sb("conv_b", [P, KD])
        b_dt = sb("b_dt", [P, KD])
        b_bc = sb("b_bc", [P, 1])
        neg_a = sb("neg_a", [P, KD, NS])
        d_skip = sb("d_skip", [P, KD])
        ln_g = sb("ln_g", [P, KD])
        ln_b = sb("ln_b", [P, KD])
        modT = sb("modT", [P, NB, 4])
        cur_mod = sb("cur_mod", [P, 4])
        b_out_bc = sb("b_out_bc", [P, D])
        ab2_bc = sb("ab2_bc", [P, D1])
        gate_b_bc = sb("gate_b_bc", [P, NE])
        gcb_half = sb("gcb_half", [P, 1])
        eb2r = sb("eb2r", [NE, D1])
        ident = sb("ident", [P, P])
        sel = sb("sel", [P, 2 * NS], bf16)
        before = sb("before", [P, NE, NE])
        after = sb("after", [P, NE, NE])
        neg_half = sb("neg_half", [P, NT])
        eps = sb("eps", [P, NT])
        spare = sb("spare", [P, 1])

        ring = sb("ring", [P, RING, KD, CH])
        u = sb("u", [P, KD, CH])
        xin = sb("xin", [P, NT, D])
        xr = sb("xr", [P, 2, NT, D])
        res = sb("res", [P, NT, D])
        h1T = sb("h1T", [P, 2, KD, CH])
        xs = sb("xs", [P, KD, TAPS - 1 + CH])
        xc = sb("xc", [P, KD, CH])
        th = sb("th", [P, KD, CH])
        sg = sb("sg", [P, KD, CH])
        bcs = sb("bcs", [P, 2, CH], bf16)
        bcf = sb("bcf", [P, CH])
        dt = sb("dt", [P, KD, CH])
        dtx = sb("dtx", [P, 2, KD, CH])
        xnT = sb("xnT", [P, KD, CH])
        xnh = sb("xnh", [P, KD, CH], f16)
        xnl = sb("xnl", [P, KD, CH], f16)
        rows = sb("rows", [P, 5, D])
        gb_fin = sb("gb_fin", [P, D])
        hid = sb("hid", [P, 2, ME, CH])
        ab = sb("ab", [P, NT, D1])
        na = sb("na", [P, NT, D1])
        y = sb("y", [P, KD, CH])
        state = sb("state", [P, NS, KD])
        st_f = sb("st_f", [P, NT, 6]); mv_f = sb("mv_f", [P, NT, 2]); rs_f = sb("rs_f", [P, NT])
        st_b = sb("st_b", [P, NT, 6]); mv_b = sb("mv_b", [P, NT, 2]); rs_b = sb("rs_b", [P, NT])
        lg = sb("lg", [P, NT, NE]); lgm = sb("lgm", [P, NT, 1]); lgs = sb("lgs", [P, NT, 1])
        rk = sb("rk", [P, NT, NE, NE]); rk2 = sb("rk2", [P, NT, NE, NE]); rsum = sb("rsum", [P, NT, NE])
        wE = sb("wE", [P, NT, NE])
        wT = bcf[0:NE, :]
        zs = sb("zs", [P, NT, 1])
        gt = sb("gt", [P, NT, 1])

        bcp = [pb(f"bcp{i}") for i in range(3)]
        hp = [pb(f"hp{i}") for i in range(2)]
        ep = [pb(f"ep{i}") for i in range(2)]
        misc = pb("misc")

        s_ld_mod = sem("s_ld_mod"); s_ld_attn = sem("s_ld_attn"); s_ld_ffn = sem("s_ld_ffn")
        s_ld_stage = [sem(f"s_ld_stage{i}") for i in range(2)]
        s_ld_gens = sem("s_ld_gens"); s_const = sem("s_const")
        s_mod_v = sem("s_mod_v"); s_mod_a = sem("s_mod_a"); s_mod_pe = sem("s_mod_pe")
        s_rows_out = sem("s_rows_out"); s_par_v = sem("s_par_v"); s_par_a = sem("s_par_a")
        s_hi = sem("s_hi"); s_lo = sem("s_lo")
        s_ex_pe = sem("s_ex_pe"); s_ex_v = sem("s_ex_v"); s_ex_a = sem("s_ex_a"); s_v0 = sem("s_v0"); s_ex_q = sem("s_ex_q")
        s_v_pe = sem("s_v_pe"); s_v_ev = sem("s_v_ev")
        s_rt_pe = sem("s_rt_pe"); s_rt_ev = sem("s_rt_ev"); s_r_pe = sem("s_r_pe"); s_r_ev = sem("s_r_ev")
        s_aw = sem("s_aw")

        s_x_in = sem("s_x_in"); s_xr_in = [sem(f"s_xr_in{q}") for q in range(2)]; s_rows_in = sem("s_rows_in"); s_gbf_in = sem("s_gbf_in")
        s_out = sem("s_out")
        s_f_stat = sem("s_f_stat"); s_f_rstd = sem("s_f_rstd"); s_f_hat = sem("s_f_hat"); s_f_t = sem("s_f_t")
        s_curmod = sem("s_curmod"); s_h1 = sem("s_h1"); s_j = sem("s_j"); s_xs = sem("s_xs"); s_cv = sem("s_cv")
        s_th = sem("s_th"); s_xc = sem("s_xc"); s_bc_pe = sem("s_bc_pe"); s_bcf = sem("s_bcf"); s_bcs = sem("s_bcs")
        s_d_pe = sem("s_d_pe"); s_d_raw = sem("s_d_raw"); s_sp = sem("s_sp"); s_dt = sem("s_dt"); s_dtx = sem("s_dtx")
        s_g_pe = sem("s_g_pe"); s_gv = sem("s_gv"); s_gth = sem("s_gth"); s_sg = sem("s_sg")
        s_bb = sem("s_bb"); s_dA = sem("s_dA"); s_dbx = sem("s_dbx"); s_scan = sem("s_scan"); s_tail = sem("s_tail")
        s_hc = sem("s_hc"); s_y = sem("s_y"); s_yinit = sem("s_yinit"); s_y2 = sem("s_y2")
        s_o_pe = sem("s_o_pe"); s_res = sem("s_res"); s_b_stat = sem("s_b_stat"); s_b_rstd = sem("s_b_rstd")
        s_b_hat = sem("s_b_hat"); s_x1 = sem("s_x1"); s_h2 = sem("s_h2"); s_base = sem("s_base")
        s_x_t = sem("s_x_t"); s_xn = sem("s_xn"); s_xnl = sem("s_xnl")
        s_lg_pe = sem("s_lg_pe"); s_rt = sem("s_rt"); s_rexp = sem("s_rexp"); s_w = sem("s_w")
        s_wt_pe = sem("s_wt_pe"); s_wt = sem("s_wt"); s_n_pe = sem("s_n_pe"); s_na = sem("s_na")
        s_hid = sem("s_hid"); s_gelu = sem("s_gelu"); s_eo = sem("s_eo"); s_eo_ev = sem("s_eo_ev")
        s_zs = sem("s_zs"); s_gate = sem("s_gate"); s_wsum = sem("s_wsum"); s_gth4 = sem("s_gth4"); s_mix = sem("s_mix"); s_fin = sem("s_fin")

        rows_dram = nc.dram_tensor("mod_rows", (NB, 5 * D), f32, kind="Internal").ap()

        PLACE = [[n % RING for n in range(NS)], [4, 5, 0, 1, 2, 3, 4, 5, 0, 1, 4, 5, 2, 3, 4, 5]]

        def place_before(q, n):
            return next(m for m in range(n - 1, -NS - 1, -1) if PLACE[q if m >= 0 else 1 - q][m % NS] == PLACE[q][n])

        def on(c):
            return not isinstance(c, int) or 0 <= c < NC

        def wait(eng, s, value):
            if not isinstance(value, int) or value > 0:
                eng.wait_ge(s, value)

        def run_steps(eng, step):
            step(-1, 1)
            for it in range(0, LOOP0):
                step(it, 0)
                step(it, 1)
            if LOOP:
                with eng.Fori(LOOP0, LOOP1) as it:
                    step(it, 0)
                    step(it, 1)
            else:
                for it in range(LOOP0, LOOP1):
                    step(it, 0)
                    step(it, 1)
            for it in range(LOOP1, (NC + 4) // 2):
                step(it, 0)
                step(it, 1)
        LOOP = True
        LOOP0, LOOP1 = 2, (NC - 2) // 2

        MISC = [("logits", -2, s_rt, 5, 1), ("o0", -1, s_res, 2, 1), ("o1", -1, s_res, 2, 2),
                ("t0", 1, s_h1, 2, 1), ("t1", 1, s_h1, 2, 2), ("wt", -2, s_wt, 1, 1), ("j0", 1, s_xs, 2, 1),
                ("n0", -2, s_na, 4, 1), ("n1", -2, s_na, 4, 2), ("n2", -2, s_na, 4, 3), ("n3", -2, s_na, 4, 4),
                ("j1", 1, s_xs, 2, 2), ("g0", 0, s_gv, 2, 1), ("g1", 0, s_gv, 2, 2), ("bc", 1, s_bcf, 1, 1),
                ("d0", 1, s_d_raw, 4, 2), ("d1", 1, s_d_raw, 4, 4), ("x0", -1, s_xn, 4, 2), ("x1", -1, s_xn, 4, 4)]
        MISC_AT = {m[0]: i for i, m in enumerate(MISC)}

        def misc_free(eng, use, s):
            for back in range(1, 3 * len(MISC)):
                i = MISC_AT[use] - back
                steps_ago = -(i // len(MISC))
                _, delta, done, per, idx = MISC[i % len(MISC)]
                c = s - steps_ago + delta
                if on(c):
                    eng.wait_ge(done, per * c + idx)
                    return

        w1f = [w[:, :, :].rearrange("p k n -> p (k n)").bitcast(f32).rearrange("p (s c) -> p s c", c=512)
               for w in (w1h, w1l)]
        hidf = hid[:, :, :, :].rearrange("p a m c -> p (a m) c")

        def xm(i, slot):
            n = i * 6 + slot
            return (w1f + [hidf])[n // 8][:, n % 8, :].rearrange("p (k c) -> p k c", k=KD)
        eye = xnT[:, 0, :].rearrange("p (k c) -> p k c", k=KD)
        ex_bank = [hp[0], hp[1], ep[0], ep[1]]
        ROUNDS = [("T", 0, 0, 1), ("P", 1, 0, 2), ("P", 2, 1, 3), ("P", 1, 2, 4), ("P", 3, 4, 4), ("P", 3, 4, 4),
                  ("P", 3, 4, 4)]
        V_ROUNDS = (3, 4, 5, 6)
        for _ in range(SQUARINGS):
            ROUNDS += [("T", 4, 4, 5), ("P", 5, 4, 4)]
        ROUNDS += [("T", 4, 4, 5)]

        def round_taken(rd, i):
            by_v = rd in V_ROUNDS
            return (s_ex_v if by_v else s_ex_a), NROT * sum((q in V_ROUNDS) == by_v for q in range(rd)) + i + 1

        def setup_round(s, n):
            if s == -1 and n % 2 == 0:
                return n // 2
            if s == 0 and n % 2 == 0 and 8 + n // 2 < len(ROUNDS):
                return 8 + n // 2
            return None
        assert len(ROUNDS) == 16
        PAIRS = (MT - MA) // 2
        stage = [hid[:, 0, 2 * i:2 * i + 2, :].rearrange("p a c -> p (a c)").rearrange("p (k c) -> p k c", k=KD) for i in range(2)]
        wmod_sb = ring[:, 0:3, :, :].rearrange("p a b c -> p (a b c)").rearrange("p (k c) -> p k c", k=KD)
        cT = ring[:, 3, 0, 0:KD * NB].rearrange("p (k b) -> p k b", k=KD)
        cTh = ring[:, 3, 0, 64:64 + KD * NB].rearrange("p (k b) -> p k b", k=KD)
        cTs = ring[:, 3, 0, 128:128 + KD * NB].rearrange("p (k b) -> p k b", k=KD)
        mrow = ring[0:NB, 4, :, :].rearrange("p a c -> p (a c)").rearrange("p (r c) -> p r c", r=4)
        lnrow = ring[0:NB, 5, 0, :].rearrange("p (r c) -> p r c", r=2)
        mtmp = ring[0:NB, 5, 1, :].rearrange("p (r c) -> p r c", r=2)
        prow = y[0:NB, :, :].rearrange("p k c -> p (k c)")[:, 0:4 * D].rearrange("p (r c) -> p r c", r=4)
        prow2 = sg[0:NB, 0, 0:D]
        sign = sg[0:NB, 1, 0:2 * D].rearrange("p (r c) -> p r c", r=2)
        aw_tmp = res
        g1_bc = na[:, 2, 0:D]
        eb2T = na[:, 3, 0:KD * NE].rearrange("p (k e) -> p k e", k=KD)
        V = [ab[:, 0:KD, :], na[:, 0:KD, :]]
        rT = [hid[:, 1, i, :].rearrange("p (t k c) -> p t k c", t=2, k=KD) for i in range(2)]
        c_tay = [1.0 / factorial(j) for j in range(TAYLOR + 1)]
        SC = 2.0 ** -SQUARINGS
        W1_SLOT0 = 5

        def tok(c_half, b):
            return lambda t: t[b, c_half * CH:(c_half + 1) * CH, :].rearrange("(t p) d -> p t d", p=P)

        block = ctx.enter_context(nc.Block())

        @block.sync
        def _(sp):
            X = a["L0_attn_x"]
            n_mod = [0]

            def ld(s, dst, src):
                sp.dma_start(dst, src).then_inc(s, 16)

            colk = lambda v: v.rearrange("(k p) -> p k", p=P)
            with nc.allow_non_contiguous_dma(reason="small parameters, once"):
                sp.dma_start(xin[:], tok(0, 0)(X)).then_inc(s_x_in, 16)
                ld(s_ld_mod, wmod_sb, a["L0_wmod"].rearrange("(k p) n -> p k n", p=P))
                for k in range(KD):
                    ld(s_ld_mod, cT[:, k, :], a["L0_c"][:, k * P:(k + 1) * P].rearrange("b p -> p b"))
                ld(s_ld_mod, lnrow[:, 0, :], a["L0_attn_ln_g"].partition_broadcast(NB))
                ld(s_ld_mod, lnrow[:, 1, :], a["L0_attn_ln_b"].partition_broadcast(NB))
                ld(s_ld_attn, w_in[:], a["L0_attn_W_in"].rearrange("(k p) n -> p k n", p=P))
                ld(s_ld_attn, w_dt[:], a["L0_attn_W_dt"].rearrange("(k p) n -> p k n", p=P))
                for r in range(4):
                    ld(s_ld_attn, w_bc[:, :, r * 2 * NS:(r + 1) * 2 * NS],
                       a["L0_attn_W_bc"].rearrange("(k p) n -> p k n", p=P))
                    ld(s_ld_attn, b_bc[r * 2 * NS:(r + 1) * 2 * NS, :],
                       a["L0_attn_b_bc"].rearrange("(n o) -> n o", o=1))
                ld(s_ld_attn, w_out[:], a["L0_attn_W_out"].rearrange("(k p) n -> p k n", p=P))
                ld(s_ld_attn, b_in[:], colk(a["L0_attn_b_in"]))
                ld(s_ld_attn, conv_w[:], a["L0_attn_conv_w"].rearrange("(k p) o t -> p k (o t)", p=P))
                ld(s_ld_attn, conv_b[:], colk(a["L0_attn_conv_b"]))
                ld(s_ld_attn, b_dt[:], colk(a["L0_attn_b_dt"]))
                ld(s_ld_attn, neg_a[:], a["L0_attn_A_log"].rearrange("(k p) n -> p k n", p=P))
                ld(s_ld_attn, d_skip[:], colk(a["L0_attn_D"]))
                ld(s_ld_attn, b_out_bc[:], a["L0_attn_b_out"].partition_broadcast(P))
                for i in range(NROT):
                    ld(s_ld_gens, xm(i, 0), a["L0_ffn_gens"][i].rearrange("(k p) n -> p k n", p=P))
                ld(s_ld_ffn, ln_g[:], colk(a["L0_ffn_ln_g"]))
                ld(s_ld_ffn, ln_b[:], colk(a["L0_ffn_ln_b"]))
                ld(s_ld_ffn, gate_w[:], a["L0_ffn_gate_w"].rearrange("(k p) e -> p k e", p=P))
                ld(s_ld_ffn, gate_b_bc[:], a["L0_ffn_gate_b"].partition_broadcast(P))
                ld(s_ld_ffn, gcb_half[:], a["L0_ffn_gc_b"].partition_broadcast(P))
                ld(s_ld_ffn, ab2_bc[:, 0:D], a["L0_ffn_ab2"].partition_broadcast(P))
                ld(s_ld_ffn, b1[:, 0:MA], a["L0_ffn_ab1"].rearrange("(m p) -> p m", p=P))
                ld(s_ld_ffn, b1[:, MA:MT], a["L0_ffn_eb1"].rearrange("e (m p) -> p (e m)", p=P))
                ld(s_ld_ffn, g1_bc, a["L0_ffn_gc_w"][0:D, :].rearrange("d o -> (d o)").partition_broadcast(P))
                ld(s_ld_ffn, V[0][:, :, D:D1], a["L0_ffn_gc_w"][D:2 * D, :].rearrange("(k p) o -> p k o", p=P))
                for k in range(KD):
                    ld(s_ld_ffn, eb2T[:, k, :], a["L0_ffn_eb2"][:, k * P:(k + 1) * P].rearrange("e p -> p e"))
                ld(s_ld_ffn, w2[:, 0:MA, 0:D], a["L0_ffn_aw2"].rearrange("(m p) d -> p m d", p=P))
                for e in range(NE):
                    ld(s_ld_ffn, w2[:, MA + e * ME:MA + (e + 1) * ME, 0:D],
                       a["L0_ffn_ew2"][e].rearrange("(m p) d -> p m d", p=P))
                sp.wait_ge(s_mod_v, 12)
                sp.dma_start(rows_dram[:, 0:4 * D].rearrange("b (r c) -> b r c", r=4), prow).then_inc(s_rows_out, 16)
                sp.dma_start(rows_dram[:, 4 * D:5 * D], prow2).then_inc(s_rows_out, 16)
                sp.wait_ge(s_rows_out, 32)
                sp.dma_start(rows[:], rows_dram[0, :].partition_broadcast(P).rearrange("p (r c) -> p r c", r=5))\
                    .then_inc(s_rows_in, 16)
                sp.dma_start(gb_fin[:], rows_dram[0, 4 * D:5 * D].partition_broadcast(P)).then_inc(s_gbf_in, 16)

            def load_piece(j):
                src = a["L0_ffn_aw1"][:, j * H:(j + 1) * H] if j < 2 else a["L0_ffn_ew1"][j - 2]
                sp.dma_start(stage[j % 2], src.rearrange("(k p) n -> p k n", p=P)).then_inc(s_ld_stage[j % 2], 16)

            def step(it, r):
                s = 2 * it + r
                batch = lambda d: it + (r + d) // 2
                par = lambda d: (r + d) % 2
                if on(s - 1):
                    wait(sp, s_fin, 2 * (s - 2))
                    sp.dma_start(xr[:, par(-1), :, :], tok(par(-1), batch(-1))(X)).then_inc(s_xr_in[par(-1)], 16)
                if isinstance(s, int) and s == 1:
                    sp.wait_ge(s_v_ev, 2 * NROT)
                    load_piece(0)
                    load_piece(1)
                if on(s - 3) and r == 0 and on(s - 2):
                    wait(sp, s_fin, 2 * (s - 2))
                    sp.dma_start(gb_fin[:], rows_dram[batch(-2), 4 * D:5 * D].partition_broadcast(P))\
                        .then_inc(s_gbf_in, 16)
                if on(s + 2):
                    wait(sp, s_f_t, 2 * (s + 2))
                    sp.dma_start(xin[:], tok(par(2), batch(2))(X)).then_inc(s_x_in, 16)
                if isinstance(s, int) and s == 1:
                    for j in range(2, MT // ME):
                        sp.wait_ge(s_hi, j - 1)
                        sp.wait_ge(s_lo, j - 1)
                        load_piece(j)
                if r == 0 and on(s - 1) and on(s):
                    wait(sp, s_base, 2 * (s - 1) + 2)
                    sp.dma_start(rows[:], rows_dram[batch(0), :].partition_broadcast(P)
                                 .rearrange("p (r c) -> p r c", r=5)).then_inc(s_rows_in, 16)
            run_steps(sp, step)

        N_LD_MOD = 16 * (1 + KD + 2)
        N_LD_ATTN = 16 * (2 + 8 + 8)
        N_LD_FFN = 16 * (10 + KD + 1 + NE)

        @block.gpsimd
        def _(g):
            G = nc.gpsimd
            G.memset(ident[:], 0.0).then_inc(s_const, 1)
            G.memset(sel[:], 0.0).then_inc(s_const, 1)
            G.memset(before[:], 0.0).then_inc(s_const, 1)
            G.memset(after[:], 0.0).then_inc(s_const, 1)
            G.memset(neg_half[:], -0.5).then_inc(s_const, 1)
            G.memset(eps[:], EPS).then_inc(s_const, 1)
            G.memset(xs[:, :, 0:TAPS - 1], 0.0).then_inc(s_const, 1)
            g.wait_ge(s_const, 7)
            G.affine_select(out=ident[:], in_=ident[:], compare_op=ALU.not_equal, fill=1.0, base=0,
                            pattern=[[-1, P]], channel_multiplier=1).then_inc(s_const, 1)
            for e in range(1, NE):
                G.memset(before[:, e, 0:e], 1.0).then_inc(s_const, 1)
                G.memset(after[:, e - 1, e:NE], 1.0).then_inc(s_const, 1)
            n0 = 8 + 2 * (NE - 1)
            for n, r in enumerate((0, 2, 3)):
                g.wait_ge(s_const, n0 + n)
                G.affine_select(out=sel[:], in_=sel[:], compare_op=ALU.not_equal, fill=1.0, base=-r * 2 * NS,
                                pattern=[[-1, 2 * NS]], channel_multiplier=1).then_inc(s_const, 1)

            def rstd(mv, rs, ready, value, done, per_c):
                g.wait_ge(ready, value)
                G.tensor_tensor(rs[:], mv[:, :, 1], eps[:], ALU.add).then_inc(done, 1)
                g.wait_ge(done, per_c + 1)
                G.tensor_tensor(rs[:], rs[:], neg_half[:], ALU.pow).then_inc(done, 1)

            tmp_rows = xnT[:, :, :].rearrange("p k c -> p (k c)").rearrange("p (t d) -> p t d", t=NT)

            def row(r):
                return rows[:, r:r + 1, :].to_broadcast([P, NT, D])

            g.wait_ge(s_ld_attn, N_LD_ATTN)
            g.wait_ge(s_rows_out, 32)

            def step(it, r):
                s = 2 * it + r
                par = lambda d: (r + d) % 2
                for n in range(NS):
                    if n == 0:
                        if on(s - 1):
                            g.wait_ge(s_sg, 2 * (s - 1) + 2)
                            g.wait_ge(s_y, NS * s)
                            for k in range(KD):
                                G.tensor_tensor(sg[:, k, :], sg[:, k, :], y[:, k, :], ALU.mult).then_inc(s_y2, 1)
                        if on(s):
                            g.wait_ge(s_xc, 2 * s + 2)
                            wait(g, s_y2, 2 * s)
                            for k in range(KD):
                                G.tensor_tensor(y[:, k, :], xc[:, k, :], d_skip[:, k:k + 1].to_broadcast([P, CH]), ALU.mult)\
                                    .then_inc(s_yinit, 1)
                    if on(s):
                        i = NS * s + n
                        g.wait_ge(s_hc, i + 1)
                        if n == 0:
                            g.wait_ge(s_yinit, 2 * s + 2)
                        else:
                            g.wait_ge(s_y, i)
                        G.tensor_tensor(y[:], y[:], ring[:, PLACE[par(0)][n], :, :], ALU.add).then_inc(s_y, 1)
                    if n == 0 and on(s + 1):
                        rstd(mv_f, rs_f, s_f_stat, 8 * (s + 1) + 8, s_f_rstd, 2 * (s + 1))
                    if n == 2 and on(s - 3):
                        c = s - 3
                        g.wait_ge(s_mix, 5 * c + 5)
                        g.wait_ge(s_gbf_in, 16 * (it + (r - 3) // 2) + 16)
                        G.tensor_tensor(na[:, :, 0:D], na[:, :, 0:D], gb_fin[:, :].unsqueeze(1).to_broadcast([P, NT, D]),
                                        ALU.mult).then_inc(s_fin, 1)
                        g.wait_ge(s_fin, 2 * c + 1)
                        G.tensor_tensor(na[:, :, 0:D], xr[:, par(-3), :, :], na[:, :, 0:D], ALU.add)\
                            .then_inc(s_fin, 1)
                    if on(s - 1):
                        c = s - 1
                        X = xr[:, par(-1), :, :]
                        if n == 3:
                            rstd(mv_b, rs_b, s_b_stat, 24 * c + 8, s_b_rstd, 6 * c)
                        if n == 5:
                            g.wait_ge(s_b_hat, 12 * c + 4)
                            g.wait_ge(s_rows_in, 16 * (it + (r - 1) // 2) + 16)
                            g.wait_ge(s_xr_in[par(-1)], 16 * (it + (r - 1) // 2) + 16)
                            G.tensor_tensor(res[:], res[:], row(0), ALU.mult).then_inc(s_x1, 1)
                            G.tensor_tensor(X, X, row(1), ALU.add).then_inc(s_x1, 1)
                            g.wait_ge(s_x1, 3 * c + 2)
                            G.tensor_tensor(X, X, res[:], ALU.add).then_inc(s_x1, 1)
                        if n == 8:
                            rstd(mv_b, rs_b, s_b_stat, 24 * c + 16, s_b_rstd, 6 * c + 2)
                        if n == 10:
                            g.wait_ge(s_b_hat, 12 * c + 8)
                            G.tensor_tensor(res[:], res[:], row(2), ALU.mult).then_inc(s_h2, 1)
                            g.wait_ge(s_h2, 2 * c + 1)
                            G.tensor_tensor(res[:], res[:], row(3), ALU.add).then_inc(s_h2, 1)
                            g.wait_ge(s_h2, 2 * c + 2)
                            wait(g, s_lg_pe, c)
                            wait(g, s_xnl, 2 * c)
                            G.tensor_tensor(tmp_rows, res[:], row(4), ALU.mult).then_inc(s_base, 1)
                        if n == 11:
                            rstd(mv_b, rs_b, s_b_stat, 24 * c + 24, s_b_rstd, 6 * c + 4)
                    if n == 12 and on(s - 1):
                        c = s - 1
                        g.wait_ge(s_base, 2 * c + 1)
                        G.tensor_tensor(X, X, tmp_rows, ALU.add).then_inc(s_base, 1)
                    if n == 14 and on(s + 1):
                        c = s + 1
                        for k in range(KD):
                            g.wait_ge(s_sp, 2 * c + 2)
                            G.tensor_tensor(dt[:, k, :], dt[:, k, :], th[:, k, :], ALU.add).then_inc(s_dt, 1)
                        for k in range(KD):
                            g.wait_ge(s_dt, 2 * c + k + 1)
                            G.tensor_tensor(dtx[:, par(1), k, :], dt[:, k, :], xc[:, k, :], ALU.mult)\
                                .then_inc(s_dtx, 1)
            run_steps(g, step)

        @block.tensor
        def _(pe):
            M = nc.tensor.matmul
            TR = nc.tensor.transpose
            pe.wait_ge(s_mod_v, 2)
            for j in range(4):
                for k in range(KD):
                    last = M(misc[:, j * NB:(j + 1) * NB], wmod_sb[:, k, j * P:(j + 1) * P], cTs[:, k, :],
                             start=(k == 0), stop=(k == KD - 1))
            last.then_inc(s_mod_pe, 1)
            for h in range(2):
                for k in range(KD):
                    last = M(ep[h][0:NB, :], cTs[:, k, :], wmod_sb[:, k, 512 * (h + 1):512 * (h + 2)],
                             start=(k == 0), stop=(k == KD - 1))
                last.then_inc(s_mod_pe, 1)

            def exp_round(rd):
                kind, lhsT, rhs, _ = ROUNDS[rd]
                for i in range(NROT):
                    if rd == 0:
                        pe.wait_ge(s_ld_gens, 16 * NROT)
                        pe.wait_ge(s_mod_v, 4)
                    else:
                        pe.wait_ge(*round_taken(rd - 1, i))
                    if kind == "T":
                        for kr in range(KD):
                            for kc in range(KD):
                                last = TR(ex_bank[i][:, kc * D + kr * P:kc * D + (kr + 1) * P],
                                          xm(i, lhsT)[:, kr, kc * P:(kc + 1) * P], ident[:])
                    else:
                        for m in range(KD):
                            for k in range(KD):
                                last = M(ex_bank[i][:, m * D:(m + 1) * D], xm(i, lhsT)[:, k, m * P:(m + 1) * P],
                                         xm(i, rhs)[:, k, :], start=(k == 0), stop=(k == KD - 1))
                    last.then_inc(s_ex_pe, 1)

            def chain_round(j):
                if j == 0:
                    for i in range(NROT):
                        pe.wait_ge(*round_taken(len(ROUNDS) - 1, i))
                    pe.wait_ge(s_ld_ffn, N_LD_FFN)
                    pe.wait_ge(s_v0, 1)
                else:
                    pe.wait_ge(s_v_ev, 2 * j)
                for m in range(KD):
                    for k in range(KD):
                        last = M(ep[m][:, 0:D1], xm(NROT - 1 - j, 5)[:, k, m * P:(m + 1) * P], V[j % 2][:, k, :],
                                 start=(k == 0), stop=(k == KD - 1))
                    last.then_inc(s_v_pe, 1)
            R = V[NROT % 2]

            def fold_round(j):
                if j == 0:
                    pe.wait_ge(s_v_ev, 2 * NROT)
                    for k in range(KD):
                        last = M(hp[1][0:NE, 0:D1], eb2T[:, k, :], R[:, k, :], start=(k == 0), stop=(k == KD - 1))
                    last.then_inc(s_r_pe, 1)
                if j < PAIRS:
                    if j == 1:
                        pe.wait_ge(s_r_ev, 1)
                    if j >= 2:
                        pe.wait_ge(s_rt_ev, j - 1)
                    for t in range(2):
                        for k in range(KD):
                            last = TR(hp[j % 2][:, (2 * t + k) * P:(2 * t + k + 1) * P],
                                      w2[:, MA + 2 * j + t, k * P:(k + 1) * P], ident[:])
                    last.then_inc(s_rt_pe, 1)
                if j >= 1:
                    jj = j - 1
                    pe.wait_ge(s_rt_ev, jj + 1)
                    for t in range(2):
                        if jj >= 1:
                            pe.wait_ge(s_r_ev, 2 * (jj - 1) + t + 2)
                        for k in range(KD):
                            last = M(ep[t][:, 0:D1], rT[jj % 2][:, t, k, :], R[:, k, :], start=(k == 0), stop=(k == KD - 1))
                        last.then_inc(s_r_pe, 1)

            def setup(s, n):
                rd = setup_round(s, n)
                if rd is not None:
                    exp_round(rd)
                if s == 1 and n < NROT:
                    chain_round(n)
                if s == 1 and n >= NROT - 1:
                    fold_round(n - NROT + 1)
            pe.wait_ge(s_const, 8 + 2 * (NE - 1) + 3)
            pe.wait_ge(s_ld_attn, N_LD_ATTN)
            pe.wait_ge(s_mod_a, 2)

            def spread(c, n, j, q):
                i = 2 * n + j
                prev = i - 3 if i >= 3 else {0: 30, 1: 31, 2: 29}[i] - 2 * NS
                wait(pe, s_hc if prev % 2 else s_dbx, NS * c + prev // 2 + 1)
                M(bcp[i % 3][:], sel[:, j * NS + n:j * NS + n + 1].to_broadcast([P, P]), bcs[:, q, :],
                  start=True, stop=True).then_inc(s_bb, 1)

            def step(it, r):
                s = 2 * it + r
                par = lambda d: (r + d) % 2
                f, sc, b, m = s + 1, s, s - 1, s - 2

                def small(use):
                    misc_free(pe, use, s)
                    if use == "logits":
                        pe.wait_ge(s_xn, 4 * m + 4)
                        for t in range(NT):
                            for k in range(KD):
                                last = M(misc[:, t * 8:t * 8 + NE], xnT[:, k, t * P:(t + 1) * P], gate_w[:, k, :],
                                         start=(k == 0), stop=(k == KD - 1))
                        last.then_inc(s_lg_pe, 1)
                    elif use in ("o0", "o1"):
                        pe.wait_ge(s_y2, 2 * b + 2)
                        for t in range(2):
                            tt = 2 * (use == "o1") + t
                            ts = slice(tt * P, (tt + 1) * P)
                            for k in range(KD):
                                M(misc[:, t * D:(t + 1) * D], sg[:, k, ts], w_out[:, k, :], start=(k == 0), stop=False)
                            for k in range(KD):
                                last = M(misc[:, t * D + k * P:t * D + (k + 1) * P], h1T[:, par(-1), k, ts], ident[:],
                                         start=False, stop=(k == KD - 1))
                        last.then_inc(s_o_pe, 1)
                    elif use in ("t0", "t1"):
                        k = int(use[1])
                        pe.wait_ge(s_f_hat, 4 * f + 4)
                        for t in range(NT):
                            last = TR(misc[:, t * P:(t + 1) * P], xin[:, t, k * P:(k + 1) * P], ident[:])
                        last.then_inc(s_f_t, 1)
                    elif use in ("j0", "j1", "g0", "g1"):
                        j = int(use[1]) + 2 * (use[0] == "g")
                        c, q, done = (f, par(1), s_j) if use[0] == "j" else (sc, par(0), s_g_pe)
                        pe.wait_ge(s_h1, 2 * c + 2)
                        for k in range(KD):
                            last = M(misc[:], w_in[:, k, j * P:(j + 1) * P], h1T[:, q, k, :],
                                     start=(k == 0), stop=(k == KD - 1))
                        last.then_inc(done, 1)
                    elif use == "bc":
                        pe.wait_ge(s_xc, 2 * f + 2)
                        for k in range(KD):
                            last = M(misc[0:P, :], w_bc[:, k, :], xc[:, k, :], start=(k == 0), stop=(k == KD - 1))
                        last.then_inc(s_bc_pe, 1)
                    elif use in ("d0", "d1"):
                        j = int(use[1])
                        for k in range(KD):
                            last = M(misc[:], w_dt[:, k, j * P:(j + 1) * P], xc[:, k, :], start=(k == 0), stop=(k == KD - 1))
                        last.then_inc(s_d_pe, 1)
                    elif use in ("x0", "x1"):
                        k = int(use[1])
                        pe.wait_ge(s_b_hat, 12 * b + 12)
                        for t in range(NT):
                            last = TR(misc[:, t * P:(t + 1) * P], res[:, t, k * P:(k + 1) * P], ident[:])
                        last.then_inc(s_x_t, 1)
                    elif use == "wt":
                        pe.wait_ge(s_w, 3 * m + 3)
                        for t in range(NT):
                            last = TR(misc[0:NE, t * P:(t + 1) * P], wE[:, t, :], ident[:])
                        last.then_inc(s_wt_pe, 1)
                    else:
                        t = int(use[1])
                        pe.wait_ge(s_wt, m + 1)
                        M(misc[:, 0:D1], wT[:, t * P:(t + 1) * P], eb2r[:], start=True, stop=True).then_inc(s_n_pe, 1)

                def hidden(j, half):
                    for mm in (2 * half, 2 * half + 1):
                        h = ME * j + mm
                        wait(pe, s_gelu, MT * m + h - 1)
                        if h == 0 and isinstance(m, int) and m == 0:
                            pe.wait_ge(s_hi, MT // ME)
                            pe.wait_ge(s_lo, MT // ME)
                        if h == 0:
                            pe.wait_ge(s_xnl, 2 * m + 2)
                        ms = slice(h * P, (h + 1) * P)
                        n = 0
                        for wpart, xpart in ((w1h, xnh), (w1h, xnl), (w1l, xnh)):
                            for k in range(KD):
                                last = M(hp[h % 2][:], wpart[:, k, ms], xpart[:, k, :], start=(n == 0), stop=(n == 5))
                                n += 1
                        last.then_inc(s_hid, 1)

                def second(o):
                    j0, nk, t = (0, MA, o) if o < NT else (2 + (o - NT) // NT, ME, (o - NT) % NT)
                    wait(pe, s_eo_ev, NOUT * m + o - 1)
                    if o == 0 and isinstance(m, int) and m == 0:
                        pe.wait_ge(s_aw, 6)
                        pe.wait_ge(s_r_ev, MT - MA + 1)
                    pe.wait_ge(s_gelu, MT * m + ME * j0 + nk)
                    for kk in range(nk):
                        last = M(ep[o % 2][:, 0:D1], hid[:, (j0 + kk // ME) % 2, kk % ME, t * P:(t + 1) * P],
                                 w2[:, ME * j0 + kk, :], start=(kk == 0), stop=(kk == nk - 1))
                    last.then_inc(s_eo, 1)

                before_main = {0: ["logits"], 1: ["o0"], 2: ["o1"], 3: ["t0"], 4: ["wt"], 5: ["n0"], 6: ["n3"],
                               7: ["g0"], 8: ["g1"], 10: ["bc"], 12: ["d0"], 14: ["x0"]}
                amid = {3: ["t1"], 4: ["j0"], 5: ["n1"], 6: ["j1"], 12: ["d1"], 14: ["x1"]}
                at_end = {5: ["n2"]}

                def smalls(uses):
                    for use in uses:
                        if on(s + MISC[MISC_AT[use]][1]):
                            small(use)
                for n in range(NS):
                    if on(sc):
                        if n == 0:
                            pe.wait_ge(s_bcs, 4 * sc + 4)
                            spread(sc, 0, 0, par(0))
                        spread(sc, n, 1, par(0))
                        if n + 1 < NS:
                            spread(sc, n + 1, 0, par(0))
                    grp, i = n // 4, n % 4
                    smalls(before_main.get(n, []))
                    if on(m):
                        if i < 2:
                            hidden(2 * grp + i, 0)
                        elif grp == 0:
                            second(2 * (i - 2))
                        else:
                            for t in range(2):
                                second(NT + NT * (2 * grp + i - 4) + t)
                    smalls(amid.get(n, []))
                    if on(m):
                        if i < 2:
                            hidden(2 * grp + i, 1)
                        elif grp == 0:
                            second(2 * (i - 2) + 1)
                        else:
                            for t in range(2, 4):
                                second(NT + NT * (2 * grp + i - 4) + t)
                    smalls(at_end.get(n, []))
                    if isinstance(s, int):
                        setup(s, n)
            run_steps(pe, step)

        @block.scalar
        def _(act):
            A = nc.scalar.activation
            act.wait_ge(s_ld_mod, N_LD_MOD)
            A(cTh, cT, ACT.Tanh, scale=0.5).then_inc(s_mod_a, 1)
            act.wait_ge(s_mod_pe, 3)
            A(modT[:, :, :].rearrange("p b j -> p j b"), misc[:, 0:4 * NB].rearrange("p (j b) -> p j b", j=4), ACT.Copy)\
                .then_inc(s_mod_a, 1)
            act.wait_ge(s_ld_attn, N_LD_ATTN)
            A(neg_a[:], neg_a[:], ACT.Exp).then_inc(s_par_a, 1)
            A(b_gh[:], b_in[:, 2:4], ACT.Copy, scale=0.5).then_inc(s_par_a, 1)
            act.wait_ge(s_par_v, 5)

            def setup(s, n):
                rd = setup_round(s, n)
                if rd is not None and rd not in V_ROUNDS:
                    for i in range(NROT):
                        act.wait_ge(s_ex_pe, NROT * rd + i + 1)
                        bank = ex_bank[i][:].rearrange("p (k c) -> p k c", k=KD)
                        if rd == 0:
                            A(xm(i, 0), xm(i, 0), ACT.Copy, scale=SC)
                        A(xm(i, ROUNDS[rd][3]), bank, ACT.Copy, scale=SC if rd == 0 else 1.0).then_inc(s_ex_a, 1)
                if s == 0 and n == 0:
                    act.wait_ge(s_ld_ffn, N_LD_FFN)
                    A(gcb_half[:], gcb_half[:], ACT.Copy, scale=0.5).then_inc(s_par_a, 1)
                if s == 1 and n < NROT:
                    for m in range(KD):
                        act.wait_ge(s_v_pe, 2 * n + m + 1)
                        A(V[(n + 1) % 2][:, m, :], ep[m][:, 0:D1], ACT.Copy).then_inc(s_v_ev, 1)
                if s == 1 and n >= NROT - 1:
                    j = n - NROT + 1
                    if j == 0:
                        act.wait_ge(s_r_pe, 1)
                        A(eb2r[:], hp[1][0:NE, 0:D1], ACT.Copy).then_inc(s_r_ev, 1)
                    if j < PAIRS:
                        act.wait_ge(s_rt_pe, j + 1)
                        if j >= 2:
                            act.wait_ge(s_r_pe, 2 * (j - 1) + 1)
                        A(rT[j % 2], hp[j % 2][:].rearrange("p (t k c) -> p t k c", t=2, k=KD), ACT.Copy)\
                            .then_inc(s_rt_ev, 1)
                    if j >= 1:
                        for t in range(2):
                            kt = 2 * (j - 1) + t
                            act.wait_ge(s_r_pe, kt + 2)
                            A(w2[:, MA + kt, :], ep[t][:, 0:D1], ACT.Copy).then_inc(s_r_ev, 1)
                j = n - W1_SLOT0
                if s == 1 and 0 <= j < MT // ME:
                    act.wait_ge(s_ld_stage[j % 2], 16 * (j // 2 + 1))
                    A(w1h[:, :, j * H:(j + 1) * H], stage[j % 2], ACT.Copy, scale=WS).then_inc(s_hi, 1)

            def exps(c, n, q):
                for k in range(KD):
                    if k == 0:
                        act.wait_ge(s_dt, 2 * c + 2)
                        wait(act, s_y, NS * c + place_before(q, n) + 1)
                    A(ring[:, PLACE[q][n], k, :], dt[:, k, :], ACT.Exp, scale=neg_a[:, k, n:n + 1]).then_inc(s_dA, 1)

            def step(it, r):
                s = 2 * it + r
                par = lambda d: (r + d) % 2
                f, sc, b, m, o = s + 1, s, s - 1, s - 2, s - 3

                def small(use):
                    if use in ("t0", "t1"):
                        k = int(use[1])
                        if k == 0 and (r + 1) % 2 == 0:
                            bt = it + (r + 1) // 2
                            if not (isinstance(bt, int) and bt == 0):
                                wait(act, s_h1, 2 * f)
                            A(cur_mod[:, :], modT[:, bass.ds(bt, 1), :].rearrange("p o j -> p (o j)"), ACT.Copy)\
                                .then_inc(s_curmod, 1)
                            act.wait_ge(s_curmod, bt + 1)
                        act.wait_ge(s_f_t, 2 * f + k + 1)
                        wait(act, s_o_pe, 2 * f - 2)
                        A(h1T[:, par(1), k, :], misc[:], ACT.Identity, bias=cur_mod[:, k:k + 1],
                          scale=cur_mod[:, 2 + k:3 + k]).then_inc(s_h1, 1)
                    elif use in ("j0", "j1"):
                        k = int(use[1])
                        act.wait_ge(s_j, 2 * f + k + 1)
                        wait(act, s_cv, 9 * f)
                        A(xs[:, k, TAPS - 1:], misc[:], ACT.Identity, bias=b_in[:, k:k + 1]).then_inc(s_xs, 1)
                    elif use in ("g0", "g1"):
                        k = int(use[1])
                        act.wait_ge(s_g_pe, 2 * sc + k + 1)
                        wait(act, s_o_pe, 2 * sc)
                        A(sg[:, k, :], misc[:], ACT.Identity, bias=b_gh[:, k:k + 1], scale=0.5).then_inc(s_gv, 1)
                    elif use == "wt":
                        act.wait_ge(s_wt_pe, m + 1)
                        wait(act, s_bcs, 4 * (sc + 1) if on(sc) else 0)
                        A(wT[:], misc[0:NE, :], ACT.Copy).then_inc(s_wt, 1)
                    elif use[0] == "n":
                        t = int(use[1])
                        act.wait_ge(s_n_pe, 4 * m + t + 1)
                        wait(act, s_out, 16 * m)
                        A(na[:, t, :], misc[:, 0:D1], ACT.Copy).then_inc(s_na, 1)
                    elif use == "bc":
                        act.wait_ge(s_bc_pe, f + 1)
                        wait(act, s_bcs, 4 * f)
                        A(bcf[:], misc[0:P, :], ACT.Identity, bias=b_bc[:]).then_inc(s_bcf, 1)
                    elif use in ("d0", "d1"):
                        k = int(use[1])
                        act.wait_ge(s_d_pe, 2 * f + k + 1)
                        wait(act, s_sg, 2 * f)
                        wait(act, s_dtx, 2 * f)
                        wait(act, s_dA, 2 * NS * f)
                        A(dt[:, k, :], misc[:], ACT.Relu, bias=b_dt[:, k:k + 1]).then_inc(s_d_raw, 1)
                        A(th[:, k, :], misc[:], ACT.Abs, bias=b_dt[:, k:k + 1]).then_inc(s_d_raw, 1)
                    elif use in ("x0", "x1"):
                        k = int(use[1])
                        act.wait_ge(s_x_t, 2 * b + k + 1)
                        wait(act, s_hid, MT * b)
                        act.wait_ge(s_base, 2 * b + 2)
                        A(xnT[:, k, :], misc[:], ACT.Identity, bias=ln_b[:, k:k + 1], scale=ln_g[:, k:k + 1])\
                            .then_inc(s_xn, 1)
                        A(xnh[:, k, :], misc[:], ACT.Identity, bias=ln_b[:, k:k + 1], scale=ln_g[:, k:k + 1])\
                            .then_inc(s_xn, 1)

                def gelus(j, half):
                    if not on(m):
                        return
                    for mm in (2 * half, 2 * half + 1):
                        h = ME * j + mm
                        act.wait_ge(s_hid, MT * m + h + 1)
                        if h == 0 and isinstance(m, int) and m == 0:
                            act.wait_ge(s_lo, MT // ME)
                            act.wait_ge(s_r_pe, MT - MA + 1)
                        if mm == 0:
                            read = NOUT * m + (-NT * (1 - j) if j < 2 else NT if j < 4 else NT + NT * (j - 3))
                            wait(act, s_eo, read)
                        A(hid[:, j % 2, mm, :], hp[h % 2][:], ACT.Gelu, bias=b1[:, h:h + 1], scale=1.0 / WS)\
                            .then_inc(s_gelu, 1)

                def smalls(uses):
                    for use in uses:
                        if on(s + MISC[MISC_AT[use]][1]):
                            small(use)
                before_main = {3: ["t0"], 4: ["wt"], 5: ["n0"], 6: ["n3"],
                               7: ["g0"], 8: ["g1"], 10: ["bc"], 12: ["d0"], 14: ["x0"]}
                amid = {3: ["t1"], 4: ["j0"], 5: ["n1"], 6: ["j1"], 12: ["d1"], 14: ["x1"]}
                at_end = {5: ["n2"]}
                for n in range(NS):
                    grp, i = n // 4, n % 4
                    smalls(before_main.get(n, []))
                    if i < 2:
                        gelus(2 * grp + i, 0)
                    if n == 0 and on(o):
                        act.wait_ge(s_zs, o + 1)
                        A(gt[:], zs[:], ACT.Tanh, scale=0.5, bias=gcb_half[:]).then_inc(s_gth4, 1)
                    if n == 2 and on(m):
                        act.wait_ge(s_rt, 5 * m + 4)
                        A(wE[:], lg[:], ACT.Exp).then_inc(s_rexp, 1)
                    if n == 14 and on(f):
                        act.wait_ge(s_d_raw, 4 * f + 4)
                        A(th[:], th[:], ACT.Exp, scale=-1.0).then_inc(s_sp, 1)
                        act.wait_ge(s_sp, 2 * f + 1)
                        A(th[:], th[:], ACT.Ln, bias=1.0).then_inc(s_sp, 1)
                    if i >= 2 and n < 14 and on(sc):
                        exps(sc, 4 * grp + 4 + 2 * (i - 2), par(0))
                        exps(sc, 4 * grp + 5 + 2 * (i - 2), par(0))
                    smalls(amid.get(n, []))
                    if i < 2:
                        gelus(2 * grp + i, 1)
                    if n == 3 and on(o):
                        act.wait_ge(s_fin, 2 * o + 2)
                        act.dma_start(tok(par(-3), it + (r - 3) // 2)(out), na[:, :, 0:D]).then_inc(s_out, 16)
                    smalls(at_end.get(n, []))
                    if n == 8 and on(f):
                        act.wait_ge(s_cv, 9 * f + 8)
                        A(th[:], xc[:], ACT.Tanh).then_inc(s_th, 1)
                    if n == 9 and on(sc):
                        if on(f):
                            act.wait_ge(s_xc, 2 * f + 2)
                        act.wait_ge(s_gv, 2 * sc + 2)
                        A(th[:], sg[:], ACT.Tanh).then_inc(s_gth, 1)
                    if n == 15 and on(f):
                        for nn in range(4):
                            exps(f, nn, par(1))
                    if isinstance(s, int):
                        setup(s, n)
            run_steps(act, step)
            act.wait_ge(s_out, 16 * NC)

        @block.vector
        def _(v):
            V_ = nc.vector
            v.wait_ge(s_ld_mod, N_LD_MOD)
            v.wait_ge(s_mod_a, 1)
            V_.tensor_scalar(cTs, cT, 0.5, None, ALU.mult).then_inc(s_mod_v, 1)
            v.wait_ge(s_mod_v, 1)
            V_.scalar_tensor_tensor(cTs, cTh, 1.0, cTs, ALU.add, ALU.mult).then_inc(s_mod_v, 1)
            v.wait_ge(s_mod_pe, 3)
            V_.tensor_copy(mrow[:, 0:2, :], ep[0][0:NB, :].rearrange("p (r c) -> p r c", r=2)).then_inc(s_mod_v, 1)
            V_.tensor_copy(mrow[:, 2:4, :], ep[1][0:NB, :].rearrange("p (r c) -> p r c", r=2)).then_inc(s_mod_v, 1)
            v.wait_ge(s_mod_v, 4)
            V_.tensor_scalar(sign, mrow[:, 0:4:3, :], 0.0, 2.0, ALU.is_ge, ALU.mult).then_inc(s_mod_v, 1)
            V_.tensor_scalar(mtmp, mrow[:, 0:4:3, :], -1.0, None, ALU.mult).then_inc(s_mod_v, 1)
            v.wait_ge(s_mod_v, 6)
            V_.tensor_tensor(mtmp, mtmp, mrow[:, 0:4:3, :], ALU.max).then_inc(s_mod_v, 1)
            v.wait_ge(s_mod_v, 7)
            V_.tensor_scalar(mtmp, mtmp, 0.25, None, ALU.max).then_inc(s_mod_v, 1)
            v.wait_ge(s_mod_v, 8)
            V_.scalar_tensor_tensor(mrow[:, 0:4:3, :], sign, -1.0, mtmp, ALU.add, ALU.mult).then_inc(s_mod_v, 1)
            v.wait_ge(s_mod_v, 9)
            V_.tensor_tensor(prow[:, 0:2, :], lnrow, mrow[:, 0:1, :].to_broadcast([NB, 2, D]), ALU.mult)
            V_.tensor_scalar(prow[:, 2, :], mrow[:, 2, :], 1.0, None, ALU.add).then_inc(s_mod_v, 1)
            V_.tensor_copy(prow[:, 3, :], mrow[:, 1, :]).then_inc(s_mod_v, 1)
            V_.tensor_copy(prow2, mrow[:, 3, :]).then_inc(s_mod_v, 1)
            v.wait_ge(s_mod_a, 2)
            V_.tensor_scalar(modT[:, :, 2:4], modT[:, :, 2:4], 1.0, None, ALU.add).then_inc(s_par_v, 1)
            v.wait_ge(s_par_a, 2)
            V_.tensor_scalar(neg_a[:], neg_a[:], -1.0, None, ALU.mult).then_inc(s_par_v, 1)
            V_.tensor_scalar(conv_w[:], conv_w[:], 0.5, None, ALU.mult).then_inc(s_par_v, 1)
            V_.tensor_scalar(conv_b[:], conv_b[:], 0.5, None, ALU.mult).then_inc(s_par_v, 1)
            v.wait_ge(s_const, 8)
            V_.memset(xnT[:, 0, :], 0.0).then_inc(s_par_v, 1)
            v.wait_ge(s_par_v, 5)
            for k in range(KD):
                V_.tensor_copy(eye[:, k, k * P:(k + 1) * P], ident[:]).then_inc(s_ex_q, 1)
            nq = [KD]

            def setup(s, n):
                rd = setup_round(s, n)
                if rd in V_ROUNDS:
                    g = V_ROUNDS[-1] - rd
                    for i in range(NROT):
                        v.wait_ge(*round_taken(1, i))
                        if rd > V_ROUNDS[0]:
                            v.wait_ge(*round_taken(rd - 1, i))
                        terms = ((eye, c_tay[3 * g]), (xm(i, 0), c_tay[3 * g + 1]), (xm(i, 2), c_tay[3 * g + 2]))
                        for t, (src, cf) in enumerate(terms):
                            v.wait_ge(s_ex_q, nq[0])
                            if t == 0:
                                V_.tensor_scalar(xm(i, 5), src, cf, None, ALU.mult).then_inc(s_ex_q, 1)
                            else:
                                V_.scalar_tensor_tensor(xm(i, 5), src, cf, xm(i, 5), ALU.mult, ALU.add).then_inc(s_ex_q, 1)
                            nq[0] += 1
                    v.wait_ge(s_ex_q, nq[0])
                    for i in range(NROT):
                        v.wait_ge(s_ex_pe, NROT * rd + i + 1)
                        V_.scalar_tensor_tensor(xm(i, 4), ex_bank[i][:].rearrange("p (k c) -> p k c", k=KD),
                                                c_tay[TAYLOR] if rd == V_ROUNDS[0] else 1.0, xm(i, 5), ALU.mult, ALU.add)\
                            .then_inc(s_ex_v, 1)
                if s == 0 and n == 1:
                    v.wait_ge(s_ld_ffn, N_LD_FFN)
                    for h in range(2):
                        if h:
                            v.wait_ge(s_aw, 2)
                        V_.tensor_tensor(aw_tmp[:], w2[:, 4 * h:4 * h + 4, 0:D], g1_bc.unsqueeze(1).to_broadcast([P, 4, D]),
                                         ALU.mult).then_inc(s_aw, 1)
                        v.wait_ge(s_aw, 2 * h + 1)
                        V_.tensor_reduce(w2[:, 4 * h:4 * h + 4, D:D1], aw_tmp[:], AX, ALU.add).then_inc(s_aw, 1)
                    v.wait_ge(s_aw, 4)
                    V_.tensor_tensor(aw_tmp[:, 0, :], ab2_bc[:, 0:D], g1_bc, ALU.mult).then_inc(s_aw, 1)
                    v.wait_ge(s_aw, 5)
                    V_.tensor_reduce(ab2_bc[:, D:D1], aw_tmp[:, 0, :], AX, ALU.add).then_inc(s_aw, 1)
                    V_.tensor_copy(V[0][:, :, 0:D], eye).then_inc(s_v0, 1)
                j = n - W1_SLOT0
                if s == 1 and 0 <= j < MT // ME:
                    v.wait_ge(s_hi, j + 1)
                    V_.scalar_tensor_tensor(w1l[:, :, j * H:(j + 1) * H], stage[j % 2], WS, w1h[:, :, j * H:(j + 1) * H],
                                            ALU.mult, ALU.subtract).then_inc(s_lo, 1)

            def stats(src, st, mv, done, base):
                for t in range(NT):
                    V_.bn_stats(st[:, t, :], src[:, t, :]).then_inc(done, 1)
                v.wait_ge(done, base + NT)
                V_.memset(spare[:], 0.0)
                for t in range(NT):
                    V_.bn_aggr(mv[:, t, :], st[:, t, :]).then_inc(done, 1)

            def normalise(dst, src, mv, rs, done):
                for t in range(NT):
                    V_.tensor_scalar(dst[:, t, :], src[:, t, :], mv[:, t, 0:1], rs[:, t:t + 1], ALU.subtract, ALU.mult)\
                        .then_inc(done, 1)

            def step(it, r):
                s = 2 * it + r
                par = lambda d: (r + d) % 2
                f, sc, b, m, o = s + 1, s, s - 1, s - 2, s - 3

                def take(oo):
                    if not on(m):
                        return
                    v.wait_ge(s_eo, NOUT * m + oo + 1)
                    bank = ep[oo % 2][:, 0:D1]
                    if oo < NT:
                        if oo == 0:
                            wait(v, s_mix, 5 * m)
                            if isinstance(m, int) and m == 0:
                                v.wait_ge(s_r_pe, MT - MA + 1)
                        V_.tensor_tensor(ab[:, oo, :], bank, ab2_bc[:], ALU.add).then_inc(s_eo_ev, 1)
                    else:
                        e, t = (oo - NT) // NT, (oo - NT) % NT
                        if e == 0:
                            v.wait_ge(s_na, 4 * m + t + 1)
                        else:
                            v.wait_ge(s_eo_ev, NOUT * m + oo - NT + 1)
                        V_.scalar_tensor_tensor(na[:, t, :], bank, wE[:, t, e:e + 1], na[:, t, :], ALU.mult, ALU.add)\
                            .then_inc(s_eo_ev, 1)

                for n in range(NS):
                    grp, i = n // 4, n % 4
                    outs = [] if i < 2 else [None, 2 * (i - 2), None, 2 * (i - 2) + 1] if grp == 0 else \
                        [NT + NT * (2 * grp + i - 4) + t for t in range(NT)]

                    def take_at(pos):
                        if outs and outs[pos] is not None:
                            take(outs[pos])
                    if n == 0 and on(o):
                        v.wait_ge(s_eo_ev, NOUT * o + NOUT)
                        V_.tensor_tensor(zs[:], ab[:, :, D:D1], na[:, :, D:D1], ALU.add).then_inc(s_zs, 1)
                        V_.tensor_tensor(na[:, :, 0:D], na[:, :, 0:D], ab[:, :, 0:D], ALU.subtract).then_inc(s_mix, 1)
                    if on(sc):
                        base = 2 * NS * sc + 2 * n
                        bi, ci = 2 * NS * sc + 2 * n + 1, 2 * NS * sc + 2 * n + 2
                        v.wait_ge(s_bb, bi)
                        if n == 0:
                            v.wait_ge(s_dtx, 2 * sc + 2)
                        wait(v, s_scan, base)
                        V_.tensor_tensor(u[:], dtx[:, par(0), :, :], bcp[(2 * n) % 3][:].unsqueeze(1).to_broadcast([P, KD, CH]),
                                         ALU.mult).then_inc(s_dbx, 1)
                    take_at(0)
                    if on(sc):
                        slot_ = ring[:, PLACE[par(0)][n], :, :]
                        for k in range(KD):
                            v.wait_ge(s_dA, base + k + 1)
                            v.wait_ge(s_dbx, NS * sc + n + 1)
                            V_.tensor_tensor_scan(slot_[:, k, :], slot_[:, k, :], u[:, k, :],
                                                  0.0 if par(0) == 0 else state[:, n, k:k + 1], ALU.mult, ALU.add)\
                                .then_inc(s_scan, 1)
                            take_at(1 + k)
                        if par(0) == 0:
                            v.wait_ge(s_scan, base + 2)
                            V_.tensor_copy(state[:, n, :], slot_[:, :, CH - 1]).then_inc(s_tail, 1)
                        v.wait_ge(s_bb, ci)
                        if par(0) == 0:
                            v.wait_ge(s_tail, NS // 2 * sc + n + 1)
                        v.wait_ge(s_scan, base + 2)
                        V_.tensor_tensor(slot_, slot_, bcp[(2 * n + 1) % 3][:].unsqueeze(1).to_broadcast([P, KD, CH]),
                                         ALU.mult).then_inc(s_hc, 1)
                    else:
                        take_at(1)
                        take_at(2)
                    take_at(3)

                    if n == 0:
                        if on(f):
                            v.wait_ge(s_x_in, 16 * (f + 1))
                            stats(xin, st_f, mv_f, s_f_stat, 8 * f)
                        if on(m):
                            v.wait_ge(s_lg_pe, m + 1)
                            V_.tensor_tensor(lg[:], misc[:, 0:8 * NT].rearrange("p (t e) -> p t e", t=NT)[:, :, 0:NE],
                                             gate_b_bc[:].unsqueeze(1).to_broadcast([P, NT, NE]), ALU.add)\
                                .then_inc(s_rt, 1)
                            v.wait_ge(s_rt, 5 * m + 1)
                            other = lg[:].unsqueeze(2).to_broadcast([P, NT, NE, NE])
                            mine = lg[:].unsqueeze(3).to_broadcast([P, NT, NE, NE])
                            V_.tensor_tensor(rk[:], other, mine, ALU.is_ge)
                            V_.tensor_tensor(rk2[:], other, mine, ALU.is_gt)
                            V_.tensor_reduce(lgm[:], lg[:], AX, ALU.max).then_inc(s_rt, 1)
                            v.wait_ge(s_rt, 5 * m + 2)
                            V_.tensor_tensor(lg[:], lg[:], lgm[:].to_broadcast([P, NT, NE]), ALU.subtract)
                            V_.tensor_tensor(rk[:], rk[:], before[:].unsqueeze(1).to_broadcast([P, NT, NE, NE]), ALU.mult)
                            V_.tensor_tensor(rk2[:], rk2[:], after[:].unsqueeze(1).to_broadcast([P, NT, NE, NE]), ALU.mult)\
                                .then_inc(s_rt, 1)
                            v.wait_ge(s_rt, 5 * m + 3)
                            V_.tensor_tensor(rk[:], rk[:], rk2[:], ALU.add).then_inc(s_rt, 1)
                            v.wait_ge(s_rt, 5 * m + 4)
                            V_.tensor_reduce(rsum[:], rk[:], AX, ALU.add).then_inc(s_rt, 1)
                    if n == 1:
                        if on(b):
                            v.wait_ge(s_o_pe, 2 * b + 1)
                            V_.tensor_tensor(res[:, 0:2, :], misc[:].rearrange("p (t c) -> p t c", t=2),
                                             b_out_bc[:].unsqueeze(1).to_broadcast([P, 2, D]), ALU.add).then_inc(s_res, 1)
                        if on(f):
                            v.wait_ge(s_f_rstd, 2 * f + 2)
                            normalise(xin, xin, mv_f, rs_f, s_f_hat)
                        if on(o):
                            v.wait_ge(s_gth4, o + 1)
                            v.wait_ge(s_mix, 5 * o + 1)
                            V_.tensor_scalar(gt[:], gt[:], 0.5, 0.5, ALU.mult, ALU.add).then_inc(s_gate, 1)
                            v.wait_ge(s_gate, o + 1)
                            for t in range(NT):
                                V_.scalar_tensor_tensor(na[:, t, 0:D], na[:, t, 0:D], gt[:, t, :], ab[:, t, 0:D],
                                                        ALU.mult, ALU.add).then_inc(s_mix, 1)
                    if n == 2 and on(b):
                        v.wait_ge(s_o_pe, 2 * b + 2)
                        V_.tensor_tensor(res[:, 2:4, :], misc[:].rearrange("p (t c) -> p t c", t=2),
                                         b_out_bc[:].unsqueeze(1).to_broadcast([P, 2, D]), ALU.add).then_inc(s_res, 1)
                        v.wait_ge(s_res, 2 * b + 2)
                        stats(res, st_b, mv_b, s_b_stat, 24 * b)
                    if n == 3 and on(m):
                        v.wait_ge(s_rexp, m + 1)
                        v.wait_ge(s_rt, 5 * m + 5)
                        V_.scalar_tensor_tensor(wE[:], rsum[:], 1.5, wE[:], ALU.is_lt, ALU.mult).then_inc(s_w, 1)
                        v.wait_ge(s_w, 3 * m + 1)
                        V_.tensor_reduce(lgs[:], wE[:], AX, ALU.add).then_inc(s_wsum, 1)
                        v.wait_ge(s_wsum, m + 1)
                        V_.reciprocal(lgs[:], lgs[:]).then_inc(s_w, 1)
                        v.wait_ge(s_w, 3 * m + 2)
                        V_.tensor_tensor(wE[:], wE[:], lgs[:].to_broadcast([P, NT, NE]), ALU.mult).then_inc(s_w, 1)
                    if n == 4 and on(b):
                        v.wait_ge(s_b_rstd, 6 * b + 2)
                        normalise(res, res, mv_b, rs_b, s_b_hat)
                    if n in (5, 7) and on(f):
                        k = (n - 5) // 2
                        v.wait_ge(s_xs, 2 * f + k + 1)
                        if k == 0:
                            wait(v, s_yinit, 2 * f)
                            wait(v, s_dtx, 2 * f)
                        for j in range(TAPS):
                            src = xs[:, k, j:j + CH]
                            if j == 0:
                                if k == 0 and isinstance(f, int) and f == 0:
                                    v.wait_ge(s_par_v, 4)
                                V_.tensor_scalar(xc[:, k, :], src, conv_w[:, k, 0:1], conv_b[:, k:k + 1], ALU.mult, ALU.add)\
                                    .then_inc(s_cv, 1)
                            else:
                                v.wait_ge(s_cv, 9 * f + 4 * k + j)
                                V_.scalar_tensor_tensor(xc[:, k, :], src, conv_w[:, k, j:j + 1], xc[:, k, :],
                                                        ALU.mult, ALU.add).then_inc(s_cv, 1)
                        if k == 1:
                            v.wait_ge(s_cv, 9 * f + 8)
                            if par(1) == 0:
                                V_.tensor_copy(xs[:, :, 0:TAPS - 1], xs[:, :, CH:CH + TAPS - 1]).then_inc(s_cv, 1)
                            else:
                                V_.memset(xs[:, :, 0:TAPS - 1], 0.0).then_inc(s_cv, 1)
                    if n == 7 and on(b):
                        v.wait_ge(s_x1, 3 * b + 3)
                        stats(xr[:, par(-1)], st_b, mv_b, s_b_stat, 24 * b + 8)
                    if n == 9:
                        if on(f):
                            v.wait_ge(s_th, f + 1)
                            for k in range(KD):
                                V_.scalar_tensor_tensor(xc[:, k, :], th[:, k, :], 1.0, xc[:, k, :], ALU.add, ALU.mult)\
                                    .then_inc(s_xc, 1)
                        if on(b):
                            v.wait_ge(s_b_rstd, 6 * b + 4)
                            normalise(res, xr[:, par(-1)], mv_b, rs_b, s_b_hat)
                    if n == 10 and on(sc):
                        v.wait_ge(s_gth, sc + 1)
                        for k in range(KD):
                            V_.scalar_tensor_tensor(sg[:, k, :], th[:, k, :], 1.0, sg[:, k, :], ALU.add, ALU.mult)\
                                .then_inc(s_sg, 1)
                    if n == 11:
                        if on(b):
                            v.wait_ge(s_h2, 2 * b + 2)
                            stats(res, st_b, mv_b, s_b_stat, 24 * b + 16)
                        if on(f):
                            v.wait_ge(s_bcf, f + 1)
                            q = par(1)
                            V_.tensor_copy(bcs[:, q, :], bcf[:]).then_inc(s_bcs, 1)
                            v.wait_ge(s_bcs, 4 * f + 1)
                            V_.tensor_tensor(bcf[P // 2:P, :], bcf[P // 2:P, :], bcs[P // 2:P, q, :], ALU.subtract)\
                                .then_inc(s_bcs, 1)
                            v.wait_ge(s_bcs, 4 * f + 2)
                            V_.tensor_copy(bcs[P // 2:P, q, :], bcf[P // 2:P, :]).then_inc(s_bcs, 1)
                            v.wait_ge(s_bcs, 4 * f + 3)
                            V_.tensor_tensor(bcs[3 * P // 4:P, q, :], bcf[3 * P // 4:P, :], bcs[3 * P // 4:P, q, :],
                                             ALU.subtract).then_inc(s_bcs, 1)
                    if n == 12 and on(b):
                        v.wait_ge(s_b_rstd, 6 * b + 6)
                        v.wait_ge(s_base, 2 * b + 1)
                        normalise(res, res, mv_b, rs_b, s_b_hat)
                    if n == 15 and on(b):
                        v.wait_ge(s_xn, 4 * b + 4)
                        wait(v, s_hid, MT * b)
                        for k in range(KD):
                            V_.tensor_tensor(xnl[:, k, :], xnT[:, k, :], xnh[:, k, :], ALU.subtract).then_inc(s_xnl, 1)
                    if isinstance(s, int):
                        setup(s, n)
            run_steps(v, step)


def kernel(**inputs):
    import numpy as _np
    import concourse.bacc as _bacc
    from concourse import mybir as _mybir
    from concourse.bass_utils import run_bass_kernel_spmd as _run

    nc = _bacc.Bacc("TRN2", target_bir_lowering=False, num_devices=1)
    arrays, args = {}, {}
    for name, value in inputs.items():
        arr = _np.ascontiguousarray(value)
        arrays[f"in_{name}_dram"] = arr
        args[name] = nc.dram_tensor(f"in_{name}_dram", arr.shape, _mybir.dt.from_np(arr.dtype), kind="ExternalInput").ap()
    shape = inputs["L0_attn_x"].shape
    out = nc.dram_tensor("out_0_dram", shape, _mybir.dt.float32, kind="ExternalOutput").ap()
    build_adaln_mamba_moe(nc, args, out)
    r = _run(nc, [arrays], core_ids=[0])
    return r.results[0]["out_0_dram"]
```

```python
import concourse.bass as bass
from concourse import mybir
from contextlib import ExitStack
from math import factorial

f32 = mybir.dt.float32
f16 = mybir.dt.float16
bf16 = mybir.dt.bfloat16
ALU = mybir.AluOpType
ACT = mybir.ActivationFunctionType
AX = mybir.AxisListType.X


def build_adaln_mamba_moe(nc, a, out):
    NB, T, D = a["L0_attn_x"].shape
    NS = a["L0_attn_A_log"].shape[1]
    NE, _, H = a["L0_ffn_ew1"].shape
    HA = a["L0_ffn_aw1"].shape[1]
    P = 128
    KD = D // P
    CH = 512
    NT = CH // P
    CPB = T // CH
    NC = NB * CPB
    TAPS = a["L0_attn_conv_w"].shape[2]
    MA = HA // P
    ME = H // P
    MT = MA + NE * ME
    NOUT = NT + NE * NT
    D1 = D + 1
    RING = 6
    FULL = 3
    WS = 64.0
    EPS = 1e-5
    SQUARINGS = 4
    TAYLOR = 12
    NROT = a["L0_ffn_gens"].shape[0]
    assert CPB == 2 and KD == 2 and NT == 4 and NS == 16 and ME == 4 and MA == 8

    ctx = ExitStack()
    with ctx:
        def sb(name, shape, dt=f32):
            return ctx.enter_context(nc.sbuf_tensor(name, shape, dt))

        def pb(name, shape=(P, 512), dt=f32):
            return ctx.enter_context(nc.psum_tensor(name, list(shape), dt))

        def sem(name):
            return ctx.enter_context(nc.semaphore(name))

        w_inh = sb("w_inh", [P, KD, 2 * D], f16)
        w_inl = sb("w_inl", [P, KD, 2 * D], f16)
        w_dt = sb("w_dt", [P, KD, D])
        w_bc = sb("w_bc", [P, KD, P])
        w_out = sb("w_out", [P, KD, D])
        w1h = sb("w1h", [P, KD, MT * P], f16)
        w1l = sb("w1l", [P, KD, MT * P], f16)
        w2 = sb("w2", [P, MT, D1])
        w2_16 = w2[:, :, :].bitcast(f16)
        w2h, w2l = w2_16[:, :, 0:D1], w2_16[:, :, D1:2 * D1]
        gate_w = sb("gate_w", [P, KD, NE])
        b1 = sb("b1", [P, MT])
        b_in = sb("b_in", [P, 4])
        b_gh = sb("b_gh", [P, KD])
        conv_w = sb("conv_w", [P, KD, TAPS])
        conv_b = sb("conv_b", [P, KD])
        b_dt = sb("b_dt", [P, KD])
        b_bc = sb("b_bc", [P, 1])
        neg_a = sb("neg_a", [P, KD, NS])
        d_skip = sb("d_skip", [P, KD])
        ln_g = sb("ln_g", [P, KD])
        ln_b = sb("ln_b", [P, KD])
        modT = sb("modT", [P, NB, 4])
        cur_mod = sb("cur_mod", [P, 4])
        b_out_bc = sb("b_out_bc", [P, D])
        ab2_bc = sb("ab2_bc", [P, D1])
        gate_b_bc = sb("gate_b_bc", [P, NE])
        gcb_half = sb("gcb_half", [P, 1])
        eb2r = sb("eb2r", [NE, D1])
        ident = sb("ident", [P, P])
        ident16 = sb("ident16", [P, P], f16)
        sel = sb("sel", [P, 2 * NS], bf16)
        before = sb("before", [P, NE, NE])
        after = sb("after", [P, NE, NE])
        neg_half = sb("neg_half", [P, NT])
        eps = sb("eps", [P, NT])
        spare = sb("spare", [P, 1])
        warm = sb("warm", [P, 1])
        zero = sb("zero", [P, NT])
        aw_col = sb("aw_col", [P, MA, 1])

        ring = sb("ring", [P, RING, KD, CH])
        u = sb("u", [P, CH])
        xin = sb("xin", [P, NT, D])
        xr = sb("xr", [P, 2, NT, D])
        res = sb("res", [P, NT, D])
        h1h = sb("h1h", [P, 2, KD, CH], f16)
        h1l = sb("h1l", [P, 2, KD, CH], f16)
        xs = sb("xs", [P, KD, TAPS - 1 + CH])
        xc = sb("xc", [P, KD, CH])
        th = sb("th", [P, KD, CH])
        sg = sb("sg", [P, KD, CH])
        bcs = sb("bcs", [P, 2, CH], bf16)
        bcf = xin[:, 0:2, :].rearrange("p t d -> p (t d)")
        dt = sb("dt", [P, KD, CH])
        dtx = sb("dtx", [P, 2, KD, CH])
        xnT = sb("xnT", [P, KD, CH])
        xnh = sb("xnh", [P, KD, CH], f16)
        xnl = sb("xnl", [P, KD, CH], f16)
        rows = sb("rows", [P, 5, D])
        gb_fin = sb("gb_fin", [P, D])
        hid = sb("hid", [P, 2, ME, CH])
        hidh = hid[:, 0, :, :].bitcast(f16).rearrange("p m (l c) -> p (m l) c", l=2).rearrange("p (j m) c -> p j m c", j=2)
        hidl = hid[:, 1, :, :].bitcast(f16).rearrange("p m (l c) -> p (m l) c", l=2).rearrange("p (j m) c -> p j m c", j=2)
        full = sb("full", [P, FULL, CH])
        ab = sb("ab", [P, NT, D1])
        na = sb("na", [P, NT, D1])
        y = sb("y", [P, KD, CH])
        state = sb("state", [P, NS, KD])
        st_f = sb("st_f", [P, NT, 6]); mv_f = sb("mv_f", [P, NT, 2]); rs_f = sb("rs_f", [P, NT]); nb_f = sb("nb_f", [P, NT])
        st_b = sb("st_b", [P, NT, 6]); mv_b = sb("mv_b", [P, NT, 2]); rs_b = sb("rs_b", [P, NT]); nb_b = sb("nb_b", [P, NT])
        lg = sb("lg", [P, NT, NE]); lgm = sb("lgm", [P, NT, 1]); lgs = sb("lgs", [P, NT, 1])
        rk, rk2 = [th[:, k, 0:NT * NE * NE].rearrange("p (t i j) -> p t i j", t=NT, i=NE) for k in range(KD)]
        rsum = sb("rsum", [P, NT, NE])
        wE = sb("wE", [P, NT, NE])
        wT = xin[0:NE, 2:4, :].rearrange("p t d -> p (t d)")
        zs = sb("zs", [P, NT, 1])
        gt = sb("gt", [P, NT, 1])

        bcp = [pb(f"bcp{i}") for i in range(3)]
        hp = [pb(f"hp{i}") for i in range(2)]
        ep = [pb(f"ep{i}") for i in range(2)]
        misc = pb("misc")

        s_ld_mod = sem("s_ld_mod"); s_ld_attn = sem("s_ld_attn"); s_ld_ffn = sem("s_ld_ffn")
        s_ld_stage = [sem(f"s_ld_stage{i}") for i in range(2)]
        s_ld_gens = sem("s_ld_gens"); s_const = sem("s_const")
        s_mod_v = sem("s_mod_v"); s_mod_a = sem("s_mod_a"); s_mod_pe = sem("s_mod_pe")
        s_rows_out = sem("s_rows_out"); s_par_v = sem("s_par_v"); s_par_a = sem("s_par_a")
        s_hi = sem("s_hi"); s_lo = sem("s_lo")
        s_ex_pe = sem("s_ex_pe"); s_ex_v = sem("s_ex_v"); s_ex_a = sem("s_ex_a"); s_v0 = sem("s_v0"); s_ex_q = sem("s_ex_q")
        s_v_pe = sem("s_v_pe"); s_v_ev = sem("s_v_ev")
        s_rt_pe = sem("s_rt_pe"); s_rt_ev = sem("s_rt_ev"); s_r_pe = sem("s_r_pe"); s_r_ev = sem("s_r_ev")
        s_r_hi = sem("s_r_hi"); s_eb2 = sem("s_eb2"); s_aw_hi = sem("s_aw_hi")
        s_aw = sem("s_aw"); s_win_hi = sem("s_win_hi"); s_win_lo = sem("s_win_lo"); s_h1l = sem("s_h1l"); s_warm = sem("s_warm")

        s_x_in = sem("s_x_in"); s_xr_in = [sem(f"s_xr_in{q}") for q in range(2)]; s_rows_in = sem("s_rows_in"); s_gbf_in = sem("s_gbf_in")
        s_out = sem("s_out")
        s_f_stat = sem("s_f_stat"); s_f_rstd = sem("s_f_rstd"); s_f_hat = sem("s_f_hat"); s_f_t = sem("s_f_t")
        s_curmod = sem("s_curmod"); s_h1 = sem("s_h1"); s_j = sem("s_j"); s_xs = sem("s_xs"); s_cv0 = sem("s_cv0"); s_cv = sem("s_cv")
        s_th = sem("s_th"); s_xc = sem("s_xc"); s_bc_pe = sem("s_bc_pe"); s_bcf = sem("s_bcf"); s_bcs = sem("s_bcs")
        s_d_pe = sem("s_d_pe"); s_d_raw = sem("s_d_raw"); s_sp = sem("s_sp"); s_dt = sem("s_dt"); s_dtx = sem("s_dtx")
        s_g_pe = sem("s_g_pe"); s_gv = sem("s_gv"); s_gth = sem("s_gth"); s_sg = sem("s_sg")
        s_bb = sem("s_bb"); s_dA = [sem(f"s_dA{k}") for k in range(KD)]; s_dbx = sem("s_dbx"); s_scan = sem("s_scan"); s_tail = sem("s_tail")
        s_hc = sem("s_hc"); s_y = sem("s_y"); s_yinit = sem("s_yinit"); s_y2 = sem("s_y2")
        s_o_pe = sem("s_o_pe"); s_res = sem("s_res"); s_b_stat = sem("s_b_stat"); s_b_rstd = sem("s_b_rstd")
        s_b_hat = sem("s_b_hat"); s_x1 = sem("s_x1"); s_h2 = sem("s_h2"); s_base = sem("s_base")
        s_x_t = sem("s_x_t"); s_xn = sem("s_xn"); s_xnl = sem("s_xnl")
        s_lg_pe = sem("s_lg_pe"); s_rt = sem("s_rt"); s_rexp = sem("s_rexp"); s_w = sem("s_w")
        s_wt_pe = sem("s_wt_pe"); s_wt = sem("s_wt"); s_n_pe = sem("s_n_pe"); s_na = sem("s_na")
        s_hid = sem("s_hid"); s_gelu = sem("s_gelu"); s_hlo_v = sem("s_hlo_v"); s_hlo_p = sem("s_hlo_p"); s_eo = sem("s_eo"); s_eo_ev = sem("s_eo_ev")
        s_zs = sem("s_zs"); s_gate = sem("s_gate"); s_wsum = sem("s_wsum"); s_gth4 = sem("s_gth4"); s_mix = sem("s_mix"); s_fin = sem("s_fin")

        rows_dram = nc.dram_tensor("mod_rows", (NB, 5 * D), f32, kind="Internal").ap()

        PLACE = [[0, 1, 2, 3, 4, 5, 0, 1, 2, 4, 3, 5, 0, 1, 2, 4], [3, 0, 5, 1, 4, 2, 3, 0, 5, 4, 1, 2, 0, 3, 5, 4]]

        def place_before(q, n):
            return next(m for m in range(n - 1, -NS - 1, -1) if PLACE[q if m >= 0 else 1 - q][m % NS] == PLACE[q][n])

        def on(c):
            return not isinstance(c, int) or 0 <= c < NC

        def wait(eng, s, value):
            if not isinstance(value, int) or value > 0:
                eng.wait_ge(s, value)

        def run_steps(eng, step):
            step(-1, 1)
            for it in range(0, LOOP0):
                step(it, 0)
                step(it, 1)
            if LOOP:
                with eng.Fori(LOOP0, LOOP1) as it:
                    step(it, 0)
                    step(it, 1)
            else:
                for it in range(LOOP0, LOOP1):
                    step(it, 0)
                    step(it, 1)
            for it in range(LOOP1, (NC + 4) // 2):
                step(it, 0)
                step(it, 1)
        LOOP = True
        LOOP0, LOOP1 = 2, (NC - 2) // 2

        MISC = [("logits", -2, s_rt, 5, 1), ("o0", -1, s_res, 2, 1), ("o1", -1, s_res, 2, 2),
                ("t0", 1, s_h1, 2, 1), ("t1", 1, s_h1, 2, 2), ("wt", -2, s_wt, 1, 1), ("j0", 1, s_xs, 2, 1),
                ("j1", 1, s_xs, 2, 2), ("n0", -2, s_na, 4, 1), ("n1", -2, s_na, 4, 2), ("n2", -2, s_na, 4, 3),
                ("n3", -2, s_na, 4, 4), ("g0", 0, s_gv, 2, 1), ("g1", 0, s_gv, 2, 2), ("bc", 1, s_bcf, 1, 1),
                ("d0", 1, s_d_raw, 4, 2), ("d1", 1, s_d_raw, 4, 4), ("x0", -1, s_xn, 4, 2), ("x1", -1, s_xn, 4, 4)]
        BEFORE = {0: ["logits"], 3: ["t1"], 12: ["d0"]}
        AMID = {1: ["o1"], 2: ["t0"], 3: ["wt"], 4: ["j1"], 5: ["n1"], 6: ["n3"], 7: ["g1"], 11: ["bc"], 12: ["d1"]}
        AFTER = {0: ["o0"], 3: ["j0"], 4: ["n0"], 5: ["n2"], 6: ["g0"], 13: ["x0"], 14: ["x1"]}
        MISC_AT = {m[0]: i for i, m in enumerate(MISC)}

        def misc_free(eng, use, s):
            for back in range(1, 3 * len(MISC)):
                i = MISC_AT[use] - back
                steps_ago = -(i // len(MISC))
                _, delta, done, per, idx = MISC[i % len(MISC)]
                c = s - steps_ago + delta
                if on(c):
                    eng.wait_ge(done, per * c + idx)
                    return

        w1f = [w[:, :, :].rearrange("p k n -> p (k n)").bitcast(f32).rearrange("p (s c) -> p s c", c=512)
               for w in (w1h, w1l)]
        hidf = hid[:, :, :, :].rearrange("p a m c -> p (a m) c")

        def xm(i, slot):
            n = i * 6 + slot
            return (w1f + [hidf])[n // 8][:, n % 8, :].rearrange("p (k c) -> p k c", k=KD)
        eye = xnT[:, 0, :].rearrange("p (k c) -> p k c", k=KD)
        ex_bank = [hp[0], hp[1], ep[0], ep[1]]
        ROUNDS = [("T", 0, 0, 1), ("P", 1, 0, 2), ("P", 2, 1, 3), ("P", 1, 2, 4), ("P", 3, 4, 4), ("P", 3, 4, 4),
                  ("P", 3, 4, 4)]
        V_ROUNDS = (3, 4, 5, 6)
        for _ in range(SQUARINGS):
            ROUNDS += [("T", 4, 4, 5), ("P", 5, 4, 4)]
        ROUNDS += [("T", 4, 4, 5)]

        def round_taken(rd, i):
            by_v = rd in V_ROUNDS
            return (s_ex_v if by_v else s_ex_a), NROT * sum((q in V_ROUNDS) == by_v for q in range(rd)) + i + 1

        def setup_round(s, n):
            if s == -1 and n % 2 == 0:
                return n // 2
            if s == 0 and n % 2 == 0 and 8 + n // 2 < len(ROUNDS):
                return 8 + n // 2
            return None
        assert len(ROUNDS) == 16
        PAIRS = (MT - MA) // 2
        stage = [hid[:, 0, 2 * i:2 * i + 2, :].rearrange("p a c -> p (a c)").rearrange("p (k c) -> p k c", k=KD) for i in range(2)]
        wmod_sb = ring[:, 0:3, :, :].rearrange("p a b c -> p (a b c)").rearrange("p (k c) -> p k c", k=KD)
        cT = ring[:, 3, 0, 0:KD * NB].rearrange("p (k b) -> p k b", k=KD)
        cTh = ring[:, 3, 0, 64:64 + KD * NB].rearrange("p (k b) -> p k b", k=KD)
        cTs = ring[:, 3, 0, 128:128 + KD * NB].rearrange("p (k b) -> p k b", k=KD)
        mrow = ring[0:NB, 4, :, :].rearrange("p a c -> p (a c)").rearrange("p (r c) -> p r c", r=4)
        lnrow = ring[0:NB, 5, 0, :].rearrange("p (r c) -> p r c", r=2)
        mtmp = ring[0:NB, 5, 1, :].rearrange("p (r c) -> p r c", r=2)
        prow = y[0:NB, :, :].rearrange("p k c -> p (k c)")[:, 0:4 * D].rearrange("p (r c) -> p r c", r=4)
        prow2 = sg[0:NB, 0, 0:D]
        sign = sg[0:NB, 1, 0:2 * D].rearrange("p (r c) -> p r c", r=2)
        aw_tmp = res
        aw = xr[:, :, :, :].rearrange("p a t d -> p (a t) d")
        g1_bc = na[:, 2, 0:D]
        eb2T = na[:, 3, 0:KD * NE].rearrange("p (k e) -> p k e", k=KD)
        V = [ab[:, 0:KD, :], na[:, 0:KD, :]]
        rT = [hid[:, 1, i, :].rearrange("p (t k c) -> p t k c", t=2, k=KD) for i in range(2)]
        c_tay = [1.0 / factorial(j) for j in range(TAYLOR + 1)]
        SC = 2.0 ** -SQUARINGS
        W1_SLOT0 = 5

        def tok(c_half, b):
            return lambda t: t[b, c_half * CH:(c_half + 1) * CH, :].rearrange("(t p) d -> p t d", p=P)

        block = ctx.enter_context(nc.Block())

        @block.sync
        def _(sp):
            X = a["L0_attn_x"]
            n_mod = [0]

            def ld(s, dst, src):
                sp.dma_start(dst, src).then_inc(s, 16)

            colk = lambda v: v.rearrange("(k p) -> p k", p=P)
            with nc.allow_non_contiguous_dma(reason="small parameters, once"):
                sp.dma_start(xin[:], tok(0, 0)(X)).then_inc(s_x_in, 16)
                ld(s_ld_mod, wmod_sb, a["L0_wmod"].rearrange("(k p) n -> p k n", p=P))
                for k in range(KD):
                    ld(s_ld_mod, cT[:, k, :], a["L0_c"][:, k * P:(k + 1) * P].rearrange("b p -> p b"))
                ld(s_ld_mod, lnrow[:, 0, :], a["L0_attn_ln_g"].partition_broadcast(NB))
                ld(s_ld_mod, lnrow[:, 1, :], a["L0_attn_ln_b"].partition_broadcast(NB))
                ld(s_ld_attn, th[:], a["L0_attn_W_in"].rearrange("(k p) n -> p k n", p=P))
                ld(s_ld_attn, w_dt[:], a["L0_attn_W_dt"].rearrange("(k p) n -> p k n", p=P))
                for r in range(4):
                    ld(s_ld_attn, w_bc[:, :, r * 2 * NS:(r + 1) * 2 * NS],
                       a["L0_attn_W_bc"].rearrange("(k p) n -> p k n", p=P))
                    ld(s_ld_attn, b_bc[r * 2 * NS:(r + 1) * 2 * NS, :],
                       a["L0_attn_b_bc"].rearrange("(n o) -> n o", o=1))
                ld(s_ld_attn, w_out[:], a["L0_attn_W_out"].rearrange("(k p) n -> p k n", p=P))
                ld(s_ld_attn, b_in[:], colk(a["L0_attn_b_in"]))
                ld(s_ld_attn, conv_w[:], a["L0_attn_conv_w"].rearrange("(k p) o t -> p k (o t)", p=P))
                ld(s_ld_attn, conv_b[:], colk(a["L0_attn_conv_b"]))
                ld(s_ld_attn, b_dt[:], colk(a["L0_attn_b_dt"]))
                ld(s_ld_attn, neg_a[:], a["L0_attn_A_log"].rearrange("(k p) n -> p k n", p=P))
                ld(s_ld_attn, d_skip[:], colk(a["L0_attn_D"]))
                ld(s_ld_attn, b_out_bc[:], a["L0_attn_b_out"].partition_broadcast(P))
                for i in range(NROT):
                    ld(s_ld_gens, xm(i, 0), a["L0_ffn_gens"][i].rearrange("(k p) n -> p k n", p=P))
                ld(s_ld_ffn, ln_g[:], colk(a["L0_ffn_ln_g"]))
                ld(s_ld_ffn, ln_b[:], colk(a["L0_ffn_ln_b"]))
                ld(s_ld_ffn, gate_w[:], a["L0_ffn_gate_w"].rearrange("(k p) e -> p k e", p=P))
                ld(s_ld_ffn, gate_b_bc[:], a["L0_ffn_gate_b"].partition_broadcast(P))
                ld(s_ld_ffn, gcb_half[:], a["L0_ffn_gc_b"].partition_broadcast(P))
                ld(s_ld_ffn, ab2_bc[:, 0:D], a["L0_ffn_ab2"].partition_broadcast(P))
                ld(s_ld_ffn, b1[:, 0:MA], a["L0_ffn_ab1"].rearrange("(m p) -> p m", p=P))
                ld(s_ld_ffn, b1[:, MA:MT], a["L0_ffn_eb1"].rearrange("e (m p) -> p (e m)", p=P))
                ld(s_ld_ffn, g1_bc, a["L0_ffn_gc_w"][0:D, :].rearrange("d o -> (d o)").partition_broadcast(P))
                ld(s_ld_ffn, V[0][:, :, D:D1], a["L0_ffn_gc_w"][D:2 * D, :].rearrange("(k p) o -> p k o", p=P))
                for k in range(KD):
                    ld(s_ld_ffn, eb2T[:, k, :], a["L0_ffn_eb2"][:, k * P:(k + 1) * P].rearrange("e p -> p e"))
                ld(s_ld_ffn, aw, a["L0_ffn_aw2"].rearrange("(m p) d -> p m d", p=P))
                for e in range(NE):
                    ld(s_ld_ffn, w2[:, MA + e * ME:MA + (e + 1) * ME, 0:D],
                       a["L0_ffn_ew2"][e].rearrange("(m p) d -> p m d", p=P))
                sp.wait_ge(s_mod_v, 12)
                sp.dma_start(rows_dram[:, 0:4 * D].rearrange("b (r c) -> b r c", r=4), prow).then_inc(s_rows_out, 16)
                sp.dma_start(rows_dram[:, 4 * D:5 * D], prow2).then_inc(s_rows_out, 16)
                sp.wait_ge(s_rows_out, 32)
                sp.dma_start(rows[:], rows_dram[0, :].partition_broadcast(P).rearrange("p (r c) -> p r c", r=5))\
                    .then_inc(s_rows_in, 16)
                sp.dma_start(gb_fin[:], rows_dram[0, 4 * D:5 * D].partition_broadcast(P)).then_inc(s_gbf_in, 16)

            def load_piece(j):
                src = a["L0_ffn_aw1"][:, j * H:(j + 1) * H] if j < 2 else a["L0_ffn_ew1"][j - 2]
                sp.dma_start(stage[j % 2], src.rearrange("(k p) n -> p k n", p=P)).then_inc(s_ld_stage[j % 2], 16)

            def step(it, r):
                s = 2 * it + r
                batch = lambda d: it + (r + d) // 2
                par = lambda d: (r + d) % 2
                if on(s - 1):
                    wait(sp, s_fin, 2 * (s - 2))
                    if isinstance(s, int) and s == 1:
                        sp.wait_ge(s_aw, 8)
                    sp.dma_start(xr[:, par(-1), :, :], tok(par(-1), batch(-1))(X)).then_inc(s_xr_in[par(-1)], 16)
                if isinstance(s, int) and s == 1:
                    sp.wait_ge(s_v_ev, 2 * NROT)
                    load_piece(0)
                    load_piece(1)
                if on(s - 3) and r == 0 and on(s - 2):
                    wait(sp, s_fin, 2 * (s - 2))
                    sp.dma_start(gb_fin[:], rows_dram[batch(-2), 4 * D:5 * D].partition_broadcast(P))\
                        .then_inc(s_gbf_in, 16)
                if isinstance(s, int) and s == 1:
                    for j in range(2, MT // ME):
                        sp.wait_ge(s_hi, j - 1)
                        sp.wait_ge(s_lo, j - 1)
                        load_piece(j)
                if on(s + 2):
                    wait(sp, s_bcs, 4 * (s + 2))
                    sp.dma_start(xin[:], tok(par(2), batch(2))(X)).then_inc(s_x_in, 16)
                if r == 0 and on(s - 1) and on(s):
                    wait(sp, s_base, 2 * (s - 1) + 2)
                    sp.dma_start(rows[:], rows_dram[batch(0), :].partition_broadcast(P)
                                 .rearrange("p (r c) -> p r c", r=5)).then_inc(s_rows_in, 16)
            run_steps(sp, step)

        N_LD_MOD = 16 * (1 + KD + 2)
        N_LD_ATTN = 16 * (2 + 8 + 8)
        N_LD_FFN = 16 * (10 + KD + 1 + NE)

        @block.gpsimd
        def _(g):
            G = nc.gpsimd
            G.memset(ident[:], 0.0).then_inc(s_const, 1)
            G.memset(sel[:], 0.0).then_inc(s_const, 1)
            G.memset(before[:], 0.0).then_inc(s_const, 1)
            G.memset(after[:], 0.0).then_inc(s_const, 1)
            G.memset(neg_half[:], -0.5).then_inc(s_const, 1)
            G.memset(eps[:], EPS).then_inc(s_const, 1)
            G.memset(xs[:, :, 0:TAPS - 1], 0.0).then_inc(s_const, 1)
            G.memset(zero[:], 0.0).then_inc(s_const, 1)
            g.wait_ge(s_const, 8)
            G.affine_select(out=ident[:], in_=ident[:], compare_op=ALU.not_equal, fill=1.0, base=0,
                            pattern=[[-1, P]], channel_multiplier=1).then_inc(s_const, 1)
            for e in range(1, NE):
                G.memset(before[:, e, 0:e], 1.0).then_inc(s_const, 1)
                G.memset(after[:, e - 1, e:NE], 1.0).then_inc(s_const, 1)
            n0 = 9 + 2 * (NE - 1)
            for n, r in enumerate((0, 2, 3)):
                g.wait_ge(s_const, n0 + n)
                G.affine_select(out=sel[:], in_=sel[:], compare_op=ALU.not_equal, fill=1.0, base=-r * 2 * NS,
                                pattern=[[-1, 2 * NS]], channel_multiplier=1).then_inc(s_const, 1)

            def rstd(mv, rs, nb, ready, value, done, per_c):
                g.wait_ge(ready, value)
                G.tensor_tensor(rs[:], mv[:, :, 1], eps[:], ALU.add).then_inc(done, 1)
                g.wait_ge(done, per_c + 1)
                G.tensor_tensor(rs[:], rs[:], neg_half[:], ALU.pow).then_inc(done, 1)
                g.wait_ge(done, per_c + 2)
                G.tensor_tensor(nb[:], mv[:, :, 0], rs[:], ALU.mult).then_inc(done, 1)
                g.wait_ge(done, per_c + 3)
                G.tensor_tensor(nb[:], zero[:], nb[:], ALU.subtract).then_inc(done, 1)

            tmp_rows = xnT[:, :, :].rearrange("p k c -> p (k c)").rearrange("p (t d) -> p t d", t=NT)

            def row(r):
                return rows[:, r:r + 1, :].to_broadcast([P, NT, D])

            def hidden_low(m, h):
                g.wait_ge(s_gelu, MT * m + h + 1)
                G.tensor_tensor(hidl[:, h // ME % 2, h % ME, :], full[:, h % FULL, :], hidh[:, h // ME % 2, h % ME, :],
                                ALU.subtract).then_inc(s_hlo_p, 1)


            def step(it, r):
                s = 2 * it + r
                par = lambda d: (r + d) % 2
                for n in range(NS):
                    if n == 0:
                        if on(s - 1):
                            g.wait_ge(s_sg, 2 * (s - 1) + 2)
                            g.wait_ge(s_y, NS * s)
                            for k in range(KD):
                                G.tensor_tensor(sg[:, k, :], sg[:, k, :], y[:, k, :], ALU.mult).then_inc(s_y2, 1)
                        if on(s):
                            g.wait_ge(s_xc, 2 * s + 2)
                            wait(g, s_y2, 2 * s)
                            if isinstance(s, int) and s == 0:
                                g.wait_ge(s_ld_attn, N_LD_ATTN)
                                g.wait_ge(s_rows_out, 32)
                            for k in range(KD):
                                G.tensor_tensor(y[:, k, :], xc[:, k, :], d_skip[:, k:k + 1].to_broadcast([P, CH]), ALU.mult)\
                                    .then_inc(s_yinit, 1)
                    if n == 0 and on(s + 1):
                        rstd(mv_f, rs_f, nb_f, s_f_stat, 8 * (s + 1) + 8, s_f_rstd, 4 * (s + 1))
                    if n == 3 and on(s - 1):
                        rstd(mv_b, rs_b, nb_b, s_b_stat, 24 * (s - 1) + 8, s_b_rstd, 12 * (s - 1))
                    if on(s - 2) and n % 4 < 2:
                        hidden_low(s - 2, ME * (2 * (n // 4) + n % 4) + 1)
                        hidden_low(s - 2, ME * (2 * (n // 4) + n % 4) + 3)
                    if n == 14 and on(s + 1):
                        for k in range(KD):
                            g.wait_ge(s_sp, 2 * (s + 1) + 2)
                            G.tensor_tensor(dt[:, k, :], dt[:, k, :], th[:, k, :], ALU.add).then_inc(s_dt, 1)
                    if on(s):
                        i = NS * s + n
                        g.wait_ge(s_hc, i + 1)
                        if n == 0:
                            g.wait_ge(s_yinit, 2 * s + 2)
                        else:
                            g.wait_ge(s_y, i)
                        G.tensor_tensor(y[:], y[:], ring[:, PLACE[par(0)][n], :, :], ALU.add).then_inc(s_y, 1)
                    if n == 14 and on(s + 1):
                        c = s + 1
                        for k in range(KD):
                            g.wait_ge(s_dt, 2 * c + k + 1)
                            G.tensor_tensor(dtx[:, par(1), k, :], dt[:, k, :], xc[:, k, :], ALU.mult)\
                                .then_inc(s_dtx, 1)
                    if n == 2 and on(s - 3):
                        c = s - 3
                        g.wait_ge(s_mix, 5 * c + 5)
                        g.wait_ge(s_gbf_in, 16 * (it + (r - 3) // 2) + 16)
                        G.tensor_tensor(na[:, :, 0:D], na[:, :, 0:D], gb_fin[:, :].unsqueeze(1).to_broadcast([P, NT, D]),
                                        ALU.mult).then_inc(s_fin, 1)
                        g.wait_ge(s_fin, 2 * c + 1)
                        G.tensor_tensor(na[:, :, 0:D], xr[:, par(-3), :, :], na[:, :, 0:D], ALU.add)\
                            .then_inc(s_fin, 1)
                    if on(s - 1):
                        c = s - 1
                        X = xr[:, par(-1), :, :]
                        if n == 5:
                            g.wait_ge(s_b_hat, 12 * c + 4)
                            g.wait_ge(s_rows_in, 16 * (it + (r - 1) // 2) + 16)
                            g.wait_ge(s_xr_in[par(-1)], 16 * (it + (r - 1) // 2) + 16)
                            G.tensor_tensor(res[:], res[:], row(0), ALU.mult).then_inc(s_x1, 1)
                            G.tensor_tensor(X, X, row(1), ALU.add).then_inc(s_x1, 1)
                            g.wait_ge(s_x1, 3 * c + 2)
                            G.tensor_tensor(X, X, res[:], ALU.add).then_inc(s_x1, 1)
                        if n == 8:
                            rstd(mv_b, rs_b, nb_b, s_b_stat, 24 * c + 16, s_b_rstd, 12 * c + 4)
                        if n == 10:
                            g.wait_ge(s_b_hat, 12 * c + 8)
                            G.tensor_tensor(res[:], res[:], row(2), ALU.mult).then_inc(s_h2, 1)
                            g.wait_ge(s_h2, 2 * c + 1)
                            G.tensor_tensor(res[:], res[:], row(3), ALU.add).then_inc(s_h2, 1)
                            g.wait_ge(s_h2, 2 * c + 2)
                            wait(g, s_lg_pe, c)
                            wait(g, s_xnl, 2 * c)
                            G.tensor_tensor(tmp_rows, res[:], row(4), ALU.mult).then_inc(s_base, 1)
                        if n == 11:
                            rstd(mv_b, rs_b, nb_b, s_b_stat, 24 * c + 24, s_b_rstd, 12 * c + 8)
                    if n == 12 and on(s - 1):
                        c = s - 1
                        g.wait_ge(s_base, 2 * c + 1)
                        G.tensor_tensor(X, X, tmp_rows, ALU.add).then_inc(s_base, 1)
            run_steps(g, step)

        @block.tensor
        def _(pe):
            M = nc.tensor.matmul
            TR = nc.tensor.transpose
            pe.wait_ge(s_mod_v, 2)
            for j in range(4):
                for k in range(KD):
                    last = M(misc[:, j * NB:(j + 1) * NB], wmod_sb[:, k, j * P:(j + 1) * P], cTs[:, k, :],
                             start=(k == 0), stop=(k == KD - 1))
            last.then_inc(s_mod_pe, 1)
            for h in range(2):
                for k in range(KD):
                    last = M(ep[h][0:NB, :], cTs[:, k, :], wmod_sb[:, k, 512 * (h + 1):512 * (h + 2)],
                             start=(k == 0), stop=(k == KD - 1))
                last.then_inc(s_mod_pe, 1)

            def exp_round(rd):
                kind, lhsT, rhs, _ = ROUNDS[rd]
                for i in range(NROT):
                    if rd == 0:
                        pe.wait_ge(s_ld_gens, 16 * NROT)
                        pe.wait_ge(s_mod_v, 4)
                    else:
                        pe.wait_ge(*round_taken(rd - 1, i))
                    if kind == "T":
                        for kr in range(KD):
                            for kc in range(KD):
                                last = TR(ex_bank[i][:, kc * D + kr * P:kc * D + (kr + 1) * P],
                                          xm(i, lhsT)[:, kr, kc * P:(kc + 1) * P], ident[:])
                    else:
                        for m in range(KD):
                            for k in range(KD):
                                last = M(ex_bank[i][:, m * D:(m + 1) * D], xm(i, lhsT)[:, k, m * P:(m + 1) * P],
                                         xm(i, rhs)[:, k, :], start=(k == 0), stop=(k == KD - 1))
                    last.then_inc(s_ex_pe, 1)

            def chain_round(j):
                if j == 0:
                    for i in range(NROT):
                        pe.wait_ge(*round_taken(len(ROUNDS) - 1, i))
                    pe.wait_ge(s_ld_ffn, N_LD_FFN)
                    pe.wait_ge(s_v0, 1)
                else:
                    pe.wait_ge(s_v_ev, 2 * j)
                for m in range(KD):
                    for k in range(KD):
                        last = M(ep[m][:, 0:D1], xm(NROT - 1 - j, 5)[:, k, m * P:(m + 1) * P], V[j % 2][:, k, :],
                                 start=(k == 0), stop=(k == KD - 1))
                    last.then_inc(s_v_pe, 1)
            R = V[NROT % 2]

            def fold_round(j):
                if j == 0:
                    pe.wait_ge(s_v_ev, 2 * NROT)
                    for k in range(KD):
                        last = M(hp[1][0:NE, 0:D1], eb2T[:, k, :], R[:, k, :], start=(k == 0), stop=(k == KD - 1))
                    last.then_inc(s_r_pe, 1)
                if j < PAIRS:
                    if j == 1:
                        pe.wait_ge(s_eb2, 1)
                    if j >= 2:
                        pe.wait_ge(s_rt_ev, j - 1)
                    for t in range(2):
                        for k in range(KD):
                            last = TR(hp[j % 2][:, (2 * t + k) * P:(2 * t + k + 1) * P],
                                      w2[:, MA + 2 * j + t, k * P:(k + 1) * P], ident[:])
                    last.then_inc(s_rt_pe, 1)
                if j >= 1:
                    jj = j - 1
                    pe.wait_ge(s_rt_ev, jj + 1)
                    for t in range(2):
                        if jj >= 1:
                            pe.wait_ge(s_r_ev, 2 * (jj - 1) + t + 1)
                        for k in range(KD):
                            last = M(ep[t][:, 0:D1], rT[jj % 2][:, t, k, :], R[:, k, :], start=(k == 0), stop=(k == KD - 1))
                        last.then_inc(s_r_pe, 1)

            def setup(s, n):
                rd = setup_round(s, n)
                if rd is not None:
                    exp_round(rd)
                if s == 1 and n < NROT:
                    chain_round(n)
                if s == 1 and n >= NROT - 1:
                    fold_round(n - NROT + 1)
            pe.wait_ge(s_const, 9 + 2 * (NE - 1) + 3)
            pe.wait_ge(s_ld_attn, N_LD_ATTN)
            pe.wait_ge(s_mod_a, 2)
            pe.wait_ge(s_win_lo, 2)

            def spread(c, n, j, q):
                i = 2 * n + j
                prev = i - 3 if i >= 3 else {0: 30, 1: 31, 2: 29}[i] - 2 * NS
                if prev % 2:
                    wait(pe, s_hc, NS * c + prev // 2 + 1)
                else:
                    wait(pe, s_dbx, 2 * NS * c + 2 * (prev // 2) + 2)
                M(bcp[i % 3][:], sel[:, j * NS + n:j * NS + n + 1].to_broadcast([P, P]), bcs[:, q, :],
                  start=True, stop=True).then_inc(s_bb, 1)

            def step(it, r):
                s = 2 * it + r
                par = lambda d: (r + d) % 2
                f, sc, b, m = s + 1, s, s - 1, s - 2

                def small(use):
                    misc_free(pe, use, s)
                    if use == "logits":
                        pe.wait_ge(s_xn, 4 * m + 4)
                        for t in range(NT):
                            for k in range(KD):
                                last = M(misc[:, t * 8:t * 8 + NE], xnT[:, k, t * P:(t + 1) * P], gate_w[:, k, :],
                                         start=(k == 0), stop=(k == KD - 1))
                        last.then_inc(s_lg_pe, 1)
                    elif use in ("o0", "o1"):
                        pe.wait_ge(s_y2, 2 * b + 2)
                        for t in range(2):
                            tt = 2 * (use == "o1") + t
                            ts = slice(tt * P, (tt + 1) * P)
                            for k in range(KD):
                                M(misc[:, t * D:(t + 1) * D], sg[:, k, ts], w_out[:, k, :], start=(k == 0), stop=False)
                            for k in range(KD):
                                for part in (h1h, h1l):
                                    last = M(misc[:, t * D + k * P:t * D + (k + 1) * P], part[:, par(-1), k, ts], ident16[:],
                                             start=False, stop=(k == KD - 1 and part is h1l))
                        last.then_inc(s_o_pe, 1)
                    elif use in ("t0", "t1"):
                        k = int(use[1])
                        pe.wait_ge(s_f_hat, 4 * f + 4)
                        for t in range(NT):
                            last = TR(misc[:, t * P:(t + 1) * P], xin[:, t, k * P:(k + 1) * P], ident[:])
                        last.then_inc(s_f_t, 1)
                    elif use in ("j0", "j1", "g0", "g1"):
                        j = int(use[1]) + 2 * (use[0] == "g")
                        c, q, done = (f, par(1), s_j) if use[0] == "j" else (sc, par(0), s_g_pe)
                        pe.wait_ge(s_h1, 2 * c + 2)
                        for k in range(KD):
                            for wpart in (w_inh, w_inl):
                                M(misc[:], wpart[:, k, j * P:(j + 1) * P], h1h[:, q, k, :],
                                  start=(k == 0 and wpart is w_inh), stop=False)
                        pe.wait_ge(s_h1l, 2 * c + 2)
                        for k in range(KD):
                            last = M(misc[:], w_inh[:, k, j * P:(j + 1) * P], h1l[:, q, k, :], start=False, stop=(k == KD - 1))
                        last.then_inc(done, 1)
                    elif use == "bc":
                        pe.wait_ge(s_xc, 2 * f + 2)
                        for k in range(KD):
                            last = M(misc[0:P, :], w_bc[:, k, :], xc[:, k, :], start=(k == 0), stop=(k == KD - 1))
                        last.then_inc(s_bc_pe, 1)
                    elif use in ("d0", "d1"):
                        j = int(use[1])
                        for k in range(KD):
                            last = M(misc[:], w_dt[:, k, j * P:(j + 1) * P], xc[:, k, :], start=(k == 0), stop=(k == KD - 1))
                        last.then_inc(s_d_pe, 1)
                    elif use in ("x0", "x1"):
                        k = int(use[1])
                        pe.wait_ge(s_b_hat, 12 * b + 12)
                        for t in range(NT):
                            last = TR(misc[:, t * P:(t + 1) * P], res[:, t, k * P:(k + 1) * P], ident[:])
                        last.then_inc(s_x_t, 1)
                    elif use == "wt":
                        pe.wait_ge(s_w, 3 * m + 3)
                        for t in range(NT):
                            last = TR(misc[0:NE, t * P:(t + 1) * P], wE[:, t, :], ident[:])
                        last.then_inc(s_wt_pe, 1)
                    else:
                        t = int(use[1])
                        pe.wait_ge(s_wt, m + 1)
                        M(misc[:, 0:D1], wT[:, t * P:(t + 1) * P], eb2r[:], start=True, stop=True).then_inc(s_n_pe, 1)

                def hidden(j, half):
                    for mm in (2 * half, 2 * half + 1):
                        h = ME * j + mm
                        wait(pe, s_gelu, MT * m + h - 1)
                        if h == 0 and isinstance(m, int) and m == 0:
                            pe.wait_ge(s_hi, MT // ME)
                            pe.wait_ge(s_lo, MT // ME)
                        if h == 0:
                            pe.wait_ge(s_xnl, 2 * m + 2)
                        ms = slice(h * P, (h + 1) * P)
                        n = 0
                        for wpart, xpart in ((w1h, xnh), (w1h, xnl), (w1l, xnh)):
                            for k in range(KD):
                                last = M(hp[h % 2][:], wpart[:, k, ms], xpart[:, k, :], start=(n == 0), stop=(n == 5))
                                n += 1
                        last.then_inc(s_hid, 1)

                def second(o):
                    j0, nk, t = (0, MA, o) if o < NT else (2 + (o - NT) // NT, ME, (o - NT) % NT)
                    wait(pe, s_eo_ev, NOUT * m + o - 1)
                    if o == 0 and isinstance(m, int) and m == 0:
                        pe.wait_ge(s_aw, 8)
                        pe.wait_ge(s_r_ev, MT - MA)
                    hs = lambda w, kk: w[:, (j0 + kk // ME) % 2, kk % ME, t * P:(t + 1) * P]
                    if o > 0:
                        pe.wait_ge(s_gelu, MT * m + ME * j0 + nk)
                    for kk in range(nk):
                        if o == 0:
                            pe.wait_ge(s_gelu, MT * m + kk + 1)
                        for wpart in (w2h, w2l):
                            M(ep[o % 2][:, 0:D1], hs(hidh, kk), wpart[:, ME * j0 + kk, :],
                              start=(kk == 0 and wpart is w2h), stop=False)
                    pe.wait_ge(s_hlo_v, MT // 2 * m + (ME * j0 + nk) // 2)
                    pe.wait_ge(s_hlo_p, MT // 2 * m + (ME * j0 + nk) // 2)
                    for kk in range(nk):
                        last = M(ep[o % 2][:, 0:D1], hs(hidl, kk), w2h[:, ME * j0 + kk, :], start=False, stop=(kk == nk - 1))
                    last.then_inc(s_eo, 1)

                def smalls(uses):
                    for use in uses:
                        if on(s + MISC[MISC_AT[use]][1]):
                            small(use)
                for n in range(NS):
                    if on(sc):
                        if n == 0:
                            pe.wait_ge(s_bcs, 4 * sc + 4)
                            spread(sc, 0, 0, par(0))
                    grp, i = n // 4, n % 4
                    smalls(BEFORE.get(n, []))
                    if on(m):
                        if i < 2:
                            hidden(2 * grp + i, 0)
                        elif grp == 0:
                            second(2 * (i - 2))
                        else:
                            for t in range(2):
                                second(NT + NT * (2 * grp + i - 4) + t)
                    if on(sc):
                        spread(sc, n, 1, par(0))
                    smalls(AMID.get(n, []))
                    if on(m):
                        if i < 2:
                            hidden(2 * grp + i, 1)
                        elif grp == 0:
                            second(2 * (i - 2) + 1)
                        else:
                            for t in range(2, 4):
                                second(NT + NT * (2 * grp + i - 4) + t)
                    if on(sc) and n + 1 < NS:
                        spread(sc, n + 1, 0, par(0))
                    smalls(AFTER.get(n, []))
                    if isinstance(s, int):
                        setup(s, n)
            run_steps(pe, step)

        @block.scalar
        def _(act):
            A = nc.scalar.activation
            act.wait_ge(s_ld_mod, N_LD_MOD)
            A(cTh, cT, ACT.Tanh, scale=0.5).then_inc(s_mod_a, 1)
            act.wait_ge(s_mod_pe, 3)
            A(modT[:, :, :].rearrange("p b j -> p j b"), misc[:, 0:4 * NB].rearrange("p (j b) -> p j b", j=4), ACT.Copy)\
                .then_inc(s_mod_a, 1)
            act.wait_ge(s_ld_attn, N_LD_ATTN)
            A(neg_a[:], neg_a[:], ACT.Exp).then_inc(s_par_a, 1)
            A(b_gh[:], b_in[:, 2:4], ACT.Copy, scale=0.5).then_inc(s_par_a, 1)
            A(w_inh[:], th[:], ACT.Copy, scale=WS).then_inc(s_win_hi, 1)
            act.wait_ge(s_par_v, 5)

            def setup(s, n):
                rd = setup_round(s, n)
                if rd is not None and rd not in V_ROUNDS:
                    for i in range(NROT):
                        act.wait_ge(s_ex_pe, NROT * rd + i + 1)
                        bank = ex_bank[i][:].rearrange("p (k c) -> p k c", k=KD)
                        if rd == 0:
                            A(xm(i, 0), xm(i, 0), ACT.Copy, scale=SC)
                        A(xm(i, ROUNDS[rd][3]), bank, ACT.Copy, scale=SC if rd == 0 else 1.0).then_inc(s_ex_a, 1)
                if s == 0 and n == 0:
                    act.wait_ge(s_ld_ffn, N_LD_FFN)
                    A(gcb_half[:], gcb_half[:], ACT.Copy, scale=0.5).then_inc(s_par_a, 1)
                if s == 0 and n == 1:
                    act.wait_ge(s_aw, 6)
                    A(w2h[:, 0:MA, 0:D], aw, ACT.Copy, scale=WS).then_inc(s_aw_hi, 1)
                    A(w2h[:, 0:MA, D:D1], aw_col[:], ACT.Copy, scale=WS).then_inc(s_aw_hi, 1)
                if s == 1 and n < NROT:
                    for m in range(KD):
                        act.wait_ge(s_v_pe, 2 * n + m + 1)
                        A(V[(n + 1) % 2][:, m, :], ep[m][:, 0:D1], ACT.Copy).then_inc(s_v_ev, 1)
                if s == 1 and n >= NROT - 1:
                    j = n - NROT + 1
                    if j == 0:
                        act.wait_ge(s_r_pe, 1)
                        A(eb2r[:], hp[1][0:NE, 0:D1], ACT.Copy, scale=WS).then_inc(s_eb2, 1)
                    if j < PAIRS:
                        act.wait_ge(s_rt_pe, j + 1)
                        if j >= 2:
                            act.wait_ge(s_r_pe, 2 * (j - 1) + 1)
                        A(rT[j % 2], hp[j % 2][:].rearrange("p (t k c) -> p t k c", t=2, k=KD), ACT.Copy)\
                            .then_inc(s_rt_ev, 1)
                    if j >= 1:
                        for t in range(2):
                            kt = 2 * (j - 1) + t
                            act.wait_ge(s_r_pe, kt + 2)
                            A(w2h[:, MA + kt, :], ep[t][:, 0:D1], ACT.Copy, scale=WS).then_inc(s_r_hi, 1)
                j = n - W1_SLOT0
                if s == 1 and 0 <= j < MT // ME:
                    act.wait_ge(s_ld_stage[j % 2], 16 * (j // 2 + 1))
                    A(w1h[:, :, j * H:(j + 1) * H], stage[j % 2], ACT.Copy, scale=WS).then_inc(s_hi, 1)

            def load_table(func, s, n):
                if isinstance(s, int) and s < 2:
                    loads = 4 * (s + 1) + (n + 1) // 4
                elif isinstance(s, int) and s >= NC:
                    loads = 8 * NC - 3 + 4 * (s - NC) + n // 4
                else:
                    loads = 8 * s - 3 + n // 2
                wait(act, s_warm, loads)
                A(warm[:], eps[:, 0:1], func).then_inc(s_warm, 1)

            def decay(c, n, q, k):
                act.wait_ge(s_dt, 2 * c + k + 1)
                wait(act, s_y, NS * c + place_before(q, n) + 1)
                A(ring[:, PLACE[q][n], k, :], dt[:, k, :], ACT.Exp, scale=neg_a[:, k, n:n + 1]).then_inc(s_dA[k], 1)

            def exps(c, n, q):
                for k in range(KD):
                    decay(c, n, q, k)

            def step(it, r):
                s = 2 * it + r
                par = lambda d: (r + d) % 2
                f, sc, b, m, o = s + 1, s, s - 1, s - 2, s - 3

                def first_tap(k):
                    act.wait_ge(s_xs, 2 * f + k + 1)
                    wait(act, s_yinit, 2 * f)
                    wait(act, s_dtx, 2 * f)
                    A(xc[:, k, :], xs[:, k, 0:CH], ACT.Identity, bias=conv_b[:, k:k + 1], scale=conv_w[:, k, 0:1])\
                        .then_inc(s_cv0, 1)

                def small(use):
                    if use in ("t0", "t1"):
                        k = int(use[1])
                        if k == 0 and (r + 1) % 2 == 0:
                            bt = it + (r + 1) // 2
                            if not (isinstance(bt, int) and bt == 0):
                                wait(act, s_h1, 2 * f)
                            A(cur_mod[:, :], modT[:, bass.ds(bt, 1), :].rearrange("p o j -> p (o j)"), ACT.Copy)\
                                .then_inc(s_curmod, 1)
                            act.wait_ge(s_curmod, bt + 1)
                        act.wait_ge(s_f_t, 2 * f + k + 1)
                        wait(act, s_o_pe, 2 * f - 2)
                        if on(m):
                            act.wait_ge(s_hlo_v, MT // 2 * m + ME)
                            act.wait_ge(s_hlo_p, MT // 2 * m + ME)
                        for dst in (full[:, k, :], h1h[:, par(1), k, :]):
                            last = A(dst, misc[:], ACT.Identity, bias=cur_mod[:, k:k + 1], scale=cur_mod[:, 2 + k:3 + k])
                        last.then_inc(s_h1, 1)
                    elif use in ("j0", "j1"):
                        k = int(use[1])
                        act.wait_ge(s_j, 2 * f + k + 1)
                        wait(act, s_cv, 7 * f)
                        A(xs[:, k, TAPS - 1:], misc[:], ACT.Identity, bias=b_in[:, k:k + 1], scale=1.0 / WS).then_inc(s_xs, 1)
                        if k == 0:
                            first_tap(0)
                    elif use in ("g0", "g1"):
                        k = int(use[1])
                        act.wait_ge(s_g_pe, 2 * sc + k + 1)
                        wait(act, s_o_pe, 2 * sc)
                        A(sg[:, k, :], misc[:], ACT.Identity, bias=b_gh[:, k:k + 1], scale=0.5 / WS).then_inc(s_gv, 1)
                    elif use == "wt":
                        act.wait_ge(s_wt_pe, m + 1)
                        wait(act, s_f_t, 2 * (f + 1) if on(f) else 2 * NC)
                        A(wT, misc[0:NE, :], ACT.Copy).then_inc(s_wt, 1)
                    elif use[0] == "n":
                        t = int(use[1])
                        act.wait_ge(s_n_pe, 4 * m + t + 1)
                        wait(act, s_out, 16 * m)
                        A(na[:, t, :], misc[:, 0:D1], ACT.Copy).then_inc(s_na, 1)
                    elif use == "bc":
                        act.wait_ge(s_bc_pe, f + 1)
                        act.wait_ge(s_f_t, 2 * f + 2)
                        A(bcf, misc[0:P, :], ACT.Identity, bias=b_bc[:]).then_inc(s_bcf, 1)
                    elif use in ("d0", "d1"):
                        k = int(use[1])
                        act.wait_ge(s_d_pe, 2 * f + k + 1)
                        wait(act, s_sg, 2 * f)
                        wait(act, s_dtx, 2 * f)
                        wait(act, s_dA[k], NS * f)
                        A(dt[:, k, :], misc[:], ACT.Relu, bias=b_dt[:, k:k + 1]).then_inc(s_d_raw, 1)
                        A(th[:, k, :], misc[:], ACT.Abs, bias=b_dt[:, k:k + 1]).then_inc(s_d_raw, 1)
                    elif use in ("x0", "x1"):
                        k = int(use[1])
                        act.wait_ge(s_x_t, 2 * b + k + 1)
                        wait(act, s_hid, MT * b)
                        act.wait_ge(s_base, 2 * b + 2)
                        A(xnT[:, k, :], misc[:], ACT.Identity, bias=ln_b[:, k:k + 1], scale=ln_g[:, k:k + 1])\
                            .then_inc(s_xn, 1)
                        A(xnh[:, k, :], misc[:], ACT.Identity, bias=ln_b[:, k:k + 1], scale=ln_g[:, k:k + 1])\
                            .then_inc(s_xn, 1)

                def normalise(dst, src, rs, nb, ready, value, done, tiles=range(NT)):
                    act.wait_ge(ready, value)
                    for t in tiles:
                        A(dst[:, t, :], src[:, t, :], ACT.Identity, bias=nb[:, t:t + 1], scale=rs[:, t:t + 1])\
                            .then_inc(done, 1)

                def gelus(j, half):
                    if not on(m):
                        return
                    for mm in (2 * half, 2 * half + 1):
                        h = ME * j + mm
                        act.wait_ge(s_hid, MT * m + h + 1)
                        if h == 0 and isinstance(m, int) and m == 0:
                            act.wait_ge(s_lo, MT // ME)
                            act.wait_ge(s_r_pe, MT - MA + 1)
                        if h in (9, 10) and on(f):
                            act.wait_ge(s_h1l, 2 * f + h - 8)
                        wait(act, s_hlo_p if h % 2 == 0 else s_hlo_v, MT // 2 * m + (h - FULL) // 2 + 1)
                        if mm == 0:
                            read = NOUT * m + (-NT * (1 - j) if j < 2 else NT if j < 4 else NT + NT * (j - 3))
                            wait(act, s_eo, read)
                        A(full[:, h % FULL, :], hp[h % 2][:], ACT.Gelu, bias=b1[:, h:h + 1], scale=1.0 / WS)
                        A(hidh[:, j % 2, mm, :], hp[h % 2][:], ACT.Gelu, bias=b1[:, h:h + 1], scale=1.0 / WS)\
                            .then_inc(s_gelu, 1)

                def smalls(uses):
                    for use in uses:
                        if use not in ("logits", "o0", "o1") and on(s + MISC[MISC_AT[use]][1]):
                            small(use)
                for n in range(NS):
                    grp, i = n // 4, n % 4
                    smalls(BEFORE.get(n, []))
                    if i < 2:
                        gelus(2 * grp + i, 0)
                    if n == 0 and on(o):
                        act.wait_ge(s_zs, o + 1)
                        A(gt[:], zs[:], ACT.Tanh, scale=0.5, bias=gcb_half[:]).then_inc(s_gth4, 1)
                    if n == 10 and on(b):
                        normalise(res, xr[:, par(-1)], rs_b, nb_b, s_b_rstd, 12 * b + 8, s_b_hat)
                    if n == 6 and on(f):
                        first_tap(1)
                    if n == 14 and on(f):
                        act.wait_ge(s_d_raw, 4 * f + 4)
                        A(th[:], th[:], ACT.Exp, scale=-1.0).then_inc(s_sp, 1)
                        act.wait_ge(s_sp, 2 * f + 1)
                        A(th[:], th[:], ACT.Ln, bias=1.0).then_inc(s_sp, 1)
                    if i >= 2 and n < 14 and on(sc):
                        exps(sc, 4 * grp + 4 + 2 * (i - 2), par(0))
                        exps(sc, 4 * grp + 5 + 2 * (i - 2), par(0))
                    if n == 2 and on(m):
                        act.wait_ge(s_rt, 5 * m + 4)
                        A(wE[:], lg[:], ACT.Exp).then_inc(s_rexp, 1)
                    if i == 3 and n < 15 and on(m):
                        load_table(ACT.Gelu, s, n)
                    smalls(AMID.get(n, []))
                    if n == 9 and on(f):
                        act.wait_ge(s_cv, 7 * f + 6)
                        if on(m):
                            act.wait_ge(s_rt, 5 * m + 5)
                        A(th[:], xc[:], ACT.Tanh).then_inc(s_th, 1)
                    if n == 1 and on(f):
                        normalise(xin, xin, rs_f, nb_f, s_f_rstd, 4 * f + 4, s_f_hat)
                    if n == 4 and on(b):
                        normalise(res, res, rs_b, nb_b, s_b_rstd, 12 * b + 4, s_b_hat, (0, 1))
                    if n == 11 and on(sc):
                        if on(f):
                            act.wait_ge(s_xc, 2 * f + 2)
                        act.wait_ge(s_gv, 2 * sc + 2)
                        A(th[:], sg[:], ACT.Tanh).then_inc(s_gth, 1)
                    if n == 13 and on(b):
                        normalise(res, res, rs_b, nb_b, s_b_rstd, 12 * b + 12, s_b_hat, (2, 3))
                    if i < 2:
                        gelus(2 * grp + i, 1)
                    if i == 1 and (on(sc) or on(f)):
                        load_table(ACT.Exp, s, n)
                    if n == 3 and on(o):
                        act.wait_ge(s_fin, 2 * o + 2)
                        act.dma_start(tok(par(-3), it + (r - 3) // 2)(out), na[:, :, 0:D]).then_inc(s_out, 16)
                    smalls(AFTER.get(n, []))
                    if n == 4 and on(b):
                        normalise(res, res, rs_b, nb_b, s_b_rstd, 12 * b + 4, s_b_hat, (2, 3))
                    if n == 12 and on(b):
                        act.wait_ge(s_base, 2 * b + 1)
                        normalise(res, res, rs_b, nb_b, s_b_rstd, 12 * b + 12, s_b_hat, (0, 1))
                    if n == 15 and on(f):
                        for k in range(KD):
                            for nn in range(4):
                                decay(f, nn, par(1), k)
                    if n == 15 and on(b):
                        load_table(ACT.Gelu, s, n)
                    if isinstance(s, int):
                        setup(s, n)
            run_steps(act, step)
            act.wait_ge(s_out, 16 * NC)

        @block.vector
        def _(v):
            V_ = nc.vector
            v.wait_ge(s_ld_mod, N_LD_MOD)
            v.wait_ge(s_mod_a, 1)
            V_.tensor_scalar(cTs, cT, 0.5, None, ALU.mult).then_inc(s_mod_v, 1)
            v.wait_ge(s_mod_v, 1)
            V_.scalar_tensor_tensor(cTs, cTh, 1.0, cTs, ALU.add, ALU.mult).then_inc(s_mod_v, 1)
            v.wait_ge(s_mod_pe, 3)
            V_.tensor_copy(mrow[:, 0:2, :], ep[0][0:NB, :].rearrange("p (r c) -> p r c", r=2)).then_inc(s_mod_v, 1)
            V_.tensor_copy(mrow[:, 2:4, :], ep[1][0:NB, :].rearrange("p (r c) -> p r c", r=2)).then_inc(s_mod_v, 1)
            v.wait_ge(s_mod_v, 4)
            V_.tensor_scalar(sign, mrow[:, 0:4:3, :], 0.0, 2.0, ALU.is_ge, ALU.mult).then_inc(s_mod_v, 1)
            V_.tensor_scalar(mtmp, mrow[:, 0:4:3, :], -1.0, None, ALU.mult).then_inc(s_mod_v, 1)
            v.wait_ge(s_mod_v, 6)
            V_.tensor_tensor(mtmp, mtmp, mrow[:, 0:4:3, :], ALU.max).then_inc(s_mod_v, 1)
            v.wait_ge(s_mod_v, 7)
            V_.tensor_scalar(mtmp, mtmp, 0.25, None, ALU.max).then_inc(s_mod_v, 1)
            v.wait_ge(s_mod_v, 8)
            V_.scalar_tensor_tensor(mrow[:, 0:4:3, :], sign, -1.0, mtmp, ALU.add, ALU.mult).then_inc(s_mod_v, 1)
            v.wait_ge(s_mod_v, 9)
            V_.tensor_tensor(prow[:, 0:2, :], lnrow, mrow[:, 0:1, :].to_broadcast([NB, 2, D]), ALU.mult)
            V_.tensor_scalar(prow[:, 2, :], mrow[:, 2, :], 1.0, None, ALU.add).then_inc(s_mod_v, 1)
            V_.tensor_copy(prow[:, 3, :], mrow[:, 1, :]).then_inc(s_mod_v, 1)
            V_.tensor_copy(prow2, mrow[:, 3, :]).then_inc(s_mod_v, 1)
            v.wait_ge(s_mod_a, 2)
            V_.tensor_scalar(modT[:, :, 2:4], modT[:, :, 2:4], 1.0, None, ALU.add).then_inc(s_par_v, 1)
            v.wait_ge(s_par_a, 2)
            V_.tensor_scalar(neg_a[:], neg_a[:], -1.0, None, ALU.mult).then_inc(s_par_v, 1)
            V_.tensor_scalar(conv_w[:], conv_w[:], 0.5, None, ALU.mult).then_inc(s_par_v, 1)
            V_.tensor_scalar(conv_b[:], conv_b[:], 0.5, None, ALU.mult).then_inc(s_par_v, 1)
            v.wait_ge(s_const, 9)
            V_.memset(xnT[:, 0, :], 0.0).then_inc(s_par_v, 1)
            v.wait_ge(s_par_v, 5)
            for k in range(KD):
                V_.tensor_copy(eye[:, k, k * P:(k + 1) * P], ident[:]).then_inc(s_ex_q, 1)
            nq = [KD]
            v.wait_ge(s_win_hi, 1)
            V_.scalar_tensor_tensor(w_inl[:], th[:], WS, w_inh[:], ALU.mult, ALU.subtract).then_inc(s_win_lo, 1)
            V_.tensor_copy(ident16[:], ident[:]).then_inc(s_win_lo, 1)

            def setup(s, n):
                rd = setup_round(s, n)
                if rd in V_ROUNDS:
                    g = V_ROUNDS[-1] - rd
                    for i in range(NROT):
                        v.wait_ge(*round_taken(1, i))
                        if rd > V_ROUNDS[0]:
                            v.wait_ge(*round_taken(rd - 1, i))
                        terms = ((eye, c_tay[3 * g]), (xm(i, 0), c_tay[3 * g + 1]), (xm(i, 2), c_tay[3 * g + 2]))
                        for t, (src, cf) in enumerate(terms):
                            v.wait_ge(s_ex_q, nq[0])
                            if t == 0:
                                V_.tensor_scalar(xm(i, 5), src, cf, None, ALU.mult).then_inc(s_ex_q, 1)
                            else:
                                V_.scalar_tensor_tensor(xm(i, 5), src, cf, xm(i, 5), ALU.mult, ALU.add).then_inc(s_ex_q, 1)
                            nq[0] += 1
                    v.wait_ge(s_ex_q, nq[0])
                    for i in range(NROT):
                        v.wait_ge(s_ex_pe, NROT * rd + i + 1)
                        V_.scalar_tensor_tensor(xm(i, 4), ex_bank[i][:].rearrange("p (k c) -> p k c", k=KD),
                                                c_tay[TAYLOR] if rd == V_ROUNDS[0] else 1.0, xm(i, 5), ALU.mult, ALU.add)\
                            .then_inc(s_ex_v, 1)
                if s == 0 and n == 1:
                    v.wait_ge(s_ld_ffn, N_LD_FFN)
                    for h in range(2):
                        if h:
                            v.wait_ge(s_aw, 2)
                        V_.tensor_tensor(aw_tmp[:], aw[:, 4 * h:4 * h + 4, :], g1_bc.unsqueeze(1).to_broadcast([P, 4, D]),
                                         ALU.mult).then_inc(s_aw, 1)
                        v.wait_ge(s_aw, 2 * h + 1)
                        V_.tensor_reduce(aw_col[:, 4 * h:4 * h + 4, :], aw_tmp[:], AX, ALU.add).then_inc(s_aw, 1)
                    v.wait_ge(s_aw, 4)
                    V_.tensor_tensor(aw_tmp[:, 0, :], ab2_bc[:, 0:D], g1_bc, ALU.mult).then_inc(s_aw, 1)
                    v.wait_ge(s_aw, 5)
                    V_.tensor_reduce(ab2_bc[:, D:D1], aw_tmp[:, 0, :], AX, ALU.add).then_inc(s_aw, 1)
                    V_.tensor_copy(V[0][:, :, 0:D], eye).then_inc(s_v0, 1)
                    v.wait_ge(s_aw_hi, 2)
                    V_.scalar_tensor_tensor(w2l[:, 0:MA, 0:D], aw, WS, w2h[:, 0:MA, 0:D], ALU.mult, ALU.subtract)\
                        .then_inc(s_aw, 1)
                    V_.scalar_tensor_tensor(w2l[:, 0:MA, D:D1], aw_col[:], WS, w2h[:, 0:MA, D:D1], ALU.mult, ALU.subtract)\
                        .then_inc(s_aw, 1)
                if s == 1 and n >= NROT:
                    for kt in range(2 * (n - NROT), min(2 * (n - NROT) + 2, MT - MA)):
                        v.wait_ge(s_r_hi, kt + 1)
                        V_.scalar_tensor_tensor(w2l[:, MA + kt, :], ep[kt % 2][:, 0:D1], WS, w2h[:, MA + kt, :],
                                                ALU.mult, ALU.subtract).then_inc(s_r_ev, 1)
                j = n - W1_SLOT0
                if s == 1 and 0 <= j < MT // ME:
                    v.wait_ge(s_hi, j + 1)
                    V_.scalar_tensor_tensor(w1l[:, :, j * H:(j + 1) * H], stage[j % 2], WS, w1h[:, :, j * H:(j + 1) * H],
                                            ALU.mult, ALU.subtract).then_inc(s_lo, 1)

            def stats(src, st, mv, done, base):
                for t in range(NT):
                    V_.bn_stats(st[:, t, :], src[:, t, :]).then_inc(done, 1)
                v.wait_ge(done, base + NT)
                V_.memset(spare[:], 0.0)
                for t in range(NT):
                    V_.bn_aggr(mv[:, t, :], st[:, t, :]).then_inc(done, 1)

            def step(it, r):
                s = 2 * it + r
                par = lambda d: (r + d) % 2
                f, sc, b, m, o = s + 1, s, s - 1, s - 2, s - 3

                def take(oo):
                    if not on(m):
                        return
                    v.wait_ge(s_eo, NOUT * m + oo + 1)
                    bank = ep[oo % 2][:, 0:D1]
                    if oo < NT:
                        if oo == 0:
                            wait(v, s_mix, 5 * m)
                            if isinstance(m, int) and m == 0:
                                v.wait_ge(s_r_pe, MT - MA + 1)
                        V_.scalar_tensor_tensor(ab[:, oo, :], bank, 1.0 / WS, ab2_bc[:], ALU.mult, ALU.add).then_inc(s_eo_ev, 1)
                    else:
                        e, t = (oo - NT) // NT, (oo - NT) % NT
                        if e == 0:
                            v.wait_ge(s_na, 4 * m + t + 1)
                        else:
                            v.wait_ge(s_eo_ev, NOUT * m + oo - NT + 1)
                        V_.scalar_tensor_tensor(na[:, t, :], bank, wE[:, t, e:e + 1], na[:, t, :], ALU.mult, ALU.add)\
                            .then_inc(s_eo_ev, 1)

                def hidden_low(h):
                    v.wait_ge(s_gelu, MT * m + h + 1)
                    V_.tensor_tensor(hidl[:, h // ME % 2, h % ME, :], full[:, h % FULL, :], hidh[:, h // ME % 2, h % ME, :],
                                     ALU.subtract).then_inc(s_hlo_v, 1)

                def out_proj(half):
                    v.wait_ge(s_o_pe, 2 * b + half + 1)
                    V_.tensor_tensor(res[:, 2 * half:2 * half + 2, :], misc[:].rearrange("p (t c) -> p t c", t=2),
                                     b_out_bc[:].unsqueeze(1).to_broadcast([P, 2, D]), ALU.add).then_inc(s_res, 1)

                def tap(k, j):
                    if not on(f):
                        return
                    if j == 1:
                        v.wait_ge(s_cv0, 2 * f + k + 1)
                    else:
                        v.wait_ge(s_cv, 7 * f + 3 * k + j - 1)
                    V_.scalar_tensor_tensor(xc[:, k, :], xs[:, k, j:j + CH], conv_w[:, k, j:j + 1], xc[:, k, :],
                                            ALU.mult, ALU.add).then_inc(s_cv, 1)
                    if k == 1 and j == TAPS - 1:
                        v.wait_ge(s_cv, 7 * f + 6)
                        if par(1) == 0:
                            V_.tensor_copy(xs[:, :, 0:TAPS - 1], xs[:, :, CH:CH + TAPS - 1]).then_inc(s_cv, 1)
                        else:
                            V_.memset(xs[:, :, 0:TAPS - 1], 0.0).then_inc(s_cv, 1)

                def input_low(k):
                    if on(b):
                        v.wait_ge(s_xn, 4 * b + 2 * k + 2)
                        wait(v, s_hid, MT * b)
                        V_.tensor_tensor(xnl[:, k, :], xnT[:, k, :], xnh[:, k, :], ALU.subtract).then_inc(s_xnl, 1)

                def silu(k):
                    v.wait_ge(s_th, f + 1)
                    V_.scalar_tensor_tensor(xc[:, k, :], th[:, k, :], 1.0, xc[:, k, :], ALU.add, ALU.mult).then_inc(s_xc, 1)

                def h1_low(k):
                    if on(f):
                        v.wait_ge(s_h1, 2 * f + k + 1)
                        V_.tensor_tensor(h1l[:, par(1), k, :], full[:, k, :], h1h[:, par(1), k, :], ALU.subtract)\
                            .then_inc(s_h1l, 1)

                def mid(n):
                    if n == 3:
                        h1_low(1)
                    if n == 10 and on(f):
                        silu(0)
                    if n == 15:
                        input_low(1)
                    if n in (6, 7, 8):
                        tap(*{6: (0, 2), 7: (1, 1), 8: (1, 3)}[n])
                    if n == 0 and on(m):
                        v.wait_ge(s_lg_pe, m + 1)
                        V_.tensor_tensor(lg[:], misc[:, 0:8 * NT].rearrange("p (t e) -> p t e", t=NT)[:, :, 0:NE],
                                         gate_b_bc[:].unsqueeze(1).to_broadcast([P, NT, NE]), ALU.add).then_inc(s_rt, 1)
                    if n == 1 and on(b):
                        out_proj(0)

                for n in range(NS):
                    grp, i = n // 4, n % 4
                    outs = [] if i < 2 else [None, 2 * (i - 2), None, 2 * (i - 2) + 1] if grp == 0 else \
                        [NT + NT * (2 * grp + i - 4) + t for t in range(NT)]

                    def take_at(pos):
                        if outs and outs[pos] is not None:
                            take(outs[pos])
                        if i < 2 and on(m) and pos in (1, 3):
                            hidden_low(ME * (2 * grp + i) + pos - 1)
                    if n == 0 and on(o):
                        v.wait_ge(s_eo_ev, NOUT * o + NOUT)
                        V_.tensor_tensor(zs[:], ab[:, :, D:D1], na[:, :, D:D1], ALU.add).then_inc(s_zs, 1)
                    if on(sc):
                        base = 2 * NS * sc + 2 * n
                        bi, ci = 2 * NS * sc + 2 * n + 1, 2 * NS * sc + 2 * n + 2
                        slot_ = ring[:, PLACE[par(0)][n], :, :]
                        for k in range(KD):
                            if k == 0:
                                take_at(0)
                                v.wait_ge(s_bb, bi)
                                if n == 0:
                                    v.wait_ge(s_dtx, 2 * sc + 2)
                            wait(v, s_scan, base + k)
                            V_.tensor_tensor(u[:], dtx[:, par(0), k, :], bcp[(2 * n) % 3][:], ALU.mult).then_inc(s_dbx, 1)
                            if k == 1:
                                take_at(2)
                            v.wait_ge(s_dA[k], NS * sc + n + 1)
                            v.wait_ge(s_dbx, base + k + 1)
                            V_.tensor_tensor_scan(slot_[:, k, :], slot_[:, k, :], u[:],
                                                  0.0 if par(0) == 0 else state[:, n, k:k + 1], ALU.mult, ALU.add)\
                                .then_inc(s_scan, 1)
                            if k == 0 and n < 2:
                                mid(n)
                            take_at(2 * k + 1)
                            if k == 0 and n >= 2:
                                mid(n)
                        if par(0) == 0:
                            v.wait_ge(s_scan, base + 2)
                            V_.tensor_copy(state[:, n, :], slot_[:, :, CH - 1]).then_inc(s_tail, 1)
                        v.wait_ge(s_bb, ci)
                        if par(0) == 0:
                            v.wait_ge(s_tail, NS // 2 * sc + n + 1)
                        v.wait_ge(s_scan, base + 2)
                        V_.tensor_tensor(slot_, slot_, bcp[(2 * n + 1) % 3][:].unsqueeze(1).to_broadcast([P, KD, CH]),
                                         ALU.mult).then_inc(s_hc, 1)
                    else:
                        take_at(0)
                        take_at(1)
                        mid(n)
                        take_at(2)
                        take_at(3)

                    if n == 0:
                        if isinstance(s, int) and s == -1:
                            v.wait_ge(s_x_in, 16)
                            stats(xin, st_f, mv_f, s_f_stat, 0)
                    if n == 0:
                        if on(m):
                            v.wait_ge(s_rt, 5 * m + 1)
                            if on(sc):
                                v.wait_ge(s_dt, 2 * sc + 2)
                            other = lg[:].unsqueeze(2).to_broadcast([P, NT, NE, NE])
                            mine = lg[:].unsqueeze(3).to_broadcast([P, NT, NE, NE])
                            V_.tensor_tensor(rk[:], other, mine, ALU.is_ge)
                            V_.tensor_tensor(rk2[:], other, mine, ALU.is_gt)
                            V_.tensor_reduce(lgm[:], lg[:], AX, ALU.max).then_inc(s_rt, 1)
                            v.wait_ge(s_rt, 5 * m + 2)
                            V_.tensor_tensor(lg[:], lg[:], lgm[:].to_broadcast([P, NT, NE]), ALU.subtract)
                            V_.tensor_tensor(rk[:], rk[:], before[:].unsqueeze(1).to_broadcast([P, NT, NE, NE]), ALU.mult)
                            V_.tensor_tensor(rk2[:], rk2[:], after[:].unsqueeze(1).to_broadcast([P, NT, NE, NE]), ALU.mult)\
                                .then_inc(s_rt, 1)
                            v.wait_ge(s_rt, 5 * m + 3)
                            V_.tensor_tensor(rk[:], rk[:], rk2[:], ALU.add).then_inc(s_rt, 1)
                            v.wait_ge(s_rt, 5 * m + 4)
                            V_.tensor_reduce(rsum[:], rk[:], AX, ALU.add).then_inc(s_rt, 1)
                    if n == 1:
                        if on(b):
                            out_proj(1)
                        if on(o):
                            V_.tensor_tensor(na[:, :, 0:D], na[:, :, 0:D], ab[:, :, 0:D], ALU.subtract).then_inc(s_mix, 1)
                            v.wait_ge(s_gth4, o + 1)
                            v.wait_ge(s_mix, 5 * o + 1)
                            V_.tensor_scalar(gt[:], gt[:], 0.5, 0.5, ALU.mult, ALU.add).then_inc(s_gate, 1)
                            v.wait_ge(s_gate, o + 1)
                            for t in range(NT):
                                V_.scalar_tensor_tensor(na[:, t, 0:D], na[:, t, 0:D], gt[:, t, :], ab[:, t, 0:D],
                                                        ALU.mult, ALU.add).then_inc(s_mix, 1)
                    if n == 2 and on(m):
                        v.wait_ge(s_rexp, m + 1)
                        v.wait_ge(s_rt, 5 * m + 5)
                        V_.scalar_tensor_tensor(wE[:], rsum[:], 1.5, wE[:], ALU.is_lt, ALU.mult).then_inc(s_w, 1)
                        v.wait_ge(s_w, 3 * m + 1)
                        V_.tensor_reduce(lgs[:], wE[:], AX, ALU.add).then_inc(s_wsum, 1)
                        v.wait_ge(s_wsum, m + 1)
                        V_.reciprocal(lgs[:], lgs[:]).then_inc(s_w, 1)
                        v.wait_ge(s_w, 3 * m + 2)
                        V_.scalar_tensor_tensor(wE[:], wE[:], 1.0 / WS, lgs[:].to_broadcast([P, NT, NE]), ALU.mult, ALU.mult)\
                            .then_inc(s_w, 1)
                    if n == 2:
                        h1_low(0)
                    if n == 2 and on(b):
                        v.wait_ge(s_res, 2 * b + 2)
                        stats(res, st_b, mv_b, s_b_stat, 24 * b)
                    if n in (5, 6, 7):
                        tap(*{5: (0, 1), 6: (0, 3), 7: (1, 2)}[n])
                    if n == 7 and on(b):
                        v.wait_ge(s_x1, 3 * b + 3)
                        stats(xr[:, par(-1)], st_b, mv_b, s_b_stat, 24 * b + 8)
                    if n == 10 and on(f):
                        silu(1)
                    if n == 11:
                        if on(sc):
                            v.wait_ge(s_gth, sc + 1)
                            for k in range(KD):
                                V_.scalar_tensor_tensor(sg[:, k, :], th[:, k, :], 1.0, sg[:, k, :], ALU.add, ALU.mult)\
                                    .then_inc(s_sg, 1)
                        if on(b):
                            v.wait_ge(s_h2, 2 * b + 2)
                            stats(res, st_b, mv_b, s_b_stat, 24 * b + 16)
                        if on(f):
                            v.wait_ge(s_bcf, f + 1)
                            q = par(1)
                            V_.tensor_copy(bcs[:, q, :], bcf).then_inc(s_bcs, 1)
                            v.wait_ge(s_bcs, 4 * f + 1)
                            V_.tensor_tensor(bcf[P // 2:P, :], bcf[P // 2:P, :], bcs[P // 2:P, q, :], ALU.subtract)\
                                .then_inc(s_bcs, 1)
                            v.wait_ge(s_bcs, 4 * f + 2)
                            V_.tensor_copy(bcs[P // 2:P, q, :], bcf[P // 2:P, :]).then_inc(s_bcs, 1)
                            v.wait_ge(s_bcs, 4 * f + 3)
                            V_.tensor_tensor(bcs[3 * P // 4:P, q, :], bcf[3 * P // 4:P, :], bcs[3 * P // 4:P, q, :],
                                             ALU.subtract).then_inc(s_bcs, 1)
                    if n == 14:
                        input_low(0)
                    if n == 15 and on(s + 2):
                        v.wait_ge(s_x_in, 16 * (s + 3))
                        stats(xin, st_f, mv_f, s_f_stat, 8 * (s + 2))
                    if isinstance(s, int):
                        setup(s, n)
            run_steps(v, step)


def kernel(**inputs):
    import numpy as _np
    import concourse.bacc as _bacc
    from concourse import mybir as _mybir
    from concourse.bass_utils import run_bass_kernel_spmd as _run

    nc = _bacc.Bacc("TRN2", target_bir_lowering=False, num_devices=1)
    arrays, args = {}, {}
    for name, value in inputs.items():
        arr = _np.ascontiguousarray(value)
        arrays[f"in_{name}_dram"] = arr
        args[name] = nc.dram_tensor(f"in_{name}_dram", arr.shape, _mybir.dt.from_np(arr.dtype), kind="ExternalInput").ap()
    shape = inputs["L0_attn_x"].shape
    out = nc.dram_tensor("out_0_dram", shape, _mybir.dt.float32, kind="ExternalOutput").ap()
    build_adaln_mamba_moe(nc, args, out)
    r = _run(nc, [arrays], core_ids=[0])
    return r.results[0]["out_0_dram"]
```
